# Optimizing a Trainium2 kernel written in Bass

```python
import numpy as np
import jax
import jax.numpy as jnp

def _softmax(x, axis=-1):
    return jax.nn.softmax(x, axis=axis)

def _gelu(x):
    return jax.nn.gelu(x, approximate=True)

def _silu(x):
    return jax.nn.silu(x)

def _sigmoid(x):
    return jax.nn.sigmoid(x)

def _layernorm(x, axis=-1, eps=1e-05):
    m = jnp.mean(x, axis=axis, keepdims=True)
    v = jnp.var(x, axis=axis, keepdims=True)
    return (x - m) / jnp.sqrt(v + eps)

def _scatter_add(tgt, idx, src, axis=0):
    return tgt.at[idx].add(src)

def _segment_sum(src, seg, n):
    return jax.ops.segment_sum(src, seg, n)
kernel_name = 'mk_gnn_preln_d2_gnn_r64_2fb2da'

def setup_inputs(seed: int=0):
    np.random.seed(seed)
    _w = jnp.asarray

    def _rec_inputs():
        import jax
        import jax.numpy as jnp
        _gk = jax.random.key(seed)
        x = -0.0005121 + 1.001 * jax.random.normal(jax.random.fold_in(_gk, 1), (50000, 64), jnp.float32)
        src = jax.random.randint(jax.random.fold_in(_gk, 2), (25000,), 0, 50000, jnp.int32)
        dst = jnp.minimum((50000 * jax.random.uniform(jax.random.fold_in(_gk, 3), (25000,)) ** 2.0).astype(jnp.int32), 49999)
        _o = jnp.argsort(dst, stable=True)
        src = src[_o]
        dst = dst[_o]
        edge_attr_64 = -9.77346e-05 + 0.999888 * jax.random.normal(jax.random.fold_in(_gk, 12), (25000, 64), jnp.float32)
        return (x, src, dst, edge_attr_64)
    x, src, dst, edge_attr_64 = _rec_inputs()

    def _L0_gnn_setup():
        import jax, jax.numpy as jnp
        import numpy as np
        N_NODES = 50000
        N_EDGES = 9375
        D = 64
        H = 4
        L = 4
        NEG_SLOPE = 0.2

        def _gat_layer(h, src_e, dst_e, W, al, ar, b):
            fs = (h @ W).reshape(N_NODES, H, D)
            el = jnp.einsum('nhd,hd->nh', fs, al)
            er = jnp.einsum('nhd,hd->nh', fs, ar)
            e = jax.nn.leaky_relu(el[src_e] + er[dst_e], NEG_SLOPE)
            m = jax.ops.segment_max(e, dst_e, num_segments=N_NODES)
            m = jax.lax.stop_gradient(m)
            ex = jnp.exp(e - m[dst_e])
            denom = jax.ops.segment_sum(ex, dst_e, num_segments=N_NODES)
            alpha = ex / denom[dst_e]
            msg = alpha[:, :, None] * fs[src_e]
            rst = jax.ops.segment_sum(msg, dst_e, num_segments=N_NODES)
            rst = rst + b.reshape(1, H, D)
            return rst.sum(axis=1)
        key = jax.random.key(seed)
        ks = jax.random.split(key, 9)
        feat = jax.random.normal(ks[0], (N_NODES, D), dtype=jnp.float32)
        src = jax.random.randint(ks[1], (N_EDGES,), 0, N_NODES, dtype=jnp.int32)
        dst = jax.random.randint(ks[2], (N_EDGES,), 0, N_NODES, dtype=jnp.int32)
        Ws = jax.random.normal(ks[3], (L, D, H * D), dtype=jnp.float32) / np.sqrt(D)
        attn_l = jax.random.normal(ks[4], (L, H, D), dtype=jnp.float32) / np.sqrt(D)
        attn_r = jax.random.normal(ks[5], (L, H, D), dtype=jnp.float32) / np.sqrt(D)
        gat_bias = jax.random.normal(ks[6], (L, H * D), dtype=jnp.float32) * 0.02
        h_bias = jax.random.normal(ks[7], (D,), dtype=jnp.float32) * 0.02
        return {'feat': feat, 'src': src, 'dst': dst, 'Ws': Ws, 'attn_l': attn_l, 'attn_r': attn_r, 'gat_bias': gat_bias, 'h_bias': h_bias}
    _L0_gnn_all = _L0_gnn_setup()
    _L0_gnn_in = {k: v for k, v in _L0_gnn_all.items() if k in ('Ws', 'attn_l', 'attn_r', 'gat_bias', 'h_bias')}
    del _L0_gnn_all

    def _L1_gnn_setup():
        import jax, jax.numpy as jnp
        import numpy as np
        N_NODES = 50000
        N_EDGES = 12500
        ATOM_F = 64
        NBR_F = 64
        EPS = 1e-05

        def batch_norm(x, gamma, beta):
            mu = x.mean(axis=0)
            var = x.var(axis=0)
            return gamma * (x - mu) * jax.lax.rsqrt(var + EPS) + beta
        key = jax.random.key(seed)
        ks = jax.random.split(key, 8)
        d_in = 2 * ATOM_F + NBR_F
        d_out = 2 * ATOM_F
        return {'atom_in_fea': jax.random.normal(ks[0], (N_NODES, ATOM_F), dtype=jnp.float32), 'nbr_fea': jax.random.normal(ks[1], (N_EDGES, NBR_F), dtype=jnp.float32), 'edge_src': jax.random.randint(ks[2], (N_EDGES,), 0, N_NODES), 'edge_dst': jax.random.randint(ks[3], (N_EDGES,), 0, N_NODES), 'W_full': jax.random.normal(ks[4], (d_in, d_out), dtype=jnp.float32) / np.sqrt(d_in), 'b_full': jnp.zeros((d_out,), dtype=jnp.float32), 'bn1_g': jnp.ones((d_out,), dtype=jnp.float32), 'bn1_b': jnp.zeros((d_out,), dtype=jnp.float32), 'bn2_g': jnp.ones((ATOM_F,), dtype=jnp.float32), 'bn2_b': jnp.zeros((ATOM_F,), dtype=jnp.float32)}
    _L1_gnn_all = _L1_gnn_setup()
    _L1_gnn_in = {k: v for k, v in _L1_gnn_all.items() if k in ('W_full', 'b_full', 'bn1_g', 'bn1_b', 'bn2_g', 'bn2_b')}
    del _L1_gnn_all
    return {'x': x, 'src': src, 'dst': dst, 'edge_attr_64': edge_attr_64, 'L0_gnn_Ws': _L0_gnn_in['Ws'], 'L0_gnn_attn_l': _L0_gnn_in['attn_l'], 'L0_gnn_attn_r': _L0_gnn_in['attn_r'], 'L0_gnn_gat_bias': _L0_gnn_in['gat_bias'], 'L0_gnn_h_bias': _L0_gnn_in['h_bias'], 'L1_gnn_W_full': _L1_gnn_in['W_full'], 'L1_gnn_b_full': _L1_gnn_in['b_full'], 'L1_gnn_bn1_g': _L1_gnn_in['bn1_g'], 'L1_gnn_bn1_b': _L1_gnn_in['bn1_b'], 'L1_gnn_bn2_g': _L1_gnn_in['bn2_g'], 'L1_gnn_bn2_b': _L1_gnn_in['bn2_b']}

def reference(x, src, dst, edge_attr_64, L0_gnn_Ws, L0_gnn_attn_l, L0_gnn_attn_r, L0_gnn_gat_bias, L0_gnn_h_bias, L1_gnn_W_full, L1_gnn_b_full, L1_gnn_bn1_g, L1_gnn_bn1_b, L1_gnn_bn2_g, L1_gnn_bn2_b):
    import jax
    import jax.numpy as jnp

    def _L0_gnn_ref(feat, src, dst, Ws, attn_l, attn_r, gat_bias, h_bias):
        import jax, jax.numpy as jnp
        import numpy as np
        N_NODES = 50000
        N_EDGES = 9375
        D = 64
        H = 4
        L = 4
        NEG_SLOPE = 0.2

        def _gat_layer(h, src_e, dst_e, W, al, ar, b):
            fs = (h @ W).reshape(N_NODES, H, D)
            el = jnp.einsum('nhd,hd->nh', fs, al)
            er = jnp.einsum('nhd,hd->nh', fs, ar)
            e = jax.nn.leaky_relu(el[src_e] + er[dst_e], NEG_SLOPE)
            m = jax.ops.segment_max(e, dst_e, num_segments=N_NODES)
            m = jax.lax.stop_gradient(m)
            ex = jnp.exp(e - m[dst_e])
            denom = jax.ops.segment_sum(ex, dst_e, num_segments=N_NODES)
            alpha = ex / denom[dst_e]
            msg = alpha[:, :, None] * fs[src_e]
            rst = jax.ops.segment_sum(msg, dst_e, num_segments=N_NODES)
            rst = rst + b.reshape(1, H, D)
            return rst.sum(axis=1)
        loops = jnp.arange(N_NODES, dtype=src.dtype)
        src_e = jnp.concatenate([src, loops])
        dst_e = jnp.concatenate([dst, loops])
        h = feat
        for i in range(L):
            h = _gat_layer(h, src_e, dst_e, Ws[i], attn_l[i], attn_r[i], gat_bias[i])
        return h + h_bias

    def _L1_gnn_ref(atom_in_fea, nbr_fea, edge_src, edge_dst, W_full, b_full, bn1_g, bn1_b, bn2_g, bn2_b):
        import jax, jax.numpy as jnp
        import numpy as np
        N_NODES = 50000
        N_EDGES = 12500
        ATOM_F = 64
        NBR_F = 64
        EPS = 1e-05

        def batch_norm(x, gamma, beta):
            mu = x.mean(axis=0)
            var = x.var(axis=0)
            return gamma * (x - mu) * jax.lax.rsqrt(var + EPS) + beta
        atom_src = atom_in_fea[edge_src]
        atom_dst = atom_in_fea[edge_dst]
        total = jnp.concatenate([atom_src, atom_dst, nbr_fea], axis=1)
        total = batch_norm(total @ W_full + b_full, bn1_g, bn1_b)
        filter_fea, core_fea = jnp.split(total, 2, axis=1)
        nbr_msg = jax.nn.sigmoid(filter_fea) * jax.nn.softplus(core_fea)
        atom_update = jax.ops.segment_sum(nbr_msg, edge_dst, num_segments=atom_in_fea.shape[0])
        return jax.nn.softplus(atom_in_fea + batch_norm(atom_update, bn2_g, bn2_b))
    h = jnp.maximum(_layernorm(x, axis=-1), 0.0)
    x = x + _L0_gnn_ref(h, src, dst, L0_gnn_Ws, L0_gnn_attn_l, L0_gnn_attn_r, L0_gnn_gat_bias, L0_gnn_h_bias)
    h = jnp.maximum(_layernorm(x, axis=-1), 0.0)
    x = x + _L1_gnn_ref(h, edge_attr_64, src, dst, L1_gnn_W_full, L1_gnn_b_full, L1_gnn_bn1_g, L1_gnn_bn1_b, L1_gnn_bn2_g, L1_gnn_bn2_b)
    return x

_drawn_inputs = setup_inputs


def setup_inputs(seed=0):
    import zlib

    import numpy as np

    out = dict(_drawn_inputs(seed))
    spreads = {'L1_gnn_b_full': (0.0, 2.0),
     'L1_gnn_bn1_g': (1.0, 0.6),
     'L1_gnn_bn1_b': (0.0, 2.0),
     'L1_gnn_bn2_g': (1.0, 0.6),
     'L1_gnn_bn2_b': (0.0, 0.8)}
    factors = {'L0_gnn_h_bias': 28.526}
    for name, (base, spread) in spreads.items():
        noise = np.random.default_rng([zlib.crc32(name.encode()), seed]).standard_normal(out[name].shape)
        drawn = base * np.exp(spread * noise) if base else spread * noise
        out[name] = jnp.asarray(drawn.astype(out[name].dtype))
    for name, factor in factors.items():
        out[name] = (out[name] * factor).astype(out[name].dtype)
    return out
```

```python
from contextlib import ExitStack

import concourse.bass as bass
from concourse import mybir

ALU = mybir.AluOpType
ACT = mybir.ActivationFunctionType
F32 = mybir.dt.float32
I32 = mybir.dt.int32
U8 = mybir.dt.uint8
AX_X = mybir.AxisListType.X

P = 128
D = 64
H = 4
L = 4
ROW = D + H
EDGE_W = D + 2 * H
HALF = 98
TILES = 2 * HALF
TPG = 4
GE = TPG * P
G = TILES // TPG
EP = TILES * P
CT = 7
CH = TILES // CT
CE = CT * P
Q = CH * H
NODE_T = 8
GN = NODE_T * P
EPS = 1e-5
SLOPE = 0.2
BIG = 1e30
FAR = 1 << 20
AHEAD = 4
EXP_MAX = 30.0
ACT_TABLES = "natural_log_exp_and_others"


class Steps:

    def __init__(self, *names, ahead=2):
        self.names, self.ahead = names, ahead
        self.start = ahead * len(names)

    def after(self, k, name, back=0):
        return k * len(self.names) + ((self.ahead - back) * len(self.names) + self.names.index(name) + 1)


def ascending(eng, body, turns=G // 2):
    with eng.Fori(0, turns) as i:
        body(i * 2, i * 2, 0, i + 0)
        body(i * 2 + 1, i * 2 + 1, 1, i + 0)
    for k in range(2 * turns, G):
        body(k, k, k % 2, k // 2)


def descending(eng, body):
    body(0, G - 1, 0, 0)
    with eng.Fori(0, G // 2) as i:
        body(i * 2 + 1, i * -2 + (G - 2), 1, i + 0)
        body(i * 2 + 2, i * -2 + (G - 3), 0, i + 1)


def at(k, back=0):
    return k + (AHEAD + 1 - back)


def pipelined(eng, stages, down=False, lead=4, slots=2):
    def peeled(i):
        for lag, fn in stages:
            k = i - lag
            if 0 <= k < G:
                fn(k, G - 1 - k if down else k, k % slots, k // slots)

    turns = (G - lead) // slots
    for i in range(lead):
        peeled(i)
    with eng.Fori(0, turns) as r:
        for c in range(slots):
            for lag, fn in stages:
                first = lead + c - lag
                g = r * -slots + (G - 1 - first) if down else r * slots + first
                fn(r * slots + first, g, first % slots, r + first // slots)
    for i in range(lead + slots * turns, G + lead):
        peeled(i)


def one_row(a):
    return a.rearrange("(a n) -> a n", a=1)


def one_col(a):
    return a.rearrange("(n a) -> n a", a=1)


def lanes(a, n):
    return one_row(a).broadcast_to([n, a.shape[0]])


def inner(a, shape):
    return a.unsqueeze(len(a.shape)).broadcast_to(shape)


def build(nc, x, src, dst, edge_attr, Ws, attn_l, attn_r, gat_bias, h_bias, W_full, b_full,
          bn1_g, bn1_b, bn2_g, bn2_b, out):
    N = x.shape[0]
    E = src.shape[0]
    LAST_P = (N - (G - 1) * GN) // NODE_T
    LAST_E = E - (G - 1) * GE
    assert (G - 1) * GN + LAST_P * NODE_T == N and 0 < LAST_P <= P
    assert TILES == CH * CT and E < EP and 0 < LAST_E
    PAD_DST = N + 1

    dram = lambda name, shape, dt=F32: nc.dram_tensor(name, shape, dt).ap()
    src_pad = dram("src_pad", [EP], I32)
    dst_pad = dram("dst_pad", [1 + EP + P], I32)
    keep_row = dram("keep_row", [EP + 1], U8)
    tables = [dram(f"table{l}", [N + EP, ROW]) for l in range(L)]
    x_dst = dram("x_dst", [P, TILES * D])
    h1_dst = dram("h1_dst", [P, TILES * D])

    top = ExitStack()

    def mem(stack, name, shape, dt=F32):
        return stack.enter_context(nc.sbuf_tensor(name, shape, dt))

    signals = []

    def sem(stack, name):
        signals.append(nc.alloc_semaphore(name=name))
        return signals[-1]

    def pool_dma_sem(name):
        return nc.alloc_semaphore(name=name)

    def clear_signals():
        with nc.Block() as block:
            @block.sync
            def _(sp):
                for signal in signals:
                    sp.sem_clear(signal)
        for signal in signals:
            nc.release_semaphore(signal)
        signals.clear()

    marks = {}
    with top:
        wide = mem(top, "wide", [P, EP + 1])
        edge = mem(top, "edge", [P, TILES, ROW])
        self_logit = mem(top, "self_logit", [P, TILES, H])
        row_of_source = mem(top, "row_of_source", [P, TILES], I32)
        src_row = mem(top, "src_row", [P, TILES], I32)
        dst_row = mem(top, "dst_row", [P, TILES], I32)
        scatter_row = mem(top, "scatter_row", [P, TILES], I32)
        src_f = mem(top, "src_f", [P, TILES])
        tiles_before = mem(top, "tiles_before", [P, TILES])
        not_above = mem(top, "not_above", [P, TILES])
        equal_to = mem(top, "equal_to", [P, TILES])
        ident = mem(top, "ident", [P, P])
        ones = mem(top, "ones", [P, P])
        eps = mem(top, "eps", [P, 1])
        w_heads = mem(top, "w_heads", [P, L, 2, D])
        w_row = mem(top, "w_row", [P, L, ROW])
        w_edge = mem(top, "w_edge", [D, L, EDGE_W])
        w_edge0 = mem(top, "w_edge0", [P, 2 * H])
        w_node = mem(top, "w_node", [D + 1, L, ROW])
        b_row = mem(top, "b_row", [P, L, ROW])
        b_all = mem(top, "b_all", [P, L])
        w_conv = mem(top, "w_conv", [P, 2 * D])
        w_conv3 = mem(top, "w_conv3", [D, 2 * D])
        bn_cols = mem(top, "bn_cols", [P, 5])
        limit = mem(top, "limit", [HALF, 2])
        steps = mem(top, "steps", [HALF + 1, 2, P + 2])
        bank = [top.enter_context(nc.psum_tensor(f"bank{n}", [P, 512], F32)) for n in range(8)]

        with ExitStack() as st:
            pad_i = mem(st, "pad_i", [1, 512], I32)
            last_keep = mem(st, "last_keep", [1, 4], U8)
            w_raw = mem(st, "w_raw", [P, L, H, D])
            a_raw = mem(st, "a_raw", [P, 2, L, H * D])
            prod = mem(st, "prod", [P, L, H * D])
            bias_raw = mem(st, "bias_raw", [P, L, H])
            hb = mem(st, "hb", [P, 1])
            w_sum = mem(st, "w_sum", [P, L, D])
            a_sum = mem(st, "a_sum", [P, 2, L, H])
            chain_t = mem(st, "chain_t", [D, L + 1, D])
            wsum_t = mem(st, "wsum_t", [D, L, D])
            c_col = mem(st, "c_col", [D, L + 1])
            c_rep = mem(st, "c_rep", [D, P])
            rows_i = mem(st, "rows_i", [HALF + 1, 4, 2, P], I32)
            rows_f = mem(st, "rows_f", [HALF + 1, 4, 2, P])
            ahead_i = mem(st, "ahead_i", [HALF + 1, 2, P], I32)
            ahead_f = mem(st, "ahead_f", [HALF + 1, 2, P])
            keep_u = mem(st, "keep_u", [HALF, 2, P], U8)
            dst_f = mem(st, "dst_f", [P, TILES])
            last_f = mem(st, "last_f", [P, TILES])
            tmp_f = mem(st, "tmp_f", [P, TILES])
            consts_set = sem(st, "consts_set")
            ident_ready = sem(st, "ident_ready")
            lists_padded = sem(st, "lists_padded")
            rows_loaded = sem(st, "rows_loaded")
            weights_loaded = sem(st, "weights_loaded")
            keep_stored = sem(st, "keep_stored")
            dve_step = sem(st, "dve_step")
            pe_step = sem(st, "pe_step")
            block = st.enter_context(nc.Block())
            WEIGHT_LOADS = 2 * (L + H + 1) + 2 + 2 + 3 + 2
            ROWS_CONVERTED, KEEP_READY, WEIGHTS_SUMMED = 1, 2, 41

            @block.gpsimd
            def _(pool):
                pool.memset(pad_i[:, 0:128], 0).then_inc(consts_set, 1)
                pool.memset(pad_i[:, 128:256], PAD_DST).then_inc(consts_set, 1)
                pool.memset(pad_i[:, 256:384], PAD_DST + 1).then_inc(consts_set, 1)
                pool.memset(pad_i[:, 384:448], -1).then_inc(consts_set, 1)
                pool.memset(pad_i[:, 448:512], 1).then_inc(consts_set, 1)
                pool.memset(last_keep[:], 0).then_inc(consts_set, 1)
                pool.memset(rows_i[:], 0).then_inc(consts_set, 1)
                pool.memset(ahead_i[:], 0).then_inc(consts_set, 1)
                pool.memset(ones[:], 1.0).then_inc(consts_set, 1)
                pool.memset(eps[:], EPS).then_inc(consts_set, 1)
                pool.memset(ident[:], 0.0).then_inc(consts_set, 1)
                pool.wait_ge(consts_set, 11)
                pool.affine_select(out=ident[:], in_=ident[:], compare_op=ALU.not_equal, fill=1.0, base=0,
                                   pattern=[[-1, P]], channel_multiplier=1).then_inc(ident_ready, 1)

            @block.sync
            def _(sp):
                sp.wait_ge(consts_set, 8)
                n_pad = EP - E
                for to, of in ((src_pad[0:E], one_row(src)), (src_pad[E:EP], pad_i[0:1, 0:n_pad]),
                               (dst_pad[1:1 + E], one_row(dst)), (dst_pad[1 + E:1 + EP], pad_i[0:1, 128:128 + n_pad]),
                               (dst_pad[0:1], pad_i[0:1, 384:385]), (dst_pad[1 + EP:1 + EP + P], pad_i[0:1, 256:384])):
                    sp.dma_start(one_row(to), of).then_inc(lists_padded, 16)
                sp.wait_ge(lists_padded, 6 * 16)
                half = lambda a: a.rearrange("(a k q) -> k a q", a=2, q=P)
                for n, a in enumerate((src_pad, dst_pad[1:1 + EP], dst_pad[0:EP], dst_pad[2:2 + EP])):
                    sp.dma_start(rows_i[0:HALF, n], half(a)).then_inc(rows_loaded, 16)
                sp.dma_start(ahead_i[0:HALF], half(dst_pad[1 + P:1 + P + EP])).then_inc(rows_loaded, 16)
                sp.dma_start(ahead_i[HALF:HALF + 1, 0], one_row(dst_pad[1:1 + P])).then_inc(rows_loaded, 16)
                sp.dma_start(rows_i[HALF:HALF + 1, 2, 0, 0:1], pad_i[0:1, 448:449]).then_inc(rows_loaded, 16)
                for r in (0, D):
                    for l in range(L):
                        sp.dma_start(w_raw[r:r + D, l].rearrange("p h o -> p (h o)"), Ws[l]).then_inc(weights_loaded, 16)
                    for h in range(H):
                        for_h = gat_bias[:, h * D:(h + 1) * D].rearrange("l f -> f l")
                        with nc.allow_non_contiguous_dma(reason="a few biases"):
                            sp.dma_start(bias_raw[r:r + D, :, h], for_h).then_inc(weights_loaded, 16)
                    sp.dma_start(hb[r:r + D], one_col(h_bias)).then_inc(weights_loaded, 16)
                for n, a in enumerate((attn_l, attn_r)):
                    flat = a.rearrange("l h f -> (l h f)")
                    sp.dma_start(a_raw[:, n].rearrange("p l n -> p (l n)"), lanes(flat, P)).then_inc(weights_loaded, 16)
                sp.dma_start(w_conv[:], W_full[0:P]).then_inc(weights_loaded, 16)
                sp.dma_start(w_conv3[:], W_full[P:P + D]).then_inc(weights_loaded, 16)
                for n, a in enumerate((b_full, bn1_g, bn1_b)):
                    sp.dma_start(bn_cols[:, n:n + 1], one_col(a)).then_inc(weights_loaded, 16)
                for n, a in enumerate((bn2_g, bn2_b)):
                    sp.dma_start(bn_cols[0:D, 3 + n:4 + n], one_col(a)).then_inc(weights_loaded, 16)
                sp.wait_ge(dve_step, KEEP_READY)
                sp.dma_start(half(keep_row[0:EP]), keep_u[:]).then_inc(keep_stored, 16)
                sp.dma_start(one_row(keep_row[EP:EP + 1]), last_keep[0:1, 0:1]).then_inc(keep_stored, 16)
                sp.wait_ge(keep_stored, 32)

            @block.vector
            def _(v):
                count = [0]

                def link(ins):
                    count[0] += 1
                    ins.then_inc(dve_step, 1)
                    v.wait_ge(dve_step, count[0])

                v.wait_ge(rows_loaded, 7 * 16)
                link(v.tensor_copy(rows_f[:], rows_i[:]))
                assert count[0] == ROWS_CONVERTED
                link(v.tensor_tensor(keep_u[:], rows_f[0:HALF, 1], rows_f[0:HALF, 2], ALU.is_equal))
                assert count[0] == KEEP_READY
                link(v.tensor_copy(ahead_f[:], ahead_i[:]))
                link(v.memset(steps[:], 1.0))
                link(v.tensor_tensor(steps[:, :, 1:2], rows_f[:, 1, :, P - 1:P], rows_f[:, 2, :, 0:1], ALU.subtract))
                link(v.tensor_tensor(steps[:, :, 2:2 + P], ahead_f[:], rows_f[:, 1], ALU.subtract))
                link(v.tensor_copy(limit[:], rows_f[0:HALF, 1, :, P - 1]))
                v.wait_ge(pe_step, 1)
                link(v.tensor_copy(src_f[:], bank[0][:, 0:TILES]))
                link(v.tensor_copy(dst_f[:], bank[1][:, 0:TILES]))
                link(v.tensor_tensor(last_f[:], dst_f[:], bank[2][:, 0:TILES], ALU.not_equal))
                link(v.tensor_copy(src_row[:], src_f[:]))
                link(v.tensor_scalar(tmp_f[:], dst_f[:], float(N - 1), None, ALU.min))
                link(v.tensor_copy(dst_row[:], tmp_f[:]))
                link(v.tensor_scalar(tmp_f[:], dst_f[:], float(-FAR), None, ALU.add))
                link(v.tensor_tensor(tmp_f[:], tmp_f[:], last_f[:], ALU.mult))
                link(v.tensor_scalar(tmp_f[:], tmp_f[:], float(FAR), None, ALU.add))
                link(v.tensor_copy(scatter_row[:], tmp_f[:]))
                v.wait_ge(weights_loaded, WEIGHT_LOADS * 16)
                link(v.tensor_reduce(w_sum[:], w_raw[:].rearrange("p l h o -> p l o h"), AX_X, ALU.add))
                for n in range(2):
                    link(v.tensor_tensor(prod[:], w_raw[:].rearrange("p l h o -> p l (h o)"), a_raw[:, n], ALU.mult))
                    link(v.tensor_reduce(a_sum[:, n], prod[:].rearrange("p l (h o) -> p l h o", h=H), AX_X, ALU.add))
                link(v.tensor_reduce(b_all[:], bias_raw[:], AX_X, ALU.add))
                link(v.tensor_tensor(b_all[:, L - 1:L], b_all[:, L - 1:L], hb[:], ALU.add))
                for h in range(H):
                    r = (h % 2) * D
                    link(v.tensor_copy(w_heads[r:r + D, :, h // 2, :], w_raw[r:r + D, :, h, :]))
                v.wait_ge(ident_ready, 1)
                link(v.memset(w_row[:], 0.0))
                link(v.memset(w_edge0[:], 0.0))
                eye = ident[0:D, 0:D].unsqueeze(1).broadcast_to([D, L, D])
                v.tensor_copy(w_row[0:D, :, 0:D], eye).then_inc(dve_step, 1)
                v.tensor_copy(w_row[0:D, 0:L - 1, D:ROW], a_sum[0:D, 0, 1:L]).then_inc(dve_step, 1)
                v.tensor_copy(w_edge[:, :, 0:D], eye).then_inc(dve_step, 1)
                v.tensor_copy(w_edge[:, :, D:D + H], a_sum[0:D, 1]).then_inc(dve_step, 1)
                v.tensor_tensor(w_edge[:, :, D + H:EDGE_W], a_sum[0:D, 0], a_sum[0:D, 1], ALU.add).then_inc(dve_step, 1)
                v.tensor_copy(w_edge0[0:D, 0:H], a_sum[0:D, 0, 0]).then_inc(dve_step, 1)
                v.tensor_copy(w_edge0[D:P, 0:H], a_sum[D:P, 1, 0]).then_inc(dve_step, 1)
                v.tensor_tensor(w_edge0[D:P, H:2 * H], a_sum[D:P, 0, 0], a_sum[D:P, 1, 0], ALU.add).then_inc(dve_step, 1)
                v.tensor_copy(chain_t[:, 0], ident[0:D, 0:D]).then_inc(dve_step, 1)
                v.memset(c_col[:, 0:1], 0.0).then_inc(dve_step, 1)
                count[0] += 10
                v.wait_ge(dve_step, count[0])
                v.tensor_copy(w_row[D:P, :, 0:D], w_sum[D:P]).then_inc(dve_step, 1)
                count[0] += 1
                assert count[0] == WEIGHTS_SUMMED, count
                for l in range(L):
                    v.wait_ge(pe_step, 2 + 2 * l)
                    v.tensor_copy(wsum_t[:, l], bank[3][0:D, 0:D]).then_inc(dve_step, 1)
                    v.tensor_copy(chain_t[:, l + 1], bank[3][0:D, D:2 * D]).then_inc(dve_step, 1)
                    v.tensor_tensor(c_col[:, l + 1:l + 2], bank[3][0:D, 2 * D:2 * D + 1], b_all[0:D, l:l + 1],
                                    ALU.add).then_inc(dve_step, 1)
                    v.tensor_scalar(c_rep[:], ones[0:D, :], b_all[0:D, l:l + 1], None, ALU.mult).then_inc(dve_step, 1)
                    v.wait_ge(pe_step, 3 + 2 * l)
                    if l < L - 1:
                        v.tensor_copy(w_row[D:P, l, D:ROW], bank[4][0:D, 0:H]).then_inc(dve_step, 1)
                    else:
                        v.memset(w_row[D:P, l, D:ROW], 0.0).then_inc(dve_step, 1)
                    v.tensor_copy(w_node[0:D, l], bank[4][0:D, 128:128 + ROW]).then_inc(dve_step, 1)
                    v.tensor_copy(w_node[D:D + 1, l], bank[4][0:1, 256:256 + ROW]).then_inc(dve_step, 1)
                    v.tensor_copy(b_row[:, l], bank[4][:, 384:384 + ROW]).then_inc(dve_step, 1)

            @block.tensor
            def _(t):
                t.wait_ge(ident_ready, 1)
                t.wait_ge(dve_step, 3)
                for n, src_rows in enumerate((0, 1, 3)):
                    for a in range(2):
                        last = t.transpose(bank[n][:, a * HALF:(a + 1) * HALF], rows_f[0:HALF, src_rows, a], ident[0:HALF, 0:HALF])
                last.then_inc(pe_step, 1)
                base = WEIGHTS_SUMMED
                t.wait_ge(dve_step, base)
                for l in range(L):
                    t.wait_ge(dve_step, base + 8 * l)
                    t.matmul(bank[3][0:D, 0:D], w_sum[0:D, l], ident[0:D, 0:D], start=True, stop=True)
                    t.matmul(bank[3][0:D, D:2 * D], w_sum[0:D, l], chain_t[:, l], start=True, stop=True)
                    t.matmul(bank[3][0:D, 2 * D:2 * D + 1], w_sum[0:D, l], c_col[:, l:l + 1], start=True, stop=True).then_inc(pe_step, 1)
                    t.wait_ge(dve_step, base + 8 * l + 4)
                    if l < L - 1:
                        t.matmul(bank[4][0:D, 0:H], wsum_t[:, l], w_row[0:D, l, D:ROW], start=True, stop=True)
                    t.matmul(bank[4][0:D, 128:128 + ROW], chain_t[:, l + 1], w_row[0:D, l], start=True, stop=True)
                    t.matmul(bank[4][0:1, 256:256 + ROW], c_col[:, l + 1:l + 2], w_row[0:D, l], start=True, stop=True)
                    t.matmul(bank[4][:, 384:384 + ROW], c_rep[:], w_row[0:D, l], start=True, stop=True).then_inc(pe_step, 1)


        with ExitStack() as st:
            got = mem(st, "got", [P, 2, TPG, 2, D])
            norm = mem(st, "norm", [P, 2, TPG, 2, D])
            square = mem(st, "square", [P, TPG * 2 * D])
            norm_t = mem(st, "norm_t", [P, GE])
            stat = mem(st, "stat", [P, 4, 8])
            logs = mem(st, "logs", [P, 8])
            nodes = mem(st, "nodes", [P, 2, NODE_T, D])
            n_centered = mem(st, "n_centered", [P, NODE_T, D])
            n_norm = mem(st, "n_norm", [P, NODE_T, D + 1])
            n_norm_t = mem(st, "n_norm_t", [D + 1, NODE_T * P])
            n_rows = mem(st, "n_rows", [P, L, TPG, ROW])
            n_stat = mem(st, "n_stat", [P, 4, NODE_T])
            n_logs = mem(st, "n_logs", [P, NODE_T])
            sources = mem(st, "sources", [HALF, GE], I32)
            reached = mem(st, "reached", [HALF + 1, 2, GE])
            matches = mem(st, "matches", [P, 2, P + 1])
            gathered = [pool_dma_sem(f"gathered{s}") for s in range(2)]
            nodes_in = [sem(st, f"nodes_in{s}") for s in range(2)]
            sources_in = sem(st, "sources_in")
            x_saved = [sem(st, f"x_saved{s}") for s in range(2)]
            rows_saved = sem(st, "rows_saved")
            vector_step = sem(st, "vector_step")
            scalar_step = sem(st, "scalar_step")
            tensor_step = sem(st, "tensor_step")
            paced = sem(st, "paced")
            sp_paced = sem(st, "sp_paced")
            V = Steps("sum", "mean", "centered", "reached_lo", "reached_hi", "n_sum", "n_mean", "n_centered",
                      "var", "n_var", "before0", "compare0", "not_above0", "compare1", "equal0",
                      "before1", "compare2", "not_above1", "compare3", "equal1",
                      "n_norm", "diff", "logit", "self", "x1_0", "x1_1")
            A = Steps("square", "n_square", "log", "rstd", "n_log", "n_rstd", "norm", "norm_t", "wide",
                      "n_t0", "n_t1", "rows00", "rows01", "rows10", "rows11")
            T = Steps("search", "norm_t", "logits", "n_t", "nodes0", "nodes1")
            ROWS0, ROWS1 = bank[4], bank[5]
            block = st.enter_context(nc.Block())

            @block.gpsimd
            def _(pool):
                for k in range(G):
                    s = k % 2
                    if k >= 2:
                        pool.wait_ge(vector_step, V.after(k, "centered", back=2))
                        pool.wait_ge(x_saved[s], 16 * (k // 2))
                    for t in range(TPG):
                        for side, rows in enumerate((src_row, dst_row)):
                            pool.indirect_dma_start(
                                out=got[:, s, t, side, 0:D], out_offset=None, in_=x,
                                in_offset=bass.IndirectOffsetOnAxis(ap=rows[:, TPG * k + t:TPG * k + t + 1], axis=0),
                            ).then_inc(gathered[s], 16)

            @block.sync
            def _(sp):
                def load(k, s):
                    lanes_used = P
                    if isinstance(k, int) and k == G - 1:
                        lanes_used = LAST_P
                    first = x[bass.ds(k * GN, lanes_used * NODE_T)]
                    sp.wait_ge(vector_step, V.after(k, "x1_1", back=2))
                    sp.sem_inc(sp_paced, 1)
                    sp.dma_start(nodes[0:lanes_used, s], first.rearrange("(p j) f -> p j f", j=NODE_T)).then_inc(nodes_in[s], 16)
                    sp.wait_ge(vector_step, V.after(k, "reached_hi", back=1))
                    sp.sem_inc(sp_paced, 1)
                    sp.dma_start(sources[:], lanes(src_pad[bass.ds(k * GE, GE)], HALF)).then_inc(sources_in, 16)

                def body(k, group, s, turn):
                    if not (isinstance(k, int) and k == G - 1):
                        load(k + 1, 1 - s)
                    sp.wait_ge(gathered[s], turn * (16 * 8) + 16 * 8)
                    sp.sem_inc(sp_paced, 1)
                    sp.dma_start(x_dst.rearrange("p (t f) -> p t f", f=D)[:, bass.ds(k * TPG, TPG)],
                                 got[:, s, :, 1, 0:D]).then_inc(x_saved[s], 16)
                    used = LAST_P if isinstance(k, int) and k == G - 1 else P
                    for half in range(2):
                        sp.wait_ge(scalar_step, A.after(k, f"rows{half}1"))
                        sp.sem_inc(sp_paced, 1)
                        sp.wait_ge(vector_step, V.after(k, f"x1_{half}"))
                        sp.sem_inc(sp_paced, 1)
                        for l in range(L):
                            to = tables[l][bass.ds(k * GN, used * NODE_T)].rearrange("(p j) w -> p (j w)", j=NODE_T)
                            sp.dma_start(to[:, half * TPG * ROW:(half + 1) * TPG * ROW],
                                         n_rows[0:used, l].rearrange("p j w -> p (j w)")).then_inc(rows_saved, 16)

                sp.sem_inc(rows_saved, 16 * L)
                load(0, 0)
                ascending(sp, body, turns=G // 2 - 1)
                sp.wait_ge(x_saved[0], 16 * (G // 2 + 1))
                sp.wait_ge(x_saved[1], 16 * (G // 2))
                sp.wait_ge(rows_saved, 16 * L * (2 * G + 1))

            @block.vector
            def _(v):
                v.sem_inc(vector_step, V.start)
                v.memset(reached[:], 1.0).then_inc(paced, 1)
                v.memset(n_norm[:], 1.0).then_inc(paced, 1)
                v.memset(n_rows[:], 0.0).then_inc(paced, 1)
                v.wait_ge(paced, 3)

                def body(k, group, s, turn):
                    def own(name):
                        v.wait_ge(vector_step, V.after(k, name))

                    tiles = bass.ds(k * TPG, TPG)
                    rows = got[:, s, :, :, 0:D]
                    v.wait_ge(gathered[s], turn * (16 * 8) + 16 * 8)
                    v.tensor_reduce(stat[:, 0], rows, AX_X, ALU.add).then_inc(vector_step, 1)
                    own("sum")
                    v.tensor_scalar(stat[:, 1], stat[:, 0], 1.0 / D, None, ALU.mult).then_inc(vector_step, 1)
                    own("mean")
                    v.wait_ge(tensor_step, T.after(k, "norm_t", back=2))
                    v.tensor_tensor(norm[:, s], rows, inner(stat[:, 1].rearrange("p (t e) -> p t e", e=2), [P, TPG, 2, D]),
                                    ALU.subtract).then_inc(vector_step, 1)
                    v.wait_ge(sources_in, k * 16 + 16)
                    v.wait_ge(tensor_step, T.after(k, "search", back=1))
                    for a in range(2):
                        v.tensor_scalar(reached[0:HALF, a], sources[:], limit[:, a:a + 1], None, ALU.is_ge).then_inc(vector_step, 1)
                    v.wait_ge(nodes_in[s], turn * 16 + 16)
                    v.tensor_reduce(n_stat[:, 0], nodes[:, s], AX_X, ALU.add).then_inc(vector_step, 1)
                    own("n_sum")
                    v.tensor_scalar(n_stat[:, 1], n_stat[:, 0], 1.0 / D, None, ALU.mult).then_inc(vector_step, 1)
                    own("n_mean")
                    v.tensor_tensor(n_centered[:], nodes[:, s], inner(n_stat[:, 1], [P, NODE_T, D]), ALU.subtract).then_inc(vector_step, 1)
                    v.wait_ge(scalar_step, A.after(k, "square"))
                    v.tensor_reduce(stat[:, 2], square[:].rearrange("p (t f) -> p t f", f=D), AX_X, ALU.add).then_inc(vector_step, 1)
                    v.wait_ge(scalar_step, A.after(k, "n_square"))
                    v.tensor_reduce(n_stat[:, 2], square[:].rearrange("p (t f) -> p t f", f=D), AX_X, ALU.add).then_inc(vector_step, 1)
                    v.wait_ge(tensor_step, T.after(k, "search"))
                    for pair in range(2):
                        found = (bank[7][:, 0:2 * (P + 2)] if pair == 0 else bank[1][:, 64:64 + 2 * (P + 2)])
                        found = found.rearrange("p (t q) -> p t q", q=P + 2)
                        two = bass.ds(k * TPG + 2 * pair, 2)
                        mine = inner(src_f[:, two], [P, 2, P + 1])
                        v.tensor_scalar(tiles_before[:, two], found[:, :, 0], -1.0, None, ALU.add).then_inc(vector_step, 1)
                        v.tensor_tensor(matches[:], found[:, :, 1:], mine, ALU.is_le).then_inc(vector_step, 1)
                        own(f"compare{2 * pair}")
                        v.sem_inc(paced, 1)
                        v.tensor_reduce(not_above[:, two], matches[:], AX_X, ALU.add).then_inc(vector_step, 1)
                        own(f"not_above{pair}")
                        v.tensor_tensor(matches[:], found[:, :, 1:], mine, ALU.is_equal).then_inc(vector_step, 1)
                        own(f"compare{2 * pair + 1}")
                        v.sem_inc(paced, 1)
                        v.tensor_reduce(equal_to[:, two], matches[:], AX_X, ALU.add).then_inc(vector_step, 1)
                        own(f"equal{pair}")
                    v.wait_ge(scalar_step, A.after(k, "n_rstd"))
                    v.wait_ge(tensor_step, T.after(k, "n_t", back=1))
                    v.scalar_tensor_tensor(out=n_norm[:, :, 0:D], in0=n_centered[:], scalar=0.0, in1=inner(n_stat[:, 3], [P, NODE_T, D]),
                                           op0=ALU.max, op1=ALU.mult).then_inc(vector_step, 1)
                    v.wait_ge(scalar_step, A.after(k, "norm"))
                    v.tensor_tensor(edge[:, tiles, 0:D], norm[:, s, :, 0], norm[:, s, :, 1], ALU.subtract).then_inc(vector_step, 1)
                    v.wait_ge(tensor_step, T.after(k, "logits"))
                    both = bank[1][:, 0:TPG * 2 * H].rearrange("p (t e) -> p t e", e=2 * H)
                    v.tensor_scalar(edge[:, tiles, D:ROW], both[:, :, 0:H], 0.0, None, ALU.add).then_inc(vector_step, 1)
                    v.tensor_scalar(self_logit[:, tiles], both[:, :, H:], 0.0, None, ALU.add).then_inc(vector_step, 1)
                    for half in range(2):
                        v.wait_ge(tensor_step, T.after(k, f"nodes{half}"))
                        v.wait_ge(rows_saved, k * (2 * 16 * L) + (half + 1) * 16 * L)
                        v.tensor_tensor(n_rows[:, L - 1, :, 0:D], bank[6][:, half * 256:half * 256 + TPG * D].rearrange("p (j f) -> p j f", f=D),
                                        nodes[:, s, half * TPG:(half + 1) * TPG], ALU.add).then_inc(vector_step, 1)

                ascending(v, body)

            @block.scalar
            def _(s_):
                s_.preload_act_table_set(ACT_TABLES)
                s_.sem_inc(scalar_step, A.start)

                def body(k, group, s, turn):
                    def own(name):
                        s_.wait_ge(scalar_step, A.after(k, name))

                    s_.wait_ge(vector_step, V.after(k, "centered"))
                    s_.wait_ge(vector_step, V.after(k, "n_var", back=1))
                    s_.activation(square[:], norm[:, s].rearrange("p t e f -> p (t e f)"), ACT.Square).then_inc(scalar_step, 1)
                    s_.wait_ge(vector_step, V.after(k, "n_centered"))
                    s_.wait_ge(vector_step, V.after(k, "var"))
                    s_.activation(square[:], n_centered[:].rearrange("p t f -> p (t f)"), ACT.Square).then_inc(scalar_step, 1)
                    s_.activation(logs[:], stat[:, 2], ACT.Ln, bias=eps[:], scale=1.0 / D).then_inc(scalar_step, 1)
                    own("log")
                    s_.activation(stat[:, 3], logs[:], ACT.Exp, scale=-0.5).then_inc(scalar_step, 1)
                    s_.wait_ge(vector_step, V.after(k, "n_var"))
                    s_.activation(n_logs[:], n_stat[:, 2], ACT.Ln, bias=eps[:], scale=1.0 / D).then_inc(scalar_step, 1)
                    own("n_log")
                    s_.activation(n_stat[:, 3], n_logs[:], ACT.Exp, scale=-0.5).then_inc(scalar_step, 1)
                    for n in range(TPG * 2):
                        part = norm[:, s, n // 2, n % 2]
                        last = s_.activation(part, part, ACT.Relu, scale=stat[:, 3, n:n + 1])
                    last.then_inc(scalar_step, 1)
                    s_.wait_ge(tensor_step, T.after(k, "norm_t"))
                    s_.activation(norm_t[:], bank[0][:], ACT.Copy).then_inc(scalar_step, 1)
                    s_.activation(wide[D:P, bass.ds(k * GE + 1, GE)], bank[0][D:P, :], ACT.Copy).then_inc(scalar_step, 1)
                    s_.wait_ge(tensor_step, T.after(k, "n_t"))
                    for half in range(2):
                        s_.activation(n_norm_t[:, half * GE:(half + 1) * GE], bank[2 + half][0:D + 1, :], ACT.Copy).then_inc(scalar_step, 1)
                    for half in range(2):
                        s_.wait_ge(tensor_step, T.after(k, f"nodes{half}"))
                        s_.wait_ge(rows_saved, k * (2 * 16 * L) + (half + 1) * 16 * L)
                        for n, rows in enumerate((ROWS0, ROWS1)):
                            s_.activation(n_rows[:, 0:L - 1, 2 * n:2 * n + 2].rearrange("p l j w -> p j l w"),
                                          rows[:, 0:2 * 3 * ROW].rearrange("p (j l w) -> p j l w", j=2, w=ROW), ACT.Copy).then_inc(scalar_step, 1)

                ascending(s_, body)

            @block.tensor
            def _(t_):
                t_.sem_inc(tensor_step, T.start)

                def body(k, group, s, turn):
                    t_.wait_ge(vector_step, V.after(k, "reached_hi"))
                    t_.wait_ge(vector_step, V.after(k, "self", back=1))
                    for t in range(TPG):
                        to = (bank[7] if t < 2 else bank[1])
                        at = (0 if t < 2 else 64) + (t % 2) * (P + 2)
                        t_.matmul(to[:, at:at + P + 2], reached[:, 0, t * P:(t + 1) * P], steps[:, 0], start=True, stop=False)
                        last = t_.matmul(to[:, at:at + P + 2], reached[0:HALF, 1, t * P:(t + 1) * P], steps[0:HALF, 1], start=False, stop=True)
                    last.then_inc(tensor_step, 1)
                    t_.wait_ge(scalar_step, A.after(k, "norm"))
                    t_.wait_ge(scalar_step, A.after(k, "wide", back=1))
                    for t in range(TPG):
                        last = t_.transpose(bank[0][:, t * P:(t + 1) * P], norm[:, s, t].rearrange("p e f -> p (e f)"), ident[:])
                    last.then_inc(tensor_step, 1)
                    t_.wait_ge(scalar_step, A.after(k, "norm_t"))
                    t_.wait_ge(vector_step, V.after(k, "equal1"))
                    for t in range(TPG):
                        last = t_.matmul(bank[1][:, t * 2 * H:(t + 1) * 2 * H], norm_t[:, t * P:(t + 1) * P], w_edge0[:], start=True, stop=True)
                    last.then_inc(tensor_step, 1)
                    t_.wait_ge(vector_step, V.after(k, "n_norm"))
                    t_.wait_ge(scalar_step, A.after(k, "n_t1", back=1))
                    for j in range(NODE_T):
                        last = t_.transpose(bank[2 + j // TPG][0:D + 1, (j % TPG) * P:(j % TPG + 1) * P], n_norm[:, j], ident[:])
                    last.then_inc(tensor_step, 1)
                    for half in range(2):
                        t_.wait_ge(scalar_step, A.after(k, f"n_t{half}"))
                        if half == 0:
                            t_.wait_ge(scalar_step, A.after(k, "rows11", back=1))
                            t_.wait_ge(vector_step, V.after(k, "x1_1", back=1))
                        else:
                            t_.wait_ge(scalar_step, A.after(k, "rows01"))
                            t_.wait_ge(vector_step, V.after(k, "x1_0"))
                        for j in range(TPG):
                            lhs = n_norm_t[:, (half * TPG + j) * P:(half * TPG + j + 1) * P]
                            t_.matmul((ROWS0, ROWS1)[j // 2][:, (j % 2) * 3 * ROW:(j % 2 + 1) * 3 * ROW], lhs,
                                      w_node[:, 0:3].rearrange("p l w -> p (l w)"), start=True, stop=True)
                            last = t_.matmul(bank[6][:, half * 256 + j * D:half * 256 + (j + 1) * D], lhs, w_node[:, 3, 0:D], start=True, stop=True)
                        last.then_inc(tensor_step, 1)

                ascending(t_, body)

        def softmax_weights(l, alpha):
            with ExitStack() as st:
                leaky = mem(st, f"leaky_{l}", [P, 2, CT, Q])
                logit = mem(st, f"logit_{l}", [Q, 2, CE])
                fwd = mem(st, f"fwd_{l}", [Q, CE])
                rev = mem(st, f"rev_{l}", [Q, CE])
                stop_q = mem(st, f"stop_q_{l}", [Q, CE + 1])
                ends = mem(st, f"ends_{l}", [1, 2, Q])
                chain = mem(st, f"chain_{l}", [1, 2, 2, Q + H])
                carry = mem(st, f"carry_{l}", [Q, 2])
                own = sem(st, f"own_{l}")
                leaky_ready = sem(st, f"leaky_ready_{l}")
                logit_t = sem(st, f"logit_t_{l}")
                logit_ready = sem(st, f"logit_ready_{l}")
                scanned = sem(st, f"scanned_{l}")
                ends_t = sem(st, f"ends_t_{l}")
                chained = sem(st, f"chained_{l}")
                carry_t = sem(st, f"carry_t_{l}")
                shifted = sem(st, f"shifted_{l}")
                exped = sem(st, f"exped_{l}")
                alpha_q = sem(st, f"alpha_q_{l}")
                alpha_t = sem(st, f"alpha_t_{l}")
                block = st.enter_context(nc.Block())

                @block.vector
                def _(v):
                    count = [0]

                    def link(ins):
                        count[0] += 1
                        ins.then_inc(own, 1)
                        v.wait_ge(own, count[0])

                    for n, e in enumerate((edge[:, :, D:ROW], self_logit[:])):
                        for b in range(CT):
                            of = e[:, b:TILES:CT]
                            v.scalar_tensor_tensor(out=leaky[:, n, b].rearrange("p (s h) -> p s h", h=H), in0=of, scalar=SLOPE,
                                                   in1=of, op0=ALU.mult, op1=ALU.max).then_inc(leaky_ready, 1)
                    link(v.tensor_scalar(stop_q[:], keep_q[:], -1.0, BIG, ALU.add, ALU.mult))
                    link(v.memset(chain[:, 0], -BIG))
                    link(v.memset(chain[:, 1], 0.0))
                    v.wait_ge(logit_ready, 4)

                    def both_ways(n, gate, op0, op1, start, values):
                        before = dict(data0=gate[:, 0:CE], data1=values, op0=op0, op1=op1)
                        behind = dict(data0=gate[:, 1:CE + 1][:, ::-1], data1=values[:, ::-1], op0=op0, op1=op1)
                        link(v.tensor_tensor_scan(out=fwd[:], initial=start, **before))
                        link(v.tensor_tensor_scan(out=rev[:, ::-1], initial=start, **behind))
                        v.sem_inc(scanned, 1)
                        v.wait_ge(ends_t, 2 * n + 2)
                        for side in range(2):
                            link(v.tensor_copy(ends[:, side], bank[side][0:1, 0:Q]))
                        for h in range(H):
                            way = lambda a, skip: a[:, skip + h:skip + Q:H]
                            link(v.tensor_tensor_scan(out=way(chain[:, n, 0], H), data0=way(carry_in[:, 2 - 2 * n], 0),
                                                      data1=way(ends[:, 0], 0), initial=start, op0=op0, op1=op1))
                            link(v.tensor_tensor_scan(out=way(chain[:, n, 1], 0)[:, ::-1], data0=way(carry_in[:, 3 - 2 * n], 0)[:, ::-1],
                                                      data1=way(ends[:, 1], 0)[:, ::-1], initial=start, op0=op0, op1=op1))
                        v.sem_inc(chained, 1)
                        v.wait_ge(carry_t, 2 * n + 2)
                        link(v.tensor_copy(carry[:], bank[2][0:Q, 0:2]))
                        link(v.tensor_tensor_scan(out=fwd[:], initial=carry[:, 0:1], **before))
                        link(v.tensor_tensor_scan(out=rev[:, ::-1], initial=carry[:, 1:2], **behind))

                    both_ways(0, stop_q, ALU.add, ALU.max, -BIG, logit[:, 0])
                    link(v.tensor_tensor(fwd[:], fwd[:], rev[:], ALU.max))
                    link(v.tensor_tensor(fwd[:], fwd[:], logit[:, 1], ALU.max))
                    for n in range(2):
                        v.tensor_tensor(logit[:, n], logit[:, n], fwd[:], ALU.subtract).then_inc(shifted, 1)
                    v.wait_ge(exped, 2)
                    both_ways(1, keep_q, ALU.mult, ALU.add, 0.0, logit[:, 0])
                    link(v.tensor_tensor(rev[:], rev[:], logit[:, 0], ALU.subtract))
                    link(v.tensor_tensor(fwd[:], fwd[:], rev[:], ALU.add))
                    link(v.tensor_tensor(fwd[:], fwd[:], logit[:, 1], ALU.add))
                    link(v.reciprocal(fwd[:], fwd[:]))
                    v.tensor_tensor(logit[:, 0], logit[:, 0], fwd[:], ALU.mult).then_inc(alpha_q, 1)
                    to = alpha[:].rearrange("p (s b) h -> p s b h", b=CT)
                    for n, (b0, b1) in enumerate(((0, 4), (4, CT))):
                        v.wait_ge(alpha_t, n + 1)
                        link(v.tensor_copy(to[:, :, b0:b1], bank[4 + n][:, 0:(b1 - b0) * Q].rearrange("p (b s h) -> p s b h", s=CH, h=H)))

                @block.scalar
                def _(s_):
                    for n in range(2):
                        for m in range(2):
                            cols = GE if m == 0 else CE - GE
                            s_.wait_ge(logit_t, 2 * n + m + 1)
                            s_.activation(logit[:, n, m * GE:m * GE + cols], bank[2 * n + m][0:Q, 0:cols], ACT.Copy).then_inc(logit_ready, 1)
                    for n in range(2):
                        s_.wait_ge(shifted, n + 1)
                        s_.activation(logit[:, n], logit[:, n], ACT.Exp).then_inc(exped, 1)

                @block.tensor
                def _(t):
                    for n in range(2):
                        t.wait_ge(leaky_ready, CT * (n + 1))
                        for b in range(CT):
                            last = t.transpose(bank[2 * n + b // 4][0:Q, (b % 4) * P:(b % 4 + 1) * P], leaky[:, n, b], ident[:])
                            if b == 3:
                                last.then_inc(logit_t, 1)
                        last.then_inc(logit_t, 1)
                    t.wait_ge(logit_ready, 4)
                    for n in range(2):
                        t.wait_ge(scanned, n + 1)
                        t.matmul(bank[0][0:1, 0:Q], fwd[:, CE - 1:CE], ident[0:Q, 0:Q], start=True, stop=True).then_inc(ends_t, 1)
                        t.matmul(bank[1][0:1, 0:Q], rev[:, 0:1], ident[0:Q, 0:Q], start=True, stop=True).then_inc(ends_t, 1)
                        t.wait_ge(chained, n + 1)
                        t.matmul(bank[2][0:Q, 0:1], chain[:, n, 0, 0:Q], ones[0:1, 0:1], start=True, stop=True).then_inc(carry_t, 1)
                        t.matmul(bank[2][0:Q, 1:2], chain[:, n, 1, H:H + Q], ones[0:1, 0:1], start=True, stop=True).then_inc(carry_t, 1)
                    t.wait_ge(alpha_q, 1)
                    for b in range(CT):
                        last = t.transpose(bank[4 + b // 4][:, (b % 4) * Q:(b % 4 + 1) * Q], logit[:, 0, b * P:(b + 1) * P], ident[0:Q, 0:Q])
                        if b == 3:
                            last.then_inc(alpha_t, 1)
                    last.then_inc(alpha_t, 1)

        def messages(l, alpha):
            with ExitStack() as st:
                scaled = mem(st, f"scaled_{l}", [P, 2, TPG, H, D])
                scaled_t = mem(st, f"scaled_t_{l}", [P, 2, GE])
                ring = mem(st, f"ring_{l}", [P, 2, GE])
                rows = mem(st, f"rows_{l}", [P, 2, TPG, ROW])
                x_again = mem(st, f"x_again_{l}", [P, 2, TPG, D]) if l == L - 1 else None
                keep = mem(st, f"keep_{l}", [D, 2, GE], U8)
                keep_in = [sem(st, f"keep_in_{l}_{s}") for s in range(2)]
                x_in = [sem(st, f"x_in_{l}_{s}") for s in range(2)]
                saved = [sem(st, f"saved_{l}_{s}") for s in range(2)]
                scaled_ready = sem(st, f"scaled_ready_{l}")
                scaled_in_psum = sem(st, f"scaled_in_psum_{l}")
                scaled_t_ready = sem(st, f"scaled_t_ready_{l}")
                message_ready = sem(st, f"message_ready_{l}")
                summed = sem(st, f"summed_{l}")
                ring_ready = sem(st, f"ring_ready_{l}")
                rows_in_psum = sem(st, f"rows_in_psum_{l}")
                rows_ready = sem(st, f"rows_ready_{l}")
                x_added = sem(st, f"x_added_{l}")
                act_paced = sem(st, f"act_paced_{l}")
                sp_paced = sem(st, f"sp_paced_{l}")
                block = st.enter_context(nc.Block())
                last_step = l == L - 1

                @block.sync
                def _(sp):
                    def load(k, g, s, turn):
                        sp.wait_ge(summed, at(k, back=2))
                        sp.sem_inc(sp_paced, 1)
                        sp.dma_start(keep[:, s], lanes(keep_row[bass.ds(g * GE, GE)], D)).then_inc(keep_in[s], 16)
                        if last_step:
                            sp.wait_ge(x_added, at(k, back=2))
                            sp.sem_inc(sp_paced, 1)
                            sp.dma_start(x_again[:, s], x_dst.rearrange("p (t f) -> p t f", f=D)[:, bass.ds(g * TPG, TPG)]).then_inc(x_in[s], 16)

                    def save(k, g, s, turn):
                        sp.wait_ge(x_added if last_step else rows_ready, at(k))
                        sp.sem_inc(sp_paced, 1)
                        sp.dma_start(tables[l][N:N + EP].rearrange("(p t) w -> p t w", p=P)[:, bass.ds(g * TPG, TPG)],
                                     rows[:, s]).then_inc(saved[s], 16)

                    for s in range(2):
                        sp.sem_inc(saved[s], 32)
                    pipelined(sp, ((1, load), (4, save)))
                    sp.wait_ge(saved[0], 16 * (G // 2 + 1) + 32)
                    sp.wait_ge(saved[1], 16 * (G // 2) + 32)

                @block.vector
                def _(v):
                    for signal in (scaled_ready, summed, rows_ready, x_added):
                        v.sem_inc(signal, AHEAD)

                    def scale(k, g, s, turn):
                        tiles = bass.ds(g * TPG, TPG)
                        v.wait_ge(scaled_in_psum, at(k, back=2))
                        v.tensor_tensor(scaled[:, s], edge[:, tiles, 0:D].unsqueeze(2).broadcast_to([P, TPG, H, D]),
                                        inner(alpha[:, tiles], [P, TPG, H, D]), ALU.mult).then_inc(scaled_ready, 1)

                    def scan(k, g, s, turn):
                        v.wait_ge(keep_in[s], turn * 16 + 16)
                        v.wait_ge(message_ready, at(k))
                        v.wait_ge(summed, at(k, back=1))
                        v.tensor_tensor_scan(out=wide[0:D, bass.ds(g * GE + 1, GE)], data0=keep[:, s], data1=bank[2 + s][0:D],
                                             initial=wide[0:D, bass.ds(g * GE, 1)], op0=ALU.mult, op1=ALU.add).then_inc(summed, 1)

                    def stage(k, g, s, turn):
                        v.wait_ge(rows_in_psum, at(k))
                        v.wait_ge(saved[s], turn * 16 + 32)
                        v.tensor_tensor(rows[:, s], bank[4 + s][:, 0:TPG * ROW].rearrange("p (t w) -> p t w", w=ROW),
                                        b_row[:, l].unsqueeze(1).broadcast_to([P, TPG, ROW]), ALU.add).then_inc(rows_ready, 1)
                        if last_step:
                            v.wait_ge(rows_ready, at(k))
                            v.wait_ge(x_in[s], turn * 16 + 16)
                            v.tensor_tensor(rows[:, s, :, 0:D], rows[:, s, :, 0:D], x_again[:, s], ALU.add).then_inc(x_added, 1)

                    v.memset(wide[0:D, 0:1], 0.0).then_inc(sp_paced, 1)
                    pipelined(v, ((0, scale), (2, scan), (3, stage)))

                @block.scalar
                def _(s_):
                    s_.preload_act_table_set(ACT_TABLES)
                    for signal in (scaled_t_ready, ring_ready):
                        s_.sem_inc(signal, AHEAD)

                    def take(k, g, s, turn):
                        s_.wait_ge(scaled_in_psum, at(k))
                        s_.wait_ge(message_ready, at(k, back=1))
                        s_.activation(scaled_t[:, 0], bank[0][:], ACT.Copy)
                        s_.activation(scaled_t[:, 1], bank[1][:], ACT.Copy).then_inc(scaled_t_ready, 1)

                    def to_ring(k, g, s, turn):
                        s_.wait_ge(summed, at(k))
                        s_.wait_ge(rows_in_psum, at(k, back=2))
                        s_.sem_inc(act_paced, 1)
                        s_.activation(ring[:, s], wide[:, bass.ds(g * GE + 1, GE)], ACT.Copy).then_inc(ring_ready, 1)

                    pipelined(s_, ((1, take), (2, to_ring)))

                @block.tensor
                def _(t_):
                    for signal in (scaled_in_psum, message_ready, rows_in_psum):
                        t_.sem_inc(signal, AHEAD)

                    def transpose(k, g, s, turn):
                        t_.wait_ge(scaled_ready, at(k))
                        t_.wait_ge(scaled_t_ready, at(k, back=1))
                        for t in range(TPG):
                            for pair in range(2):
                                last = t_.transpose(bank[pair][:, t * P:(t + 1) * P],
                                                    scaled[:, s, t, 2 * pair:2 * pair + 2].rearrange("p h f -> p (h f)"), ident[:])
                        last.then_inc(scaled_in_psum, 1)

                    def message(k, g, s, turn):
                        t_.wait_ge(scaled_t_ready, at(k))
                        t_.wait_ge(summed, at(k, back=2))
                        for pair in range(2):
                            last = t_.matmul(bank[2 + s][0:D], w_heads[:, l, pair], scaled_t[:, pair], start=pair == 0, stop=pair == 1)
                        last.then_inc(message_ready, 1)

                    def next_rows(k, g, s, turn):
                        t_.wait_ge(ring_ready, at(k))
                        t_.wait_ge(rows_ready, at(k, back=2))
                        for t in range(TPG):
                            last = t_.matmul(bank[4 + s][:, t * ROW:(t + 1) * ROW], ring[:, s, t * P:(t + 1) * P], w_row[:, l],
                                             start=True, stop=True)
                        last.then_inc(rows_in_psum, 1)

                    pipelined(t_, ((1, transpose), (2, message), (3, next_rows)))

        def spread(l):
            with ExitStack() as st:
                keep = mem(st, f"keep_next_{l}", [D, 2, GE], U8)
                ended = mem(st, f"ended_{l}", [D, 2, GE])
                h_new = mem(st, f"h_new_{l}", [D, 2, GE])
                h_full = mem(st, f"h_full_{l}", [D, 2, GE])
                keep_in = [sem(st, f"next_in_{l}_{s}") for s in range(2)]
                gathered = [pool_dma_sem(f"rows_gathered_{l}_{s}") for s in range(2)]
                through = sem(st, f"through_{l}")
                ended_ready = sem(st, f"ended_ready_{l}")
                spread_out = sem(st, f"spread_{l}")
                full_ready = sem(st, f"full_ready_{l}")
                wide_ready = sem(st, f"wide_ready_{l}")
                dst_in_psum = sem(st, f"dst_in_psum_{l}")
                self_ready = sem(st, f"self_ready_{l}")
                sp_paced = sem(st, f"sp_paced2_{l}")
                block = st.enter_context(nc.Block())

                @block.gpsimd
                def _(pool):
                    for k in range(G):
                        g, s = G - 1 - k, k % 2
                        if k >= 2:
                            pool.wait_ge(gathered[s], 16 * TPG * (k // 2))
                        for t in range(TPG):
                            at_tile = TPG * g + t
                            pool.indirect_dma_start(
                                out=edge[:, at_tile], out_offset=None, in_=tables[l],
                                in_offset=bass.IndirectOffsetOnAxis(ap=row_of_source[:, at_tile:at_tile + 1], axis=0),
                            ).then_inc(gathered[s], 16)

                @block.sync
                def _(sp):
                    def load(k, g, s, turn):
                        sp.wait_ge(spread_out, at(k, back=2))
                        sp.sem_inc(sp_paced, 1)
                        sp.dma_start(keep[:, s], lanes(keep_row[bass.ds(g * GE + 1, GE)], D)).then_inc(keep_in[s], 16)

                    pipelined(sp, ((0, load),), down=True)

                @block.tensor
                def _(t_):
                    for signal in (through, dst_in_psum):
                        t_.sem_inc(signal, AHEAD)

                    def weights(k, g, s, turn):
                        t_.wait_ge(ended_ready, at(k, back=2))
                        t_.matmul(bank[s][0:D], w_row[:, l, 0:D], wide[:, bass.ds(g * GE + 1, GE)], start=True, stop=True).then_inc(through, 1)

                    def dst_side(k, g, s, turn):
                        t_.wait_ge(full_ready, at(k))
                        t_.wait_ge(self_ready, at(k, back=2))
                        for t in range(TPG):
                            last = t_.matmul(bank[2 + s][:, t * EDGE_W:(t + 1) * EDGE_W], h_full[:, s, t * P:(t + 1) * P], w_edge[:, l + 1],
                                             start=True, stop=True)
                        last.then_inc(dst_in_psum, 1)

                    pipelined(t_, ((0, weights), (2, dst_side)), down=True)

                @block.vector
                def _(v):
                    for signal in (ended_ready, spread_out, self_ready):
                        v.sem_inc(signal, AHEAD)
                    v.memset(h_new[:, 1, 0:1], 0.0).then_inc(sp_paced, 1)

                    def end(k, g, s, turn):
                        v.wait_ge(keep_in[s], turn * 16 + 16)
                        v.wait_ge(through, at(k))
                        v.scalar_tensor_tensor(out=ended[:, s], in0=keep[:, s], scalar=0.0, in1=bank[s][0:D],
                                               op0=ALU.is_equal, op1=ALU.mult).then_inc(ended_ready, 1)

                    def back(k, g, s, turn):
                        v.wait_ge(ended_ready, at(k))
                        v.wait_ge(spread_out, at(k, back=1))
                        v.wait_ge(wide_ready, at(k, back=2))
                        v.tensor_tensor_scan(out=h_new[:, s, ::-1], data0=keep[:, s, ::-1], data1=ended[:, s, ::-1],
                                             initial=h_new[:, 1 - s, 0:1], op0=ALU.mult, op1=ALU.add).then_inc(spread_out, 1)

                    def combine(k, g, s, turn):
                        tiles = bass.ds(g * TPG, TPG)
                        here = bank[2 + s][:, 0:TPG * EDGE_W].rearrange("p (t w) -> p t w", w=EDGE_W)
                        v.wait_ge(gathered[s], turn * (16 * TPG) + 16 * TPG)
                        v.wait_ge(dst_in_psum, at(k))
                        v.tensor_tensor(edge[:, tiles, 0:D], edge[:, tiles, 0:D], here[:, :, 0:D], ALU.subtract)
                        v.tensor_tensor(edge[:, tiles, D:ROW], edge[:, tiles, D:ROW], here[:, :, D:D + H], ALU.add)
                        v.tensor_scalar(self_logit[:, tiles], here[:, :, D + H:], 0.0, None, ALU.add).then_inc(self_ready, 1)

                    pipelined(v, ((1, end), (1, back), (3, combine)), down=True)

                @block.scalar
                def _(s_):
                    s_.preload_act_table_set(ACT_TABLES)
                    for signal in (full_ready, wide_ready):
                        s_.sem_inc(signal, AHEAD)

                    def finish(k, g, s, turn):
                        s_.wait_ge(spread_out, at(k))
                        s_.wait_ge(dst_in_psum, at(k, back=2))
                        s_.activation(h_full[:, s], h_new[:, s], ACT.Identity, bias=b_all[0:D, l:l + 1]).then_inc(full_ready, 1)
                        s_.wait_ge(through, at(k))
                        s_.activation(wide[D:P, bass.ds(g * GE + 1, GE)], h_new[:, s], ACT.Identity,
                                      bias=b_all[0:D, l:l + 1]).then_inc(wide_ready, 1)

                    pipelined(s_, ((1, finish),), down=True)

        def attention_step(l):
            with ExitStack() as st:
                alpha = mem(st, f"alpha_{l}", [P, TILES, H])
                softmax_weights(l, alpha)
                messages(l, alpha)
            if l < L - 1:
                spread(l)
            clear_signals()

        keep_q = mem(top, "keep_q", [Q, CE + 1])
        carry_in = mem(top, "carry_in", [1, 4, Q])
        with ExitStack() as st:
            keep_u = mem(st, "keep_u8", [Q, CE + 1], U8)
            tmp = [mem(st, f"tmp{n}", [P, TILES]) for n in range(4)]
            low = mem(st, "low", [Q, 2])
            keep_in = sem(st, "keep_in")
            own = sem(st, "own")
            low_t = sem(st, "low_t")
            block = st.enter_context(nc.Block())

            @block.sync
            def _(sp):
                for s in range(CH):
                    sp.dma_start(keep_u[s * H:(s + 1) * H], lanes(keep_row[s * CE:(s + 1) * CE + 1], H)).then_inc(keep_in, 16)

            @block.vector
            def _(v):
                count = [0]

                def link(ins):
                    count[0] += 1
                    ins.then_inc(own, 1)
                    v.wait_ge(own, count[0])

                known, above, row, delta = tmp
                link(v.tensor_scalar(known[:], equal_to[:], 0.0, None, ALU.is_gt))
                link(v.tensor_scalar(above[:], not_above[:], 1.0, float(P * TILES - 1), ALU.is_equal, ALU.mult))
                link(v.tensor_scalar(row[:], not_above[:], -2.0, float(TILES), ALU.add, ALU.mult))
                link(v.tensor_tensor(row[:], row[:], tiles_before[:], ALU.add))
                link(v.tensor_tensor(row[:], row[:], above[:], ALU.add))
                link(v.tensor_scalar(row[:], row[:], float(N), None, ALU.add))
                link(v.tensor_tensor(delta[:], row[:], src_f[:], ALU.subtract))
                link(v.tensor_tensor(delta[:], delta[:], known[:], ALU.mult))
                link(v.tensor_tensor(delta[:], delta[:], src_f[:], ALU.add))
                link(v.tensor_copy(row_of_source[:], delta[:]))
                v.wait_ge(keep_in, 16 * CH)
                link(v.tensor_copy(keep_q[:], keep_u[:]))
                link(v.tensor_reduce(low[:, 0:1], keep_q[:, 0:CE], AX_X, ALU.min))
                link(v.tensor_reduce(low[:, 1:2], keep_q[:, 1:CE + 1], AX_X, ALU.min))
                KEEP_LOW = count[0]
                v.wait_ge(low_t, 2)
                for n in range(2):
                    link(v.tensor_copy(carry_in[:, n], bank[n][0:1, 0:Q]))
                link(v.tensor_scalar(carry_in[:, 2:4], carry_in[:, 0:2], -1.0, BIG, ALU.add, ALU.mult))
                marks["keep_low"] = KEEP_LOW

            @block.tensor
            def _(t):
                t.wait_ge(own, marks["keep_low"])
                for n in range(2):
                    t.matmul(bank[n][0:1, 0:Q], low[:, n:n + 1], ident[0:Q, 0:Q], start=True, stop=True).then_inc(low_t, 1)

        clear_signals()
        for l in range(L):
            attention_step(l)

        bn_scale = mem(top, "bn_scale", [P, 2])
        with ExitStack() as st:
            l = L - 1
            keep = mem(st, "keep_last", [D, 2, GE], U8)
            ended = mem(st, "ended_last", [D, 2, GE])
            h_new = mem(st, "h_new_last", [D, 2, GE])
            h_full = mem(st, "h_full_last", [D, 2, GE])
            x_again = mem(st, "x_last", [P, 2, TPG, D])
            norm = mem(st, "norm_last", [P, 2, TPG, 2, D])
            square = mem(st, "square_last", [P, TPG * 2 * D])
            norm_t = mem(st, "norm_t_last", [P, GE])
            attr = mem(st, "attr", [P, 2, TPG, D])
            attr_t = mem(st, "attr_t", [D, GE])
            stat = mem(st, "stat_last", [P, 2, 4, 2 * TPG])
            logs = mem(st, "logs_last", [P, 2 * TPG])
            conv_stat = mem(st, "conv_stat", [P, G, 6])
            moments = mem(st, "moments", [P, 4])
            keep_in = [sem(st, f"keep_last_in{s}") for s in range(2)]
            x_in = [sem(st, f"x_last_in{s}") for s in range(2)]
            attr_in = [sem(st, f"attr_in{s}") for s in range(2)]
            h1_saved = [sem(st, f"h1_saved{s}") for s in range(2)]
            gathered = [pool_dma_sem(f"x1_gathered{s}") for s in range(2)]
            through, ended_ready, spread_out, full_ready, full_t, centered, squared, summed2, rstd_ready, \
                norm_ready, norm_in_psum, attr_in_psum, norm_t_ready, conv_ready, conv_kept, conv_counted, x_used = [
                    sem(st, f"{name}_last") for name in (
                        "through", "ended_ready", "spread_out", "full_ready", "full_t", "centered", "squared",
                        "summed2", "rstd_ready", "norm_ready", "norm_in_psum", "attr_in_psum", "norm_t_ready",
                        "conv_ready", "conv_kept", "conv_counted", "x_used")]
            own = sem(st, "own_last")
            act_own = sem(st, "act_own_last")
            zeroed = sem(st, "attr_zeroed")
            sp_paced = sem(st, "sp_paced_last")
            act_paced = sem(st, "act_paced_last")
            pe_paced = sem(st, "pe_paced_last")
            block = st.enter_context(nc.Block())
            LEAD = 8

            @block.gpsimd
            def _(pool):
                for k in range(G):
                    g, s = G - 1 - k, k % 2
                    if k >= 2:
                        pool.wait_ge(gathered[s], 16 * TPG * (k // 2))
                    for t in range(TPG):
                        tile = TPG * g + t
                        pool.indirect_dma_start(
                            out=edge[:, tile], out_offset=None, in_=tables[l],
                            in_offset=bass.IndirectOffsetOnAxis(ap=row_of_source[:, tile:tile + 1], axis=0),
                        ).then_inc(gathered[s], 16)

            @block.sync
            def _(sp):
                def load(k, g, s, turn):
                    sp.wait_ge(spread_out, at(k, back=2))
                    sp.sem_inc(sp_paced, 1)
                    sp.dma_start(keep[:, s], lanes(keep_row[bass.ds(g * GE + 1, GE)], D)).then_inc(keep_in[s], 16)

                def load_x(k, g, s, turn):
                    sp.wait_ge(x_used, at(k, back=2))
                    sp.sem_inc(sp_paced, 1)
                    sp.dma_start(x_again[:, s], x_dst.rearrange("p (t f) -> p t f", f=D)[:, bass.ds(g * TPG, TPG)]).then_inc(x_in[s], 16)

                def load_attr(k, g, s, turn):
                    if isinstance(k, int) and k == 0:
                        full = LAST_E // P
                        sp.wait_ge(zeroed, 1)
                        sp.dma_start(attr[:, s, 0:full], edge_attr[(G - 1) * GE:(G - 1) * GE + full * P].rearrange("(t p) f -> p t f", p=P)).then_inc(attr_in[s], 16)
                        sp.dma_start(attr[0:LAST_E - full * P, s, full], edge_attr[(G - 1) * GE + full * P:E]).then_inc(attr_in[s], 16)
                        return
                    sp.wait_ge(attr_in_psum, at(k, back=2))
                    sp.sem_inc(sp_paced, 1)
                    if s == 0 and isinstance(k, int) and k == 2:
                        sp.wait_ge(attr_in[0], 32)
                    sp.dma_start(attr[:, s], edge_attr[bass.ds(g * GE, GE)].rearrange("(t p) f -> p t f", p=P)).then_inc(attr_in[s], 16)

                def save_h1(k, g, s, turn):
                    sp.wait_ge(norm_ready, at(k))
                    sp.sem_inc(sp_paced, 1)
                    sp.dma_start(h1_dst.rearrange("p (t f) -> p t f", f=D)[:, bass.ds(g * TPG, TPG)], norm[:, s, :, 1]).then_inc(h1_saved[s], 16)

                for s in range(2):
                    sp.sem_inc(h1_saved[s], 32)
                pipelined(sp, ((0, load), (2, load_x), (4, load_attr), (5, save_h1)), down=True, lead=LEAD)
                sp.wait_ge(h1_saved[0], 16 * (G // 2 + 1) + 32)
                sp.wait_ge(h1_saved[1], 16 * (G // 2) + 32)

            @block.tensor
            def _(t_):
                for signal in (through, full_t, norm_in_psum, attr_in_psum, conv_ready):
                    t_.sem_inc(signal, AHEAD)

                def weights(k, g, s, turn):
                    t_.wait_ge(ended_ready, at(k, back=2))
                    t_.matmul(bank[s][0:D], w_row[:, l, 0:D], wide[:, bass.ds(g * GE + 1, GE)], start=True, stop=True).then_inc(through, 1)

                def to_edges(k, g, s, turn):
                    t_.wait_ge(full_ready, at(k))
                    t_.wait_ge(x_used, at(k, back=1))
                    t_.sem_inc(pe_paced, 1)
                    for t in range(TPG):
                        last = t_.transpose(bank[2][:, t * D:(t + 1) * D], h_full[:, s, t * P:(t + 1) * P], ident[0:D, 0:D])
                    last.then_inc(full_t, 1)

                def transposes(k, g, s, turn):
                    t_.wait_ge(norm_ready, at(k))
                    t_.wait_ge(norm_t_ready, at(k, back=1))
                    for t in range(TPG):
                        last = t_.transpose(bank[4][:, t * P:(t + 1) * P], norm[:, s, t].rearrange("p e f -> p (e f)"), ident[:])
                    last.then_inc(norm_in_psum, 1)
                    if isinstance(k, int):
                        t_.wait_ge(attr_in[s], 16 * (turn + (1 if s else 2)))
                    else:
                        t_.wait_ge(attr_in[s], turn * 16 + (16 if s else 32))
                        t_.sem_inc(pe_paced, 1)
                    for t in range(TPG):
                        last = t_.transpose(bank[3][0:D, t * P:(t + 1) * P], attr[:, s, t], ident[:])
                    last.then_inc(attr_in_psum, 1)

                def convolve(k, g, s, turn):
                    t_.wait_ge(norm_t_ready, at(k))
                    t_.wait_ge(conv_counted, at(k, back=2))
                    t_.matmul(bank[5 + s][:], w_conv[:], norm_t[:], start=True, stop=False)
                    t_.matmul(bank[5 + s][:], w_conv3[:], attr_t[:], start=False, stop=True).then_inc(conv_ready, 1)

                pipelined(t_, ((0, weights), (5, transposes), (6, convolve), (2, to_edges)), down=True, lead=LEAD)

            @block.vector
            def _(v):
                for signal in (ended_ready, spread_out, x_used, centered, summed2, norm_ready, conv_counted):
                    v.sem_inc(signal, AHEAD)
                v.memset(h_new[:, 1, 0:1], 0.0).then_inc(sp_paced, 1)
                v.memset(attr[:], 0.0).then_inc(zeroed, 1)
                OWN = 5

                def end(k, g, s, turn):
                    v.wait_ge(keep_in[s], turn * 16 + 16)
                    v.wait_ge(through, at(k))
                    v.scalar_tensor_tensor(out=ended[:, s], in0=keep[:, s], scalar=0.0, in1=bank[s][0:D],
                                           op0=ALU.is_equal, op1=ALU.mult).then_inc(ended_ready, 1)

                def back(k, g, s, turn):
                    v.wait_ge(ended_ready, at(k))
                    v.wait_ge(spread_out, at(k, back=1))
                    v.wait_ge(full_ready, at(k, back=2))
                    v.tensor_tensor_scan(out=h_new[:, s, ::-1], data0=keep[:, s, ::-1], data1=ended[:, s, ::-1],
                                         initial=h_new[:, 1 - s, 0:1], op0=ALU.mult, op1=ALU.add).then_inc(spread_out, 1)

                def center(k, g, s, turn):
                    count = [0]

                    def link(ins):
                        count[0] += 1
                        ins.then_inc(own, 1)
                        v.wait_ge(own, k * OWN + count[0])

                    tiles = bass.ds(g * TPG, TPG)
                    here = edge[:, tiles, 0:D]
                    now = stat[:, s].rearrange("p n (t e) -> p n t e", e=2)
                    v.wait_ge(gathered[s], turn * (16 * TPG) + 16 * TPG)
                    v.wait_ge(norm_in_psum, at(k, back=2))
                    v.wait_ge(h1_saved[s], turn * 16 + 32)
                    v.sem_inc(sp_paced, 1)
                    link(v.tensor_reduce(now[:, 0, :, 0], here, AX_X, ALU.add))
                    link(v.tensor_scalar(now[:, 1, :, 0], now[:, 0, :, 0], 1.0 / D, None, ALU.mult))
                    link(v.tensor_tensor(norm[:, s, :, 0], here, inner(now[:, 1, :, 0], [P, TPG, D]), ALU.subtract))
                    v.wait_ge(x_in[s], turn * 16 + 16)
                    v.wait_ge(full_t, at(k))
                    v.tensor_tensor(here, bank[2][:, 0:TPG * D].rearrange("p (t f) -> p t f", f=D), x_again[:, s], ALU.add).then_inc(x_used, 1)
                    v.wait_ge(x_used, at(k))
                    v.sem_inc(sp_paced, 1)
                    link(v.tensor_reduce(now[:, 0, :, 1], here, AX_X, ALU.add))
                    link(v.tensor_scalar(now[:, 1, :, 1], now[:, 0, :, 1], 1.0 / D, None, ALU.mult))
                    assert count[0] == OWN
                    v.tensor_tensor(norm[:, s, :, 1], here, inner(now[:, 1, :, 1], [P, TPG, D]), ALU.subtract).then_inc(centered, 1)

                def variance(k, g, s, turn):
                    v.wait_ge(squared, at(k))
                    v.tensor_reduce(stat[:, s, 2], square[:].rearrange("p (t f) -> p t f", f=D), AX_X, ALU.add).then_inc(summed2, 1)

                def normalize(k, g, s, turn):
                    v.wait_ge(rstd_ready, at(k))
                    part = norm[:, s].rearrange("p t e f -> p (t e) f")
                    v.scalar_tensor_tensor(out=part, in0=part, scalar=0.0, in1=inner(stat[:, s, 3], [P, 2 * TPG, D]),
                                           op0=ALU.max, op1=ALU.mult).then_inc(norm_ready, 1)

                def count_in(k, g, s, turn):
                    used = LAST_E if isinstance(k, int) and k == 0 else GE
                    v.wait_ge(conv_kept, at(k))
                    v.sem_inc(sp_paced, 1)
                    v.bn_stats(conv_stat[:, bass.ds(g, 1)].rearrange("p a n -> p (a n)"), bank[5 + s][:, 0:used]).then_inc(conv_counted, 1)

                pipelined(v, ((5, normalize), (1, end), (1, back), (4, variance), (3, center), (7, count_in)), down=True, lead=LEAD)
                count = [G * OWN]

                def link(ins):
                    count[0] += 1
                    ins.then_inc(own, 1)
                    v.wait_ge(own, count[0])

                v.wait_ge(conv_counted, at(G - 1))
                link(v.bn_aggr(moments[:, 0:2], conv_stat[:]))
                v.sem_inc(summed2, 1)
                v.wait_ge(rstd_ready, at(G))
                link(v.tensor_tensor(bn_scale[:, 0:1], moments[:, 3:4], bn_cols[:, 1:2], ALU.mult))
                link(v.tensor_tensor(bn_scale[:, 1:2], moments[:, 0:1], bn_cols[:, 0:1], ALU.add))
                link(v.tensor_tensor(bn_scale[:, 1:2], bn_scale[:, 1:2], bn_scale[:, 0:1], ALU.mult))
                link(v.tensor_tensor(bn_scale[:, 1:2], bn_cols[:, 2:3], bn_scale[:, 1:2], ALU.subtract))
                link(v.tensor_scalar(bn_scale[0:D], bn_scale[0:D], -1.0, None, ALU.mult))

            @block.scalar
            def _(s_):
                s_.preload_act_table_set(ACT_TABLES)
                for signal in (full_ready, squared, rstd_ready, norm_t_ready, conv_kept):
                    s_.sem_inc(signal, AHEAD)

                def finish(k, g, s, turn):
                    s_.wait_ge(spread_out, at(k))
                    s_.wait_ge(full_t, at(k, back=2))
                    s_.activation(h_full[:, s], h_new[:, s], ACT.Identity, bias=b_all[0:D, l:l + 1]).then_inc(full_ready, 1)

                def squares(k, g, s, turn):
                    s_.wait_ge(centered, at(k))
                    s_.wait_ge(summed2, at(k, back=1))
                    s_.activation(square[:], norm[:, s].rearrange("p t e f -> p (t e f)"), ACT.Square).then_inc(squared, 1)

                def rstd(k, g, s, turn):
                    s_.wait_ge(summed2, at(k))
                    s_.activation(logs[:], stat[:, s, 2], ACT.Ln, bias=eps[:], scale=1.0 / D).then_inc(act_own, 1)
                    s_.wait_ge(act_own, k + 1)
                    s_.activation(stat[:, s, 3], logs[:], ACT.Exp, scale=-0.5).then_inc(rstd_ready, 1)

                def take(k, g, s, turn):
                    s_.wait_ge(norm_in_psum, at(k))
                    s_.wait_ge(conv_ready, at(k, back=1))
                    s_.activation(norm_t[:], bank[4][:], ACT.Copy)
                    s_.wait_ge(attr_in_psum, at(k))
                    s_.activation(attr_t[:], bank[3][0:D], ACT.Copy).then_inc(norm_t_ready, 1)

                def keep_conv(k, g, s, turn):
                    s_.wait_ge(conv_ready, at(k))
                    s_.sem_inc(act_paced, 1)
                    s_.activation(wide[:, bass.ds(g * GE + 1, GE)], bank[5 + s][:], ACT.Identity, bias=bn_cols[:, 0:1]).then_inc(conv_kept, 1)

                pipelined(s_, ((1, finish), (4, rstd), (3, squares), (5, take), (6, keep_conv)), down=True, lead=LEAD)
                s_.wait_ge(summed2, at(G))
                s_.activation(moments[:, 2:3], moments[:, 1:2], ACT.Ln, bias=eps[:]).then_inc(act_own, 1)
                s_.wait_ge(act_own, G + 1)
                s_.activation(moments[:, 3:4], moments[:, 2:3], ACT.Exp, scale=-0.5).then_inc(rstd_ready, 1)
        clear_signals()

        upd_scale = mem(top, "upd_scale", [D, 2])
        shift_row = mem(top, "shift_row", [P, D])
        with ExitStack() as st:
            keep = mem(st, "keep_conv", [D, 2, GE], U8)
            keep_next = mem(st, "keep_conv_next", [D, 2, GE], U8)
            arg = mem(st, "arg", [P, 2, GE])
            soft = mem(st, "soft", [P, 2, GE])
            gate = mem(st, "gate", [P, 2, GE])
            last_sum = mem(st, "last_sum", [D, GE])
            upd_stat = mem(st, "upd_stat", [D, G, 6])
            m2 = mem(st, "m2", [D, 6])
            shift_rep = mem(st, "shift_rep", [D, P])
            keep_in = [sem(st, f"keep_conv_in{s}") for s in range(2)]
            arg_ready, bounded, exped, logged, soft_ready, gate_ready, message_ready, summed, counted = [
                sem(st, f"{name}_conv") for name in ("arg_ready", "bounded", "exped", "logged", "soft_ready", "gate_ready",
                                                     "message_ready", "summed", "counted")]
            own = sem(st, "own_conv")
            rstd_ready = sem(st, "rstd_conv")
            moments_ready = sem(st, "moments_conv")
            rep_ready = sem(st, "rep_conv")
            row_ready = sem(st, "row_conv")
            sp_paced = sem(st, "sp_paced_conv")
            act_paced = sem(st, "act_paced_conv")
            block = st.enter_context(nc.Block())

            @block.sync
            def _(sp):
                def load(k, g, s, turn):
                    sp.wait_ge(counted, at(k, back=2))
                    sp.sem_inc(sp_paced, 1)
                    sp.dma_start(keep[:, s], lanes(keep_row[bass.ds(g * GE, GE)], D)).then_inc(keep_in[s], 16)
                    sp.dma_start(keep_next[:, s], lanes(keep_row[bass.ds(g * GE + 1, GE)], D)).then_inc(keep_in[s], 16)

                pipelined(sp, ((0, load),))

            @block.scalar
            def _(s_):
                s_.preload_act_table_set(ACT_TABLES)
                for signal in (arg_ready, exped, logged, gate_ready):
                    s_.sem_inc(signal, AHEAD)

                def norm1(k, g, s, turn):
                    s_.wait_ge(soft_ready, at(k, back=2))
                    s_.sem_inc(act_paced, 1)
                    s_.activation(arg[:, s], wide[:, bass.ds(g * GE + 1, GE)], ACT.Identity, bias=bn_scale[:, 1:2],
                                  scale=bn_scale[:, 0:1]).then_inc(arg_ready, 1)

                def softplus(k, g, s, turn):
                    s_.wait_ge(bounded, at(k))
                    s_.activation(soft[:, s], soft[:, s], ACT.Exp).then_inc(exped, 1)
                    s_.wait_ge(exped, at(k))
                    s_.activation(soft[:, s], soft[:, s], ACT.Ln, bias=1.0).then_inc(logged, 1)

                def sigmoid(k, g, s, turn):
                    s_.wait_ge(soft_ready, at(k))
                    s_.wait_ge(summed, at(k, back=2))
                    s_.activation(gate[D:P, s], soft[0:D, s], ACT.Exp, scale=-1.0).then_inc(gate_ready, 1)

                pipelined(s_, ((0, norm1), (1, softplus), (2, sigmoid)))
                s_.wait_ge(moments_ready, 1)
                s_.activation(m2[:, 4:5], m2[:, 3:4], ACT.Ln, bias=eps[0:D]).then_inc(act_paced, 1)
                s_.wait_ge(act_paced, G + 1)
                s_.activation(m2[:, 5:6], m2[:, 4:5], ACT.Exp, scale=-0.5).then_inc(rstd_ready, 1)

            @block.vector
            def _(v):
                for signal in (bounded, soft_ready, message_ready, summed, counted):
                    v.sem_inc(signal, AHEAD)

                def bound(k, g, s, turn):
                    v.wait_ge(arg_ready, at(k))
                    v.wait_ge(message_ready, at(k, back=2))
                    v.tensor_scalar(soft[:, s], arg[:, s], EXP_MAX, None, ALU.min).then_inc(bounded, 1)

                def larger(k, g, s, turn):
                    v.wait_ge(logged, at(k))
                    v.tensor_tensor(soft[:, s], soft[:, s], arg[:, s], ALU.max).then_inc(soft_ready, 1)

                def message(k, g, s, turn):
                    v.wait_ge(gate_ready, at(k))
                    v.tensor_tensor(gate[0:D, s], gate[D:P, s], soft[D:P, s], ALU.mult).then_inc(message_ready, 1)

                def scan(k, g, s, turn):
                    v.wait_ge(message_ready, at(k))
                    v.wait_ge(keep_in[s], turn * 32 + 32)
                    v.wait_ge(summed, at(k, back=1))
                    v.tensor_tensor_scan(out=wide[0:D, bass.ds(g * GE + 1, GE)], data0=keep[:, s], data1=gate[0:D, s],
                                         initial=wide[0:D, bass.ds(g * GE, 1)], op0=ALU.mult, op1=ALU.add).then_inc(summed, 1)

                def count_in(k, g, s, turn):
                    used = LAST_E if isinstance(k, int) and k == G - 1 else GE
                    v.wait_ge(summed, at(k))
                    v.wait_ge(counted, at(k, back=1))
                    v.scalar_tensor_tensor(out=last_sum[:], in0=keep_next[:, s], scalar=0.0, in1=wide[0:D, bass.ds(g * GE + 1, GE)],
                                           op0=ALU.is_equal, op1=ALU.mult).then_inc(own, 1)
                    v.wait_ge(own, k + 1)
                    v.sem_inc(sp_paced, 1)
                    v.bn_stats(upd_stat[:, bass.ds(g, 1)].rearrange("p a n -> p (a n)"), last_sum[:, 0:used]).then_inc(counted, 1)

                pipelined(v, ((2, larger), (3, message), (1, bound), (3, scan), (3, count_in)))
                count = [G]

                def link(ins):
                    count[0] += 1
                    ins.then_inc(own, 1)
                    v.wait_ge(own, count[0])

                v.wait_ge(counted, at(G - 1))
                link(v.bn_aggr(m2[:, 0:2], upd_stat[:]))
                link(v.tensor_tensor(m2[:, 2:3], m2[:, 0:1], m2[:, 0:1], ALU.mult))
                link(v.tensor_tensor(m2[:, 1:2], m2[:, 1:2], m2[:, 2:3], ALU.add))
                link(v.tensor_scalar(m2[:, 0:2], m2[:, 0:2], E / N, None, ALU.mult))
                link(v.tensor_tensor(m2[:, 2:3], m2[:, 0:1], m2[:, 0:1], ALU.mult))
                v.tensor_tensor(m2[:, 3:4], m2[:, 1:2], m2[:, 2:3], ALU.subtract).then_inc(moments_ready, 1)
                v.wait_ge(rstd_ready, 1)
                link(v.tensor_tensor(upd_scale[:, 0:1], m2[:, 5:6], bn_cols[0:D, 3:4], ALU.mult))
                link(v.tensor_tensor(upd_scale[:, 1:2], m2[:, 0:1], upd_scale[:, 0:1], ALU.mult))
                link(v.tensor_tensor(upd_scale[:, 1:2], bn_cols[0:D, 4:5], upd_scale[:, 1:2], ALU.subtract))
                v.tensor_scalar(shift_rep[:], ones[0:D], upd_scale[:, 1:2], None, ALU.mult).then_inc(rep_ready, 1)
                v.wait_ge(row_ready, 1)
                link(v.tensor_copy(shift_row[:], bank[0][:, 0:D]))

            @block.tensor
            def _(t_):
                t_.wait_ge(rep_ready, 1)
                t_.matmul(bank[0][:, 0:D], shift_rep[:], ident[0:D, 0:D], start=True, stop=True).then_inc(row_ready, 1)
        clear_signals()

        with ExitStack() as st:
            SLOTS = 4
            uses = [(G - s + SLOTS - 1) // SLOTS for s in range(SLOTS)]
            nodes = mem(st, "nodes_out", [P, SLOTS, NODE_T, ROW])
            n_norm = mem(st, "n_norm_out", [P, SLOTS, NODE_T, D])
            n_square = mem(st, "n_square_out", [P, NODE_T, D])
            n_soft = mem(st, "n_soft", [P, SLOTS, NODE_T, D])
            n_stat = mem(st, "n_stat_out", [P, SLOTS, 4, NODE_T])
            n_logs = mem(st, "n_logs_out", [P, NODE_T])
            update = mem(st, "update", [D, GE])
            e_arg = mem(st, "e_arg", [P, 2, TPG, D])
            e_soft = mem(st, "e_soft", [P, TPG, D])
            nodes_in = [sem(st, f"nodes_out_in{s}") for s in range(SLOTS)]
            h1_in = [sem(st, f"h1_in{s}") for s in range(SLOTS)]
            stored = [sem(st, f"out_stored{s}") for s in range(SLOTS)]
            scattered = [pool_dma_sem(f"scattered{s}") for s in range(2)]
            n_centered, n_squared, n_summed2, n_rstd, n_bounded, n_exped, n_logged, n_arg, n_ready, \
                update_ready, update_t, e_bounded, e_exped, e_logged, e_ready, n_mean, n_larger, e_larger, n_log = [
                    sem(st, f"{name}_out") for name in (
                        "n_centered", "n_squared", "n_summed2", "n_rstd", "n_bounded", "n_exped", "n_logged", "n_arg", "n_ready",
                        "update_ready", "update_t", "e_bounded", "e_exped", "e_logged", "e_ready", "n_mean", "n_larger",
                        "e_larger", "n_log")]
            n_sum = sem(st, "n_sum_out")
            nodes_cleared = sem(st, "nodes_cleared")
            n_normed = sem(st, "n_normed_out")
            e_arg_ready = sem(st, "e_arg_ready_out")
            sp_paced = sem(st, "sp_paced_out")
            act_paced = sem(st, "act_paced_out")
            pe_paced = sem(st, "pe_paced_out")
            block = st.enter_context(nc.Block())

            @block.sync
            def _(sp):
                def load(k, g, s, turn):
                    used = LAST_P if isinstance(k, int) and k == G - 1 else P
                    sp.wait_ge(stored[s], turn * 16 + 16)
                    sp.sem_inc(sp_paced, 1)
                    sp.dma_start(nodes[0:used, s], tables[L - 1][bass.ds(k * GN, used * NODE_T)].rearrange("(p j) w -> p j w", j=NODE_T)).then_inc(nodes_in[s], 16)
                    sp.wait_ge(e_ready, at(k, back=2))
                    sp.sem_inc(sp_paced, 1)
                    sp.dma_start(e_arg[:, s % 2], h1_dst.rearrange("p (t f) -> p t f", f=D)[:, bass.ds(k * TPG, TPG)]).then_inc(h1_in[s], 16)

                def save(k, g, s, turn):
                    used = LAST_P if isinstance(k, int) and k == G - 1 else P
                    sp.wait_ge(n_ready, at(k))
                    sp.sem_inc(sp_paced, 1)
                    sp.dma_start(out[bass.ds(k * GN, used * NODE_T)].rearrange("(p j) f -> p j f", j=NODE_T), n_soft[0:used, s]).then_inc(stored[s], 16)

                for s in range(SLOTS):
                    sp.sem_inc(stored[s], 16)
                sp.wait_ge(nodes_cleared, 1)
                pipelined(sp, ((4, save), (0, load)), slots=SLOTS)

            @block.gpsimd
            def _(pool):
                for s in range(SLOTS):
                    pool.wait_ge(stored[s], 16 * uses[s] + 16)
                for k in range(G):
                    s = k % 2
                    pool.wait_ge(e_ready, at(k))
                    if k >= 2:
                        pool.wait_ge(scattered[s], 16 * TPG * (k // 2))
                    for t in range(TPG):
                        tile = TPG * k + t
                        pool.indirect_dma_start(
                            out=out, out_offset=bass.IndirectOffsetOnAxis(ap=scatter_row[:, tile:tile + 1], axis=0),
                            in_=edge[:, tile, 0:D], in_offset=None, bounds_check=N - 1, oob_is_err=False,
                        ).then_inc(scattered[s], 16)
                pool.wait_ge(scattered[0], 16 * TPG * (G // 2 + 1))
                pool.wait_ge(scattered[1], 16 * TPG * (G // 2))

            @block.vector
            def _(v):
                for signal in (n_sum, n_mean, n_centered, n_summed2, n_normed, n_arg, n_bounded, n_larger, n_ready,
                               e_arg_ready, e_bounded, e_larger, e_ready):
                    v.sem_inc(signal, AHEAD)
                v.memset(nodes[:], 0.0).then_inc(nodes_cleared, 1)

                def center(k, g, s, turn):
                    here = nodes[:, s, :, 0:D]
                    v.wait_ge(nodes_in[s], turn * 16 + 16)
                    v.tensor_reduce(n_stat[:, s, 0], here, AX_X, ALU.add).then_inc(n_sum, 1)
                    v.wait_ge(n_sum, at(k))
                    v.tensor_scalar(n_stat[:, s, 1], n_stat[:, s, 0], 1.0 / D, None, ALU.mult).then_inc(n_mean, 1)
                    v.wait_ge(n_mean, at(k))
                    v.tensor_tensor(n_norm[:, s], here, inner(n_stat[:, s, 1], [P, NODE_T, D]), ALU.subtract).then_inc(n_centered, 1)

                def variance(k, g, s, turn):
                    v.wait_ge(n_squared, at(k))
                    v.tensor_reduce(n_stat[:, s, 2], n_square[:], AX_X, ALU.add).then_inc(n_summed2, 1)

                def normalize(k, g, s, turn):
                    v.wait_ge(n_rstd, at(k))
                    v.scalar_tensor_tensor(out=n_norm[:, s], in0=n_norm[:, s], scalar=0.0, in1=inner(n_stat[:, s, 3], [P, NODE_T, D]),
                                           op0=ALU.max, op1=ALU.mult).then_inc(n_normed, 1)
                    v.wait_ge(n_normed, at(k))
                    v.tensor_tensor(n_norm[:, s], n_norm[:, s], shift_row[:].unsqueeze(1).broadcast_to([P, NODE_T, D]), ALU.add).then_inc(n_arg, 1)
                    v.wait_ge(n_arg, at(k))
                    v.wait_ge(stored[s], turn * 16 + 16)
                    v.tensor_scalar(n_soft[:, s], n_norm[:, s], EXP_MAX, None, ALU.min).then_inc(n_bounded, 1)

                def finish(k, g, s, turn):
                    v.wait_ge(n_logged, at(k))
                    v.tensor_tensor(n_soft[:, s], n_soft[:, s], n_norm[:, s], ALU.max).then_inc(n_larger, 1)
                    v.wait_ge(n_larger, at(k))
                    v.tensor_tensor(n_soft[:, s], n_soft[:, s], nodes[:, s, :, 0:D], ALU.add).then_inc(n_ready, 1)

                def e_bound(k, g, s, turn):
                    v.wait_ge(update_t, at(k))
                    v.wait_ge(h1_in[s], turn * 16 + 16)
                    v.tensor_tensor(e_arg[:, s % 2], e_arg[:, s % 2], bank[s % 2][:, 0:TPG * D].rearrange("p (t f) -> p t f", f=D), ALU.add).then_inc(e_arg_ready, 1)
                    v.wait_ge(e_arg_ready, at(k))
                    v.wait_ge(e_ready, at(k, back=1))
                    v.tensor_scalar(e_soft[:], e_arg[:, s % 2], EXP_MAX, None, ALU.min).then_inc(e_bounded, 1)

                def e_finish(k, g, s, turn):
                    tiles = bass.ds(k * TPG, TPG)
                    v.wait_ge(e_logged, at(k))
                    v.tensor_tensor(e_soft[:], e_soft[:], e_arg[:, s % 2], ALU.max).then_inc(e_larger, 1)
                    v.wait_ge(e_larger, at(k))
                    v.tensor_tensor(edge[:, tiles, 0:D], edge[:, tiles, 0:D], e_soft[:], ALU.add).then_inc(e_ready, 1)

                pipelined(v, ((4, finish), (3, normalize), (2, e_finish), (1, center), (1, e_bound), (2, variance)), slots=SLOTS)

            @block.scalar
            def _(s_):
                s_.preload_act_table_set(ACT_TABLES)
                for signal in (update_ready, n_squared, n_log, n_rstd, n_exped, n_logged, e_exped, e_logged):
                    s_.sem_inc(signal, AHEAD)

                def updates(k, g, s, turn):
                    s_.wait_ge(update_t, at(k, back=1))
                    s_.sem_inc(act_paced, 1)
                    s_.activation(update[:], wide[0:D, bass.ds(k * GE + 1, GE)], ACT.Identity, bias=upd_scale[:, 1:2],
                                  scale=upd_scale[:, 0:1]).then_inc(update_ready, 1)

                def squares(k, g, s, turn):
                    s_.wait_ge(n_centered, at(k))
                    s_.wait_ge(n_summed2, at(k, back=1))
                    s_.activation(n_square[:].rearrange("p t f -> p (t f)"), n_norm[:, s].rearrange("p t f -> p (t f)"), ACT.Square).then_inc(n_squared, 1)

                def rstd(k, g, s, turn):
                    s_.wait_ge(n_summed2, at(k))
                    s_.activation(n_logs[:], n_stat[:, s, 2], ACT.Ln, bias=eps[:], scale=1.0 / D).then_inc(n_log, 1)
                    s_.wait_ge(n_log, at(k))
                    s_.activation(n_stat[:, s, 3], n_logs[:], ACT.Exp, scale=-0.5).then_inc(n_rstd, 1)

                def softplus(k, g, s, turn):
                    flat = n_soft[:, s].rearrange("p t f -> p (t f)")
                    s_.wait_ge(n_bounded, at(k))
                    s_.activation(flat, flat, ACT.Exp).then_inc(n_exped, 1)
                    s_.wait_ge(n_exped, at(k))
                    s_.activation(flat, flat, ACT.Ln, bias=1.0).then_inc(n_logged, 1)

                def e_softplus(k, g, s, turn):
                    flat = e_soft[:].rearrange("p t f -> p (t f)")
                    s_.wait_ge(e_bounded, at(k))
                    s_.activation(flat, flat, ACT.Exp).then_inc(e_exped, 1)
                    s_.wait_ge(e_exped, at(k))
                    s_.activation(flat, flat, ACT.Ln, bias=1.0).then_inc(e_logged, 1)

                pipelined(s_, ((0, updates), (3, softplus), (1, squares), (1, e_softplus), (2, rstd)), slots=SLOTS)

            @block.tensor
            def _(t_):
                t_.sem_inc(update_t, AHEAD)

                def to_edges(k, g, s, turn):
                    t_.wait_ge(update_ready, at(k))
                    t_.wait_ge(e_arg_ready, at(k, back=2))
                    t_.sem_inc(pe_paced, 1)
                    for t in range(TPG):
                        last = t_.transpose(bank[s % 2][:, t * D:(t + 1) * D], update[:, t * P:(t + 1) * P], ident[0:D, 0:D])
                    last.then_inc(update_t, 1)

                pipelined(t_, ((0, to_edges),), slots=SLOTS)


_INS = ("x", "src", "dst", "edge_attr_64", "L0_gnn_Ws", "L0_gnn_attn_l", "L0_gnn_attn_r", "L0_gnn_gat_bias",
        "L0_gnn_h_bias", "L1_gnn_W_full", "L1_gnn_b_full", "L1_gnn_bn1_g", "L1_gnn_bn1_b", "L1_gnn_bn2_g",
        "L1_gnn_bn2_b")


def kernel(**inputs):
    import numpy as np
    import concourse.bacc as bacc
    from concourse.bass_utils import run_bass_kernel_spmd

    nc = bacc.Bacc("TRN2", target_bir_lowering=False, num_devices=1)
    arrays, args = {}, []
    for name in _INS:
        a = np.ascontiguousarray(inputs[name])
        arrays[f"in_{name}_dram"] = a
        args.append(nc.dram_tensor(f"in_{name}_dram", a.shape, mybir.dt.from_np(a.dtype), kind="ExternalInput").ap())
    args.append(nc.dram_tensor("out_0_dram", inputs["x"].shape, F32, kind="ExternalOutput").ap())
    build(nc, *args)
    results = run_bass_kernel_spmd(nc, [arrays], core_ids=[0])
    return results.results[0]["out_0_dram"]
```

```python
from contextlib import ExitStack

import concourse.bass as bass
from concourse import mybir

ALU = mybir.AluOpType
ACT = mybir.ActivationFunctionType
F32 = mybir.dt.float32
I32 = mybir.dt.int32
U8 = mybir.dt.uint8
BF16 = mybir.dt.bfloat16
AX_X = mybir.AxisListType.X

P = 128
D = 64
H = 4
L = 4
ROW = D + H
EDGE_W = D + 2 * H
HALF = 98
TILES = 2 * HALF
TPG = 4
GE = TPG * P
G = TILES // TPG
EP = TILES * P
CT = 7
CH = TILES // CT
CE = CT * P
Q = CH * H
NODE_T = 8
GN = NODE_T * P
EPS = 1e-5
SLOPE = 0.2
BIG = 1e30
FAR = 1 << 20
AHEAD = 4
ACT_TABLES = "natural_log_exp_and_others"


def at(k, back=0):
    return k + (AHEAD + 1 - back)


def pipelined(eng, stages, down=False, lead=4, slots=2):
    def peeled(i):
        for lag, fn in stages:
            k = i - lag
            if 0 <= k < G:
                fn(k, G - 1 - k if down else k, k % slots, k // slots)

    turns = (G - lead) // slots
    for i in range(lead):
        peeled(i)
    with eng.Fori(0, turns) as r:
        for c in range(slots):
            for lag, fn in stages:
                first = lead + c - lag
                g = r * -slots + (G - 1 - first) if down else r * slots + first
                fn(r * slots + first, g, first % slots, r + first // slots)
    for i in range(lead + slots * turns, G + lead):
        peeled(i)


def one_row(a):
    return a.rearrange("(a n) -> a n", a=1)


def one_col(a):
    return a.rearrange("(n a) -> n a", a=1)


def lanes(a, n):
    return one_row(a).broadcast_to([n, a.shape[0]])


def inner(a, shape):
    return a.unsqueeze(len(a.shape)).broadcast_to(shape)


def build(nc, x, src, dst, edge_attr, Ws, attn_l, attn_r, gat_bias, h_bias, W_full, b_full,
          bn1_g, bn1_b, bn2_g, bn2_b, out):
    N = x.shape[0]
    E = src.shape[0]
    LAST_P = (N - (G - 1) * GN) // NODE_T
    LAST_E = E - (G - 1) * GE
    assert (G - 1) * GN + LAST_P * NODE_T == N and 0 < LAST_P <= P
    assert TILES == CH * CT and E < EP and 0 < LAST_E
    PAD_DST = N + 1

    dram = lambda name, shape, dt=F32: nc.dram_tensor(name, shape, dt).ap()
    src_pad = dram("src_pad", [EP], I32)
    dst_pad = dram("dst_pad", [1 + EP + P], I32)
    keep_row = dram("keep_row", [EP + 1], U8)
    tables = [dram(f"table{l}", [2 * EP, ROW]) for l in range(L - 1)] + [dram(f"table{L - 1}", [N + EP, D])]
    x_dst = dram("x_dst", [P, TILES * D])
    h1_dst = dram("h1_dst", [P, TILES * D])

    top = ExitStack()

    def mem(stack, name, shape, dt=F32):
        return stack.enter_context(nc.sbuf_tensor(name, shape, dt))

    signals = []

    def sem(stack, name):
        signals.append(nc.alloc_semaphore(name=name))
        return signals[-1]

    def pool_dma_sem(name):
        return nc.alloc_semaphore(name=name)

    def clear_signals():
        with nc.Block() as block:
            @block.sync
            def _(sp):
                for signal in signals:
                    sp.sem_clear(signal)
        for signal in signals:
            nc.release_semaphore(signal)
        signals.clear()

    marks = {}
    with top:
        wide = mem(top, "wide", [P, EP + 1])
        edge = mem(top, "edge", [P, TILES, ROW])
        self_logit = mem(top, "self_logit", [P, TILES, H])
        row_of_source = mem(top, "row_of_source", [P, TILES], I32)
        row_of_x1 = mem(top, "row_of_x1", [P, TILES], I32)
        src_row = mem(top, "src_row", [P, TILES], I32)
        dst_row = mem(top, "dst_row", [P, TILES], I32)
        scatter_row = mem(top, "scatter_row", [P, TILES], I32)
        src_f = mem(top, "src_f", [P, TILES])
        tiles_before = mem(top, "tiles_before", [P, TILES])
        not_above = mem(top, "not_above", [P, TILES])
        equal_to = mem(top, "equal_to", [P, TILES])
        ident = mem(top, "ident", [P, P])
        ones = mem(top, "ones", [P, P])
        eps = mem(top, "eps", [P, 1])
        w_heads = mem(top, "w_heads", [P, L, 2, D])
        w_row = mem(top, "w_row", [P, L, ROW])
        w_edge = mem(top, "w_edge", [D, L, EDGE_W])
        w_edge0 = mem(top, "w_edge0", [P, 2 * H])
        w_chain = mem(top, "w_chain", [D, L - 1, ROW])
        w_node = mem(top, "w_node", [D + 1, D])
        const_h = mem(top, "const_h", [D, L + 1])
        const_row = mem(top, "const_row", [P, D])
        const_logit = mem(top, "const_logit", [P, L, H])
        w_conv = mem(top, "w_conv", [P, 2 * D])
        w_conv3 = mem(top, "w_conv3", [D, 2 * D])
        bn_cols = mem(top, "bn_cols", [P, 5])
        limit = mem(top, "limit", [HALF, 2])
        steps = mem(top, "steps", [HALF + 1, 2, 2, P + 2], BF16)
        banks = top.enter_context(nc.psum_tensor("banks", [P, 8, 512], F32))
        bank = [banks[:, n] for n in range(8)]

        with ExitStack() as st:
            pad_i = mem(st, "pad_i", [1, 512], I32)
            last_keep = mem(st, "last_keep", [1, 4], U8)
            w_raw = mem(st, "w_raw", [P, L, H, D])
            a_raw = mem(st, "a_raw", [P, 2, L, H * D])
            prod = mem(st, "prod", [P, L, H * D])
            bias_raw = mem(st, "bias_raw", [P, L, H])
            hb = mem(st, "hb", [P, 1])
            w_sum = mem(st, "w_sum", [P, L, D])
            a_sum = mem(st, "a_sum", [P, 2, L, H])
            b_all = mem(st, "b_all", [P, L])
            steps_f = mem(st, "steps_f", [HALF + 1, 2, P + 2])
            steps_i = mem(st, "steps_i", [HALF + 1, 2, P + 2], I32)
            steps_low = mem(st, "steps_low", [HALF + 1, 2, P + 2])
            chain_t = mem(st, "chain_t", [D, L + 1, D])
            wsum_t = mem(st, "wsum_t", [D, L, D])
            c_rep = mem(st, "c_rep", [D, P])
            rows_i = mem(st, "rows_i", [HALF + 1, 4, 2, P], I32)
            rows_f = mem(st, "rows_f", [HALF + 1, 4, 2, P])
            ahead_i = mem(st, "ahead_i", [HALF + 1, 2, P], I32)
            ahead_f = mem(st, "ahead_f", [HALF + 1, 2, P])
            keep_u = mem(st, "keep_u", [HALF, 2, P], U8)
            dst_f = mem(st, "dst_f", [P, TILES])
            last_f = mem(st, "last_f", [P, TILES])
            tmp_f = mem(st, "tmp_f", [P, TILES])
            consts_set = sem(st, "consts_set")
            ident_ready = sem(st, "ident_ready")
            lists_padded = sem(st, "lists_padded")
            rows_loaded = sem(st, "rows_loaded")
            weights_loaded = sem(st, "weights_loaded")
            keep_stored = sem(st, "keep_stored")
            dve_step = sem(st, "dve_step")
            pe_step = sem(st, "pe_step")
            block = st.enter_context(nc.Block())
            WEIGHT_LOADS = 2 * (L + H + 1) + 2 + 2 + 3 + 2
            ROWS_CONVERTED, KEEP_READY, WEIGHTS_SUMMED = 1, 2, 46

            @block.gpsimd
            def _(pool):
                pool.memset(pad_i[:, 0:128], 0).then_inc(consts_set, 1)
                pool.memset(pad_i[:, 128:256], PAD_DST).then_inc(consts_set, 1)
                pool.memset(pad_i[:, 256:384], PAD_DST + 1).then_inc(consts_set, 1)
                pool.memset(pad_i[:, 384:448], -1).then_inc(consts_set, 1)
                pool.memset(pad_i[:, 448:512], 1).then_inc(consts_set, 1)
                pool.memset(last_keep[:], 0).then_inc(consts_set, 1)
                pool.memset(rows_i[:], 0).then_inc(consts_set, 1)
                pool.memset(ahead_i[:], 0).then_inc(consts_set, 1)
                pool.memset(ones[:], 1.0).then_inc(consts_set, 1)
                pool.memset(eps[:], EPS).then_inc(consts_set, 1)
                pool.memset(ident[:], 0.0).then_inc(consts_set, 1)
                pool.wait_ge(consts_set, 11)
                pool.affine_select(out=ident[:], in_=ident[:], compare_op=ALU.not_equal, fill=1.0, base=0,
                                   pattern=[[-1, P]], channel_multiplier=1).then_inc(ident_ready, 1)

            @block.sync
            def _(sp):
                sp.wait_ge(consts_set, 8)
                n_pad = EP - E
                for to, of in ((src_pad[0:E], one_row(src)), (src_pad[E:EP], pad_i[0:1, 0:n_pad]),
                               (dst_pad[1:1 + E], one_row(dst)), (dst_pad[1 + E:1 + EP], pad_i[0:1, 128:128 + n_pad]),
                               (dst_pad[0:1], pad_i[0:1, 384:385]), (dst_pad[1 + EP:1 + EP + P], pad_i[0:1, 256:384])):
                    sp.dma_start(one_row(to), of).then_inc(lists_padded, 16)
                sp.wait_ge(lists_padded, 6 * 16)
                half = lambda a: a.rearrange("(a k q) -> k a q", a=2, q=P)
                for n, a in enumerate((src_pad, dst_pad[1:1 + EP], dst_pad[0:EP], dst_pad[2:2 + EP])):
                    sp.dma_start(rows_i[0:HALF, n], half(a)).then_inc(rows_loaded, 16)
                sp.dma_start(ahead_i[0:HALF], half(dst_pad[1 + P:1 + P + EP])).then_inc(rows_loaded, 16)
                sp.dma_start(ahead_i[HALF:HALF + 1, 0], one_row(dst_pad[1:1 + P])).then_inc(rows_loaded, 16)
                sp.dma_start(rows_i[HALF:HALF + 1, 2, 0, 0:1], pad_i[0:1, 448:449]).then_inc(rows_loaded, 16)
                for r in (0, D):
                    for l in range(L):
                        sp.dma_start(w_raw[r:r + D, l].rearrange("p h o -> p (h o)"), Ws[l]).then_inc(weights_loaded, 16)
                    for h in range(H):
                        for_h = gat_bias[:, h * D:(h + 1) * D].rearrange("l f -> f l")
                        with nc.allow_non_contiguous_dma(reason="a few biases"):
                            sp.dma_start(bias_raw[r:r + D, :, h], for_h).then_inc(weights_loaded, 16)
                    sp.dma_start(hb[r:r + D], one_col(h_bias)).then_inc(weights_loaded, 16)
                for n, a in enumerate((attn_l, attn_r)):
                    flat = a.rearrange("l h f -> (l h f)")
                    sp.dma_start(a_raw[:, n].rearrange("p l n -> p (l n)"), lanes(flat, P)).then_inc(weights_loaded, 16)
                sp.dma_start(w_conv[:], W_full[0:P]).then_inc(weights_loaded, 16)
                sp.dma_start(w_conv3[:], W_full[P:P + D]).then_inc(weights_loaded, 16)
                for n, a in enumerate((b_full, bn1_g, bn1_b)):
                    sp.dma_start(bn_cols[:, n:n + 1], one_col(a)).then_inc(weights_loaded, 16)
                for n, a in enumerate((bn2_g, bn2_b)):
                    sp.dma_start(bn_cols[0:D, 3 + n:4 + n], one_col(a)).then_inc(weights_loaded, 16)
                sp.wait_ge(dve_step, KEEP_READY)
                sp.dma_start(half(keep_row[0:EP]), keep_u[:]).then_inc(keep_stored, 16)
                sp.dma_start(one_row(keep_row[EP:EP + 1]), last_keep[0:1, 0:1]).then_inc(keep_stored, 16)
                sp.wait_ge(keep_stored, 32)

            @block.vector
            def _(v):
                count = [0]

                def link(ins):
                    count[0] += 1
                    ins.then_inc(dve_step, 1)
                    v.wait_ge(dve_step, count[0])

                v.wait_ge(rows_loaded, 7 * 16)
                link(v.tensor_copy(rows_f[:], rows_i[:]))
                assert count[0] == ROWS_CONVERTED
                link(v.tensor_tensor(keep_u[:], rows_f[0:HALF, 1], rows_f[0:HALF, 2], ALU.is_equal))
                assert count[0] == KEEP_READY
                link(v.tensor_copy(ahead_f[:], ahead_i[:]))
                link(v.memset(steps_f[:], 1.0))
                link(v.tensor_tensor(steps_f[:, :, 1:2], rows_f[:, 1, :, P - 1:P], rows_f[:, 2, :, 0:1], ALU.subtract))
                link(v.tensor_tensor(steps_f[:, :, 2:2 + P], ahead_f[:], rows_f[:, 1], ALU.subtract))
                link(v.tensor_copy(steps_i[:], steps_f[:]))
                link(v.tensor_scalar(steps_i[:], steps_i[:], 255, None, ALU.bitwise_and))
                link(v.tensor_copy(steps_low[:], steps_i[:]))
                link(v.tensor_copy(steps[:, :, 1], steps_low[:]))
                link(v.tensor_tensor(steps[:, :, 0], steps_f[:], steps_low[:], ALU.subtract))
                link(v.tensor_copy(limit[:], rows_f[0:HALF, 1, :, P - 1]))
                v.wait_ge(pe_step, 1)
                link(v.tensor_copy(src_f[:], bank[0][:, 0:TILES]))
                link(v.tensor_copy(dst_f[:], bank[1][:, 0:TILES]))
                link(v.tensor_tensor(last_f[:], dst_f[:], bank[2][:, 0:TILES], ALU.not_equal))
                link(v.tensor_copy(src_row[:], src_f[:]))
                link(v.tensor_scalar(tmp_f[:], dst_f[:], float(N - 1), None, ALU.min))
                link(v.tensor_copy(dst_row[:], tmp_f[:]))
                link(v.tensor_scalar(tmp_f[:], dst_f[:], float(-FAR), None, ALU.add))
                link(v.tensor_tensor(tmp_f[:], tmp_f[:], last_f[:], ALU.mult))
                link(v.tensor_scalar(tmp_f[:], tmp_f[:], float(FAR), None, ALU.add))
                link(v.tensor_copy(scatter_row[:], tmp_f[:]))
                v.wait_ge(weights_loaded, WEIGHT_LOADS * 16)
                link(v.tensor_reduce(w_sum[:], w_raw[:].rearrange("p l h o -> p l o h"), AX_X, ALU.add))
                for n in range(2):
                    link(v.tensor_tensor(prod[:], w_raw[:].rearrange("p l h o -> p l (h o)"), a_raw[:, n], ALU.mult))
                    link(v.tensor_reduce(a_sum[:, n], prod[:].rearrange("p l (h o) -> p l h o", h=H), AX_X, ALU.add))
                link(v.tensor_reduce(b_all[:], bias_raw[:], AX_X, ALU.add))
                link(v.tensor_tensor(b_all[:, L - 1:L], b_all[:, L - 1:L], hb[:], ALU.add))
                for h in range(H):
                    r = (h % 2) * D
                    link(v.tensor_copy(w_heads[r:r + D, :, h // 2, :], w_raw[r:r + D, :, h, :]))
                v.wait_ge(ident_ready, 1)
                link(v.memset(w_row[:], 0.0))
                link(v.memset(w_edge0[:], 0.0))
                eye = ident[0:D, 0:D].unsqueeze(1).broadcast_to([D, L, D])
                v.tensor_copy(w_row[0:D, :, 0:D], eye).then_inc(dve_step, 1)
                v.tensor_copy(w_row[0:D, 0:L - 1, D:ROW], a_sum[0:D, 0, 1:L]).then_inc(dve_step, 1)
                v.tensor_copy(w_edge[:, :, 0:D], eye).then_inc(dve_step, 1)
                v.tensor_copy(w_edge[:, :, D:D + H], a_sum[0:D, 1]).then_inc(dve_step, 1)
                v.tensor_tensor(w_edge[:, :, D + H:EDGE_W], a_sum[0:D, 0], a_sum[0:D, 1], ALU.add).then_inc(dve_step, 1)
                v.tensor_copy(w_edge0[0:D, 0:H], a_sum[0:D, 0, 0]).then_inc(dve_step, 1)
                v.tensor_copy(w_edge0[D:P, 0:H], a_sum[D:P, 1, 0]).then_inc(dve_step, 1)
                v.tensor_tensor(w_edge0[D:P, H:2 * H], a_sum[D:P, 0, 0], a_sum[D:P, 1, 0], ALU.add).then_inc(dve_step, 1)
                v.tensor_copy(chain_t[:, 0], ident[0:D, 0:D]).then_inc(dve_step, 1)
                v.memset(const_h[:, 0:1], 0.0).then_inc(dve_step, 1)
                count[0] += 10
                v.wait_ge(dve_step, count[0])
                v.tensor_copy(w_row[D:P, :, 0:D], w_sum[D:P]).then_inc(dve_step, 1)
                count[0] += 1
                assert count[0] == WEIGHTS_SUMMED, count
                for l in range(L):
                    v.wait_ge(pe_step, 2 + 2 * l)
                    v.tensor_copy(wsum_t[:, l], bank[3][0:D, 0:D]).then_inc(dve_step, 1)
                    v.tensor_copy(chain_t[:, l + 1], bank[3][0:D, D:2 * D]).then_inc(dve_step, 1)
                    v.tensor_tensor(const_h[:, l + 1:l + 2], bank[3][0:D, 2 * D:2 * D + 1], b_all[0:D, l:l + 1],
                                    ALU.add).then_inc(dve_step, 1)
                    v.wait_ge(dve_step, WEIGHTS_SUMMED + 8 * l + 3)
                    v.tensor_scalar(c_rep[:], ones[0:D, :], const_h[:, l + 1:l + 2], None, ALU.mult).then_inc(dve_step, 1)
                    v.wait_ge(pe_step, 3 + 2 * l)
                    if l < L - 1:
                        v.tensor_copy(w_row[D:P, l, D:ROW], bank[4][0:D, 0:H]).then_inc(dve_step, 1)
                    else:
                        v.memset(w_row[D:P, l, D:ROW], 0.0).then_inc(dve_step, 1)
                    if l < L - 1:
                        v.tensor_copy(w_chain[:, l], bank[4][0:D, 128:128 + ROW]).then_inc(dve_step, 1)
                        v.tensor_copy(const_logit[:, l + 1], bank[4][:, 384:384 + H]).then_inc(dve_step, 2)
                    else:
                        v.tensor_copy(w_node[0:D], bank[4][0:D, 128:128 + D]).then_inc(dve_step, 1)
                        v.tensor_copy(w_node[D:D + 1], bank[4][0:1, 256:256 + D]).then_inc(dve_step, 1)
                        v.tensor_copy(const_row[:], bank[4][:, 384:384 + D]).then_inc(dve_step, 1)

            @block.tensor
            def _(t):
                t.wait_ge(ident_ready, 1)
                t.wait_ge(dve_step, 3)
                for n, src_rows in enumerate((0, 1, 3)):
                    for a in range(2):
                        last = t.transpose(bank[n][:, a * HALF:(a + 1) * HALF], rows_f[0:HALF, src_rows, a], ident[0:HALF, 0:HALF])
                last.then_inc(pe_step, 1)
                base = WEIGHTS_SUMMED
                t.wait_ge(dve_step, base)
                for l in range(L):
                    t.wait_ge(dve_step, base + 8 * l)
                    t.matmul(bank[3][0:D, 0:D], w_sum[0:D, l], ident[0:D, 0:D], start=True, stop=True)
                    t.matmul(bank[3][0:D, D:2 * D], w_sum[0:D, l], chain_t[:, l], start=True, stop=True)
                    t.matmul(bank[3][0:D, 2 * D:2 * D + 1], w_sum[0:D, l], const_h[:, l:l + 1], start=True, stop=True).then_inc(pe_step, 1)
                    t.wait_ge(dve_step, base + 8 * l + 4)
                    if l < L - 1:
                        t.matmul(bank[4][0:D, 0:H], wsum_t[:, l], w_row[0:D, l, D:ROW], start=True, stop=True)
                    t.matmul(bank[4][0:D, 128:128 + ROW], chain_t[:, l + 1], w_row[0:D, l], start=True, stop=True)
                    t.matmul(bank[4][0:1, 256:256 + ROW], const_h[:, l + 1:l + 2], w_row[0:D, l], start=True, stop=True)
                    of = w_edge[:, l + 1, D + H:] if l < L - 1 else ident[0:D, 0:D]
                    t.matmul(bank[4][:, 384:384 + of.shape[-1]], c_rep[:], of, start=True, stop=True).then_inc(pe_step, 1)


        with ExitStack() as st:
            SLOTS = 4
            uses = [(G - s + SLOTS - 1) // SLOTS for s in range(SLOTS)]
            got = mem(st, "got", [P, 2, TPG, D])
            norm = mem(st, "norm", [P, 2, TPG, 2, D])
            square = mem(st, "square", [P, TPG * 2, D])
            norm_t = mem(st, "norm_t", [P, GE])
            chain_rows = mem(st, "chain_rows", [P, L - 1, TPG, ROW])
            stat = mem(st, "stat", [P, 2, 4, TPG, 2])
            logs = mem(st, "logs", [P, TPG * 2])
            nodes = mem(st, "nodes", [P, SLOTS, NODE_T, D])
            n_norm = mem(st, "n_norm", [P, 2, NODE_T, D + 1])
            n_square = mem(st, "n_square", [P, NODE_T, D])
            n_norm_t = mem(st, "n_norm_t", [D + 1, NODE_T * P])
            n_stat = mem(st, "n_stat", [P, 2, 4, NODE_T])
            n_logs = mem(st, "n_logs", [P, NODE_T])
            sources = mem(st, "sources", [HALF, GE], I32)
            reached = mem(st, "reached", [HALF + 1, 2, GE], BF16)
            matches = mem(st, "matches", [P, 2, 2, 2, P + 1], BF16)
            gathered = [pool_dma_sem(f"gathered{s}") for s in range(SLOTS)]
            nodes_in = [sem(st, f"nodes_in{s}") for s in range(SLOTS)]
            x_saved = [sem(st, f"x_saved{s}") for s in range(SLOTS)]
            x1_saved = [sem(st, f"x1_saved{s}") for s in range(SLOTS)]
            sources_in = sem(st, "sources_in")
            chain_saved = sem(st, "chain_saved")
            summed, mean, centered, squared, summed2, logged, rstd, normed, subtracted, norm_in_psum, norm_t_ready, \
                wide_ready, edges_in_psum, rows_ready, logits_ready = [
                    sem(st, f"e_{name}") for name in (
                        "summed", "mean", "centered", "squared", "summed2", "logged", "rstd", "normed", "subtracted",
                        "norm_in_psum", "norm_t_ready", "wide_ready", "edges_in_psum", "rows_ready", "logits_ready")]
            n_summed, n_mean, n_centered, n_squared, n_summed2, n_logged, n_rstd, n_normed, n_in_psum, n_t_ready, \
                n_out, x1_ready = [
                    sem(st, f"n_{name}") for name in (
                        "summed", "mean", "centered", "squared", "summed2", "logged", "rstd", "normed", "in_psum",
                        "t_ready", "out", "x1_ready")]
            reached_ready = sem(st, "reached_ready")
            searched = sem(st, "searched")
            compared = sem(st, "compared")
            looked_up = sem(st, "looked_up")
            ones_set = sem(st, "ones_set")
            paced = sem(st, "paced")
            sp_paced = sem(st, "sp_paced")
            block = st.enter_context(nc.Block())
            COMPARES = 4

            @block.gpsimd
            def _(pool):
                for k in range(G):
                    s = k % SLOTS
                    if k >= 2:
                        before = k - 2
                        pool.wait_ge(centered, at(before))
                        pool.wait_ge(x_saved[before % SLOTS], 16 * (before // SLOTS + 1))
                    for t in range(TPG):
                        tile = TPG * k + t
                        for rows, to in ((src_row, edge[:, tile, 0:D]), (dst_row, got[:, k % 2, t])):
                            pool.indirect_dma_start(
                                out=to, out_offset=None, in_=x,
                                in_offset=bass.IndirectOffsetOnAxis(ap=rows[:, tile:tile + 1], axis=0),
                            ).then_inc(gathered[s], 16)

            @block.sync
            def _(sp):
                def load(k, g, s, turn):
                    used = LAST_P if isinstance(k, int) and k == G - 1 else P
                    sp.wait_ge(x1_saved[s], turn * 16 + 16)
                    sp.sem_inc(sp_paced, 1)
                    sp.dma_start(nodes[0:used, s], x[bass.ds(k * GN, used * NODE_T)].rearrange("(p j) f -> p j f", j=NODE_T)).then_inc(nodes_in[s], 16)
                    sp.wait_ge(reached_ready, at(k, back=1))
                    sp.sem_inc(sp_paced, 1)
                    sp.dma_start(sources[:], lanes(src_pad[bass.ds(k * GE, GE)], HALF)).then_inc(sources_in, 16)

                def save_x(k, g, s, turn):
                    sp.wait_ge(gathered[s], turn * (16 * 8) + 16 * 8)
                    sp.sem_inc(sp_paced, 1)
                    sp.dma_start(x_dst.rearrange("p (t f) -> p t f", f=D)[:, bass.ds(k * TPG, TPG)], got[:, s % 2]).then_inc(x_saved[s], 16)

                def save(k, g, s, turn):
                    used = LAST_P if isinstance(k, int) and k == G - 1 else P
                    sp.wait_ge(x1_ready, at(k))
                    sp.sem_inc(sp_paced, 1)
                    sp.dma_start(tables[L - 1][bass.ds(k * GN, used * NODE_T)].rearrange("(p j) f -> p j f", j=NODE_T),
                                 nodes[0:used, s]).then_inc(x1_saved[s], 16)
                    sp.wait_ge(rows_ready, at(k))
                    sp.sem_inc(sp_paced, 1)
                    for l in range(L - 1):
                        sp.dma_start(tables[l][0:EP].rearrange("(p t) w -> p t w", p=P)[:, bass.ds(k * TPG, TPG)],
                                     chain_rows[:, l]).then_inc(chain_saved, 16)

                for s in range(SLOTS):
                    sp.sem_inc(x1_saved[s], 16)
                sp.sem_inc(chain_saved, 16)
                pipelined(sp, ((1, save_x), (4, save), (0, load)), slots=SLOTS)
                for s in range(SLOTS):
                    sp.wait_ge(x_saved[s], 16 * uses[s])
                    sp.wait_ge(x1_saved[s], 16 * uses[s] + 16)
                sp.wait_ge(chain_saved, 16 * ((L - 1) * G + 1))

            @block.vector
            def _(v):
                for signal in (summed, mean, centered, summed2, normed, subtracted, n_summed, n_mean, n_centered, n_summed2,
                               n_normed, x1_ready, reached_ready, looked_up):
                    v.sem_inc(signal, AHEAD)
                v.memset(reached[:], 1.0).then_inc(ones_set, 1)
                v.memset(n_norm[:], 1.0).then_inc(ones_set, 1)
                v.wait_ge(ones_set, 2)

                def center(k, g, s, turn):
                    h = s % 2
                    v.wait_ge(gathered[s], turn * (16 * 8) + 16 * 8)
                    v.sem_inc(paced, 1)
                    v.tensor_reduce(stat[:, h, 0, :, 0], edge[:, bass.ds(k * TPG, TPG), 0:D], AX_X, ALU.add)
                    v.tensor_reduce(stat[:, h, 0, :, 1], got[:, h], AX_X, ALU.add).then_inc(summed, 1)
                    v.wait_ge(nodes_in[s], turn * 16 + 16)
                    v.tensor_reduce(n_stat[:, h, 0], nodes[:, s], AX_X, ALU.add).then_inc(n_summed, 1)
                    v.wait_ge(summed, at(k))
                    v.wait_ge(norm_in_psum, at(k, back=2))
                    v.wait_ge(subtracted, at(k, back=2))
                    for n, rows in enumerate((edge[:, bass.ds(k * TPG, TPG), 0:D], got[:, h])):
                        last = v.scalar_tensor_tensor(out=norm[:, h, :, n], in0=inner(stat[:, h, 0, :, n], [P, TPG, D]), scalar=-1.0 / D,
                                                      in1=rows, op0=ALU.mult, op1=ALU.add)
                    last.then_inc(centered, 1)
                    v.wait_ge(n_summed, at(k))
                    v.wait_ge(n_in_psum, at(k, back=2))
                    v.scalar_tensor_tensor(out=n_norm[:, h, :, 0:D], in0=inner(n_stat[:, h, 0], [P, NODE_T, D]), scalar=-1.0 / D,
                                           in1=nodes[:, s], op0=ALU.mult, op1=ALU.add).then_inc(n_centered, 1)

                def variance(k, g, s, turn):
                    v.wait_ge(squared, at(k))
                    v.tensor_reduce(stat[:, s % 2, 2].rearrange("p t e -> p (t e)"), square[:], AX_X, ALU.add).then_inc(summed2, 1)

                def normalize(k, g, s, turn):
                    h = s % 2
                    part = norm[:, h].rearrange("p t e f -> p (t e) f")
                    v.wait_ge(rstd, at(k))
                    v.scalar_tensor_tensor(out=part, in0=part, scalar=0.0, in1=inner(stat[:, h, 3].rearrange("p t e -> p (t e)"), [P, 2 * TPG, D]),
                                           op0=ALU.max, op1=ALU.mult).then_inc(normed, 1)
                    n_part = n_norm[:, h, :, 0:D]
                    v.wait_ge(n_rstd, at(k))
                    v.scalar_tensor_tensor(out=n_part, in0=n_part, scalar=0.0, in1=inner(n_stat[:, h, 3], [P, NODE_T, D]),
                                           op0=ALU.max, op1=ALU.mult).then_inc(n_normed, 1)
                    v.wait_ge(normed, at(k))
                    v.tensor_tensor(edge[:, bass.ds(k * TPG, TPG), 0:D], norm[:, h, :, 0], norm[:, h, :, 1], ALU.subtract).then_inc(subtracted, 1)

                def n_variance(k, g, s, turn):
                    v.wait_ge(n_squared, at(k))
                    v.tensor_reduce(n_stat[:, s % 2, 2], n_square[:], AX_X, ALU.add).then_inc(n_summed2, 1)

                def n_finish(k, g, s, turn):
                    v.wait_ge(n_out, at(k))
                    v.tensor_tensor(nodes[:, s], bank[1][:].rearrange("p (j f) -> p j f", f=D), nodes[:, s], ALU.add).then_inc(x1_ready, 1)

                def reach(k, g, s, turn):
                    v.wait_ge(sources_in, k * 16 + 16)
                    v.wait_ge(searched, at(k, back=1))
                    v.tensor_scalar(reached[0:HALF, 0], sources[:], limit[:, 0:1], None, ALU.is_ge)
                    v.tensor_scalar(reached[0:HALF, 1], sources[:], limit[:, 1:2], None, ALU.is_ge).then_inc(reached_ready, 1)

                def look_up(k, g, s, turn):
                    v.wait_ge(searched, at(k))
                    tiles = bass.ds(k * TPG, TPG)
                    found = banks[:, 6:8, 0:2 * (P + 2)].rearrange("p b (t q) -> p b t q", q=P + 2)
                    mine = src_f[:, tiles].rearrange("p (b t) -> p b t", b=2).unsqueeze(3).broadcast_to([P, 2, 2, P + 1])
                    v.tensor_scalar(tiles_before[:, tiles].rearrange("p (b t) -> p b t", b=2), found[:, :, :, 0], -1.0, None, ALU.add)
                    for n, op in enumerate((ALU.is_le, ALU.is_equal)):
                        v.tensor_tensor(matches[:, n], found[:, :, :, 1:], mine, op).then_inc(compared, 1)
                    for n, to in enumerate((not_above, equal_to)):
                        v.wait_ge(compared, k * COMPARES + (n + 1))
                        v.sem_inc(paced, 1)
                        v.tensor_reduce(to[:, tiles].rearrange("p (b t) -> p b t", b=2), matches[:, n], AX_X, ALU.add).then_inc(compared, 1)
                    v.wait_ge(compared, k * COMPARES + COMPARES)
                    v.sem_inc(looked_up, 1)

                pipelined(v, ((3, normalize), (2, variance), (2, n_variance), (2, look_up), (1, center), (1, reach),
                              (4, n_finish)), slots=SLOTS)

            @block.scalar
            def _(s_):
                s_.preload_act_table_set(ACT_TABLES)
                for signal in (squared, logged, rstd, norm_t_ready, wide_ready, rows_ready, logits_ready, n_squared, n_logged,
                               n_rstd, n_t_ready):
                    s_.sem_inc(signal, AHEAD)

                def squares(k, g, s, turn):
                    s_.wait_ge(centered, at(k))
                    s_.wait_ge(summed2, at(k, back=1))
                    s_.activation(square[:].rearrange("p t f -> p (t f)"), norm[:, s % 2].rearrange("p t e f -> p (t e f)"), ACT.Square).then_inc(squared, 1)

                def n_squares(k, g, s, turn):
                    s_.wait_ge(n_centered, at(k))
                    s_.wait_ge(n_summed2, at(k, back=1))
                    s_.activation(n_square[:], n_norm[:, s % 2, :, 0:D], ACT.Square).then_inc(n_squared, 1)

                def scales(k, g, s, turn):
                    s_.wait_ge(summed2, at(k))
                    s_.activation(logs[:], stat[:, s % 2, 2].rearrange("p t e -> p (t e)"), ACT.Ln, bias=eps[:], scale=1.0 / D).then_inc(logged, 1)
                    s_.wait_ge(logged, at(k))
                    s_.activation(stat[:, s % 2, 3].rearrange("p t e -> p (t e)"), logs[:], ACT.Exp, scale=-0.5).then_inc(rstd, 1)
                    s_.wait_ge(n_summed2, at(k))
                    s_.activation(n_logs[:], n_stat[:, s % 2, 2], ACT.Ln, bias=eps[:], scale=1.0 / D).then_inc(n_logged, 1)
                    s_.wait_ge(n_logged, at(k))
                    s_.activation(n_stat[:, s % 2, 3], n_logs[:], ACT.Exp, scale=-0.5).then_inc(n_rstd, 1)

                def take(k, g, s, turn):
                    s_.wait_ge(norm_in_psum, at(k))
                    s_.wait_ge(edges_in_psum, at(k, back=1))
                    s_.activation(norm_t[:], bank[0][:], ACT.Copy).then_inc(norm_t_ready, 1)
                    s_.activation(wide[D:P, bass.ds(k * GE + 1, GE)], bank[0][D:P, :], ACT.Copy).then_inc(wide_ready, 1)
                    s_.wait_ge(n_in_psum, at(k))
                    s_.wait_ge(n_out, at(k, back=1))
                    s_.activation(n_norm_t[:, 0:GE], bank[2][0:D + 1, :], ACT.Copy)
                    s_.activation(n_norm_t[:, GE:], bank[3][0:D + 1, :], ACT.Copy).then_inc(n_t_ready, 1)

                def edge_out(k, g, s, turn):
                    tiles = bass.ds(k * TPG, TPG)
                    s_.wait_ge(edges_in_psum, at(k))
                    s_.wait_ge(chain_saved, k * (16 * (L - 1)) + 16)
                    for n in range(2):
                        last = s_.activation(chain_rows[:, :, 2 * n:2 * n + 2].rearrange("p l t w -> p t l w"),
                                             bank[4 + n][:, 0:2 * (L - 1) * ROW].rearrange("p (t l w) -> p t l w", t=2, w=ROW), ACT.Copy)
                    last.then_inc(rows_ready, 1)
                    both = bank[5][:, 2 * (L - 1) * ROW:2 * (L - 1) * ROW + TPG * 2 * H].rearrange("p (t e) -> p t e", e=2 * H)
                    s_.activation(edge[:, tiles, D:ROW], both[:, :, 0:H], ACT.Copy)
                    s_.activation(self_logit[:, tiles], both[:, :, H:], ACT.Copy).then_inc(logits_ready, 1)

                pipelined(s_, ((2, scales), (3, take), (4, edge_out), (1, squares), (1, n_squares)), slots=SLOTS)

            @block.tensor
            def _(t_):
                for signal in (norm_in_psum, edges_in_psum, n_in_psum, n_out, searched):
                    t_.sem_inc(signal, AHEAD)

                def transposes(k, g, s, turn):
                    t_.wait_ge(normed, at(k))
                    t_.wait_ge(wide_ready, at(k, back=1))
                    for t in range(TPG):
                        last = t_.transpose(bank[0][:, t * P:(t + 1) * P], norm[:, s % 2, t].rearrange("p e f -> p (e f)"), ident[:])
                    last.then_inc(norm_in_psum, 1)

                def n_transposes(k, g, s, turn):
                    t_.wait_ge(n_normed, at(k))
                    t_.wait_ge(n_t_ready, at(k, back=1))
                    for j in range(NODE_T):
                        last = t_.transpose(bank[2 + j // TPG][0:D + 1, (j % TPG) * P:(j % TPG + 1) * P], n_norm[:, s % 2, j], ident[:])
                    last.then_inc(n_in_psum, 1)

                def edges(k, g, s, turn):
                    t_.wait_ge(norm_t_ready, at(k))
                    t_.wait_ge(logits_ready, at(k, back=1))
                    for t in range(TPG):
                        mine = norm_t[:, t * P:(t + 1) * P]
                        width = (L - 1) * ROW
                        t_.matmul(bank[4 + t // 2][:, (t % 2) * width:(t % 2 + 1) * width], mine[0:D], w_chain[:].rearrange("p l w -> p (l w)"),
                                  start=True, stop=True)
                        last = t_.matmul(bank[5][:, 2 * width + t * 2 * H:2 * width + (t + 1) * 2 * H], mine, w_edge0[:], start=True, stop=True)
                    last.then_inc(edges_in_psum, 1)

                def n_outs(k, g, s, turn):
                    t_.wait_ge(n_t_ready, at(k))
                    t_.wait_ge(x1_ready, at(k, back=1))
                    for j in range(NODE_T):
                        last = t_.matmul(bank[1][:, j * D:(j + 1) * D], n_norm_t[:, j * P:(j + 1) * P], w_node[:], start=True, stop=True)
                    last.then_inc(n_out, 1)

                def search(k, g, s, turn):
                    t_.wait_ge(reached_ready, at(k))
                    t_.wait_ge(looked_up, at(k, back=1))
                    for t in range(TPG):
                        to = bank[6 + t // 2][:, (t % 2) * (P + 2):(t % 2 + 1) * (P + 2)]
                        for n in range(4):
                            half, part = n // 2, n % 2
                            up_to = (HALF + 1, HALF)[half]
                            last = t_.matmul(to, reached[0:up_to, half, t * P:(t + 1) * P], steps[0:up_to, half, part], start=n == 0, stop=n == 3)
                    last.then_inc(searched, 1)

                pipelined(t_, ((3, transposes), (3, n_transposes), (4, edges), (4, n_outs), (1, search)), slots=SLOTS)

        def softmax_weights(l, alpha):
            with ExitStack() as st:
                leaky = mem(st, f"leaky_{l}", [P, 2, CT, Q])
                logit = mem(st, f"logit_{l}", [Q, 2, CE])
                fwd = mem(st, f"fwd_{l}", [Q, CE])
                rev = mem(st, f"rev_{l}", [Q, CE])
                stop_q = mem(st, f"stop_q_{l}", [Q, CE + 1])
                ends = mem(st, f"ends_{l}", [1, 2, Q])
                chain = mem(st, f"chain_{l}", [1, 2, 2, Q + H])
                carry = mem(st, f"carry_{l}", [Q, 2])
                own = sem(st, f"own_{l}")
                leaky_ready = sem(st, f"leaky_ready_{l}")
                logit_t = sem(st, f"logit_t_{l}")
                logit_ready = sem(st, f"logit_ready_{l}")
                scanned = sem(st, f"scanned_{l}")
                ends_t = sem(st, f"ends_t_{l}")
                chained = sem(st, f"chained_{l}")
                carry_t = sem(st, f"carry_t_{l}")
                shifted = sem(st, f"shifted_{l}")
                exped = sem(st, f"exped_{l}")
                alpha_q = sem(st, f"alpha_q_{l}")
                alpha_t = sem(st, f"alpha_t_{l}")
                block = st.enter_context(nc.Block())

                @block.vector
                def _(v):
                    count = [0]

                    def link(ins):
                        count[0] += 1
                        ins.then_inc(own, 1)
                        v.wait_ge(own, count[0])

                    for n, e in enumerate((edge[:, :, D:ROW], self_logit[:])):
                        if l > 0:
                            link(v.tensor_tensor(e, e, const_logit[:, l].unsqueeze(1).broadcast_to([P, TILES, H]), ALU.add))
                        for b in range(CT):
                            of = e[:, b:TILES:CT]
                            v.scalar_tensor_tensor(out=leaky[:, n, b].rearrange("p (s h) -> p s h", h=H), in0=of, scalar=SLOPE,
                                                   in1=of, op0=ALU.mult, op1=ALU.max).then_inc(leaky_ready, 1)
                    link(v.tensor_scalar(stop_q[:], keep_q[:], -1.0, BIG, ALU.add, ALU.mult))
                    link(v.memset(chain[:, 0], -BIG))
                    link(v.memset(chain[:, 1], 0.0))
                    v.wait_ge(logit_ready, 4)

                    def both_ways(n, gate, op0, op1, start, values):
                        before = dict(data0=gate[:, 0:CE], data1=values, op0=op0, op1=op1)
                        behind = dict(data0=gate[:, 1:CE + 1][:, ::-1], data1=values[:, ::-1], op0=op0, op1=op1)
                        link(v.tensor_tensor_scan(out=fwd[:], initial=start, **before))
                        link(v.tensor_tensor_scan(out=rev[:, ::-1], initial=start, **behind))
                        v.sem_inc(scanned, 1)
                        v.wait_ge(ends_t, 2 * n + 2)
                        for side in range(2):
                            link(v.tensor_copy(ends[:, side], bank[side][0:1, 0:Q]))
                        for h in range(H):
                            way = lambda a, skip: a[:, skip + h:skip + Q:H]
                            link(v.tensor_tensor_scan(out=way(chain[:, n, 0], H), data0=way(carry_in[:, 2 - 2 * n], 0),
                                                      data1=way(ends[:, 0], 0), initial=start, op0=op0, op1=op1))
                            link(v.tensor_tensor_scan(out=way(chain[:, n, 1], 0)[:, ::-1], data0=way(carry_in[:, 3 - 2 * n], 0)[:, ::-1],
                                                      data1=way(ends[:, 1], 0)[:, ::-1], initial=start, op0=op0, op1=op1))
                        v.sem_inc(chained, 1)
                        v.wait_ge(carry_t, 2 * n + 2)
                        link(v.tensor_copy(carry[:], bank[2][0:Q, 0:2]))
                        link(v.tensor_tensor_scan(out=fwd[:], initial=carry[:, 0:1], **before))
                        link(v.tensor_tensor_scan(out=rev[:, ::-1], initial=carry[:, 1:2], **behind))

                    both_ways(0, stop_q, ALU.add, ALU.max, -BIG, logit[:, 0])
                    link(v.tensor_tensor(fwd[:], fwd[:], rev[:], ALU.max))
                    link(v.tensor_tensor(fwd[:], fwd[:], logit[:, 1], ALU.max))
                    for n in range(2):
                        v.tensor_tensor(logit[:, n], logit[:, n], fwd[:], ALU.subtract).then_inc(shifted, 1)
                    v.wait_ge(exped, 2)
                    both_ways(1, keep_q, ALU.mult, ALU.add, 0.0, logit[:, 0])
                    link(v.tensor_tensor(rev[:], rev[:], logit[:, 0], ALU.subtract))
                    link(v.tensor_tensor(fwd[:], fwd[:], rev[:], ALU.add))
                    link(v.tensor_tensor(fwd[:], fwd[:], logit[:, 1], ALU.add))
                    link(v.reciprocal(fwd[:], fwd[:]))
                    v.tensor_tensor(logit[:, 0], logit[:, 0], fwd[:], ALU.mult).then_inc(alpha_q, 1)
                    to = alpha[:].rearrange("p (s b) h -> p s b h", b=CT)
                    for n, (b0, b1) in enumerate(((0, 4), (4, CT))):
                        v.wait_ge(alpha_t, n + 1)
                        link(v.tensor_copy(to[:, :, b0:b1], bank[4 + n][:, 0:(b1 - b0) * Q].rearrange("p (b s h) -> p s b h", s=CH, h=H)))

                @block.scalar
                def _(s_):
                    for n in range(2):
                        for m in range(2):
                            cols = GE if m == 0 else CE - GE
                            s_.wait_ge(logit_t, 2 * n + m + 1)
                            s_.activation(logit[:, n, m * GE:m * GE + cols], bank[2 * n + m][0:Q, 0:cols], ACT.Copy).then_inc(logit_ready, 1)
                    for n in range(2):
                        s_.wait_ge(shifted, n + 1)
                        s_.activation(logit[:, n], logit[:, n], ACT.Exp).then_inc(exped, 1)

                @block.tensor
                def _(t):
                    for n in range(2):
                        t.wait_ge(leaky_ready, CT * (n + 1))
                        for b in range(CT):
                            last = t.transpose(bank[2 * n + b // 4][0:Q, (b % 4) * P:(b % 4 + 1) * P], leaky[:, n, b], ident[:])
                            if b == 3:
                                last.then_inc(logit_t, 1)
                        last.then_inc(logit_t, 1)
                    t.wait_ge(logit_ready, 4)
                    for n in range(2):
                        t.wait_ge(scanned, n + 1)
                        t.matmul(bank[0][0:1, 0:Q], fwd[:, CE - 1:CE], ident[0:Q, 0:Q], start=True, stop=True).then_inc(ends_t, 1)
                        t.matmul(bank[1][0:1, 0:Q], rev[:, 0:1], ident[0:Q, 0:Q], start=True, stop=True).then_inc(ends_t, 1)
                        t.wait_ge(chained, n + 1)
                        t.matmul(bank[2][0:Q, 0:1], chain[:, n, 0, 0:Q], ones[0:1, 0:1], start=True, stop=True).then_inc(carry_t, 1)
                        t.matmul(bank[2][0:Q, 1:2], chain[:, n, 1, H:H + Q], ones[0:1, 0:1], start=True, stop=True).then_inc(carry_t, 1)
                    t.wait_ge(alpha_q, 1)
                    for b in range(CT):
                        last = t.transpose(bank[4 + b // 4][:, (b % 4) * Q:(b % 4 + 1) * Q], logit[:, 0, b * P:(b + 1) * P], ident[0:Q, 0:Q])
                        if b == 3:
                            last.then_inc(alpha_t, 1)
                    last.then_inc(alpha_t, 1)

        def messages(l, alpha):
            width = ROW if l < L - 1 else D
            first_row = EP if l < L - 1 else N
            with ExitStack() as st:
                scaled = mem(st, f"scaled_{l}", [P, 2, TPG, H, D])
                scaled_t = mem(st, f"scaled_t_{l}", [P, 2, 2, GE])
                ring = mem(st, f"ring_{l}", [P, 2, GE])
                rows = mem(st, f"rows_{l}", [P, 2, TPG, width])
                x_again = mem(st, f"x_again_{l}", [P, 2, TPG, D]) if l == L - 1 else None
                keep = mem(st, f"keep_{l}", [D, 2, GE], U8)
                keep_in = [sem(st, f"keep_in_{l}_{s}") for s in range(2)]
                x_in = [sem(st, f"x_in_{l}_{s}") for s in range(2)]
                saved = [sem(st, f"saved_{l}_{s}") for s in range(2)]
                scaled_ready = sem(st, f"scaled_ready_{l}")
                scaled_in_psum = sem(st, f"scaled_in_psum_{l}")
                scaled_t_ready = sem(st, f"scaled_t_ready_{l}")
                message_ready = sem(st, f"message_ready_{l}")
                summed = sem(st, f"summed_{l}")
                ring_ready = sem(st, f"ring_ready_{l}")
                rows_in_psum = sem(st, f"rows_in_psum_{l}")
                rows_ready = sem(st, f"rows_ready_{l}")
                x_added = sem(st, f"x_added_{l}")
                act_paced = sem(st, f"act_paced_{l}")
                sp_paced = sem(st, f"sp_paced_{l}")
                block = st.enter_context(nc.Block())
                last_step = l == L - 1

                @block.sync
                def _(sp):
                    def load(k, g, s, turn):
                        sp.wait_ge(summed, at(k, back=2))
                        sp.sem_inc(sp_paced, 1)
                        sp.dma_start(keep[:, s], lanes(keep_row[bass.ds(g * GE, GE)], D)).then_inc(keep_in[s], 16)
                        if last_step:
                            sp.wait_ge(x_added, at(k, back=2))
                            sp.sem_inc(sp_paced, 1)
                            sp.dma_start(x_again[:, s], x_dst.rearrange("p (t f) -> p t f", f=D)[:, bass.ds(g * TPG, TPG)]).then_inc(x_in[s], 16)

                    def save(k, g, s, turn):
                        sp.wait_ge(x_added if last_step else rows_ready, at(k))
                        sp.sem_inc(sp_paced, 1)
                        sp.dma_start(tables[l][first_row:first_row + EP].rearrange("(p t) w -> p t w", p=P)[:, bass.ds(g * TPG, TPG)],
                                     rows[:, s]).then_inc(saved[s], 16)

                    for s in range(2):
                        sp.sem_inc(saved[s], 32)
                    pipelined(sp, ((1, load), (4, save)))
                    sp.wait_ge(saved[0], 16 * (G // 2 + 1) + 32)
                    sp.wait_ge(saved[1], 16 * (G // 2) + 32)

                @block.vector
                def _(v):
                    for signal in (scaled_ready, summed, rows_ready, x_added):
                        v.sem_inc(signal, AHEAD)

                    def scale(k, g, s, turn):
                        tiles = bass.ds(g * TPG, TPG)
                        v.wait_ge(scaled_in_psum, at(k, back=2))
                        v.tensor_tensor(scaled[:, s], edge[:, tiles, 0:D].unsqueeze(2).broadcast_to([P, TPG, H, D]),
                                        inner(alpha[:, tiles], [P, TPG, H, D]), ALU.mult).then_inc(scaled_ready, 1)

                    def scan(k, g, s, turn):
                        v.wait_ge(keep_in[s], turn * 16 + 16)
                        v.wait_ge(message_ready, at(k))
                        v.wait_ge(summed, at(k, back=1))
                        v.tensor_tensor_scan(out=wide[0:D, bass.ds(g * GE + 1, GE)], data0=keep[:, s], data1=bank[2 + s][0:D],
                                             initial=wide[0:D, bass.ds(g * GE, 1)], op0=ALU.mult, op1=ALU.add).then_inc(summed, 1)

                    def stage(k, g, s, turn):
                        v.wait_ge(rows_in_psum, at(k))
                        v.wait_ge(saved[s], turn * 16 + 32)
                        here = bank[4 + s][:, 0:TPG * width].rearrange("p (t w) -> p t w", w=width)
                        if not last_step:
                            v.tensor_copy(rows[:, s], here).then_inc(rows_ready, 1)
                        if last_step:
                            v.tensor_tensor(rows[:, s], here, const_row[:].unsqueeze(1).broadcast_to([P, TPG, D]), ALU.add).then_inc(rows_ready, 1)
                            v.wait_ge(rows_ready, at(k))
                            v.wait_ge(x_in[s], turn * 16 + 16)
                            v.tensor_tensor(rows[:, s], rows[:, s], x_again[:, s], ALU.add).then_inc(x_added, 1)

                    v.memset(wide[0:D, 0:1], 0.0).then_inc(sp_paced, 1)
                    pipelined(v, ((0, scale), (2, scan), (3, stage)))

                @block.scalar
                def _(s_):
                    s_.preload_act_table_set(ACT_TABLES)
                    for signal in (scaled_t_ready, ring_ready):
                        s_.sem_inc(signal, AHEAD)

                    def take(k, g, s, turn):
                        s_.wait_ge(scaled_in_psum, at(k))
                        s_.wait_ge(message_ready, at(k, back=2))
                        s_.activation(scaled_t[:, s, 0], bank[6 * s][:], ACT.Copy)
                        s_.activation(scaled_t[:, s, 1], bank[6 * s + 1][:], ACT.Copy).then_inc(scaled_t_ready, 1)

                    def to_ring(k, g, s, turn):
                        s_.wait_ge(summed, at(k))
                        s_.wait_ge(rows_in_psum, at(k, back=2))
                        s_.sem_inc(act_paced, 1)
                        s_.activation(ring[:, s], wide[:, bass.ds(g * GE + 1, GE)], ACT.Copy).then_inc(ring_ready, 1)

                    pipelined(s_, ((1, take), (2, to_ring)))

                @block.tensor
                def _(t_):
                    for signal in (scaled_in_psum, message_ready, rows_in_psum):
                        t_.sem_inc(signal, AHEAD)

                    def transpose(k, g, s, turn):
                        t_.wait_ge(scaled_ready, at(k))
                        t_.wait_ge(scaled_t_ready, at(k, back=2))
                        for t in range(TPG):
                            for pair in range(2):
                                last = t_.transpose(bank[6 * s + pair][:, t * P:(t + 1) * P],
                                                    scaled[:, s, t, 2 * pair:2 * pair + 2].rearrange("p h f -> p (h f)"), ident[:])
                        last.then_inc(scaled_in_psum, 1)

                    def message(k, g, s, turn):
                        t_.wait_ge(scaled_t_ready, at(k))
                        t_.wait_ge(summed, at(k, back=2))
                        for pair in range(2):
                            last = t_.matmul(bank[2 + s][0:D], w_heads[:, l, pair], scaled_t[:, s, pair], start=pair == 0, stop=pair == 1)
                        last.then_inc(message_ready, 1)

                    def next_rows(k, g, s, turn):
                        t_.wait_ge(ring_ready, at(k))
                        t_.wait_ge(rows_ready, at(k, back=2))
                        for t in range(TPG):
                            last = t_.matmul(bank[4 + s][:, t * width:(t + 1) * width], ring[:, s, t * P:(t + 1) * P], w_row[:, l, 0:width],
                                             start=True, stop=True)
                        last.then_inc(rows_in_psum, 1)

                    pipelined(t_, ((1, transpose), (2, message), (3, next_rows)))

        def spread(l):
            with ExitStack() as st:
                keep = mem(st, f"keep_next_{l}", [D, 2, GE], U8)
                ended = mem(st, f"ended_{l}", [D, 2, GE])
                h_new = mem(st, f"h_new_{l}", [D, 2, GE])
                keep_in = [sem(st, f"next_in_{l}_{s}") for s in range(2)]
                gathered = [pool_dma_sem(f"rows_gathered_{l}_{s}") for s in range(2)]
                through = sem(st, f"through_{l}")
                ended_ready = sem(st, f"ended_ready_{l}")
                spread_out = sem(st, f"spread_{l}")
                wide_ready = sem(st, f"wide_ready_{l}")
                dst_in_psum = sem(st, f"dst_in_psum_{l}")
                self_ready = sem(st, f"self_ready_{l}")
                sp_paced = sem(st, f"sp_paced2_{l}")
                act_paced = sem(st, f"act_paced2_{l}")
                block = st.enter_context(nc.Block())

                @block.gpsimd
                def _(pool):
                    for k in range(G):
                        g, s = G - 1 - k, k % 2
                        if k >= 2:
                            pool.wait_ge(gathered[s], 16 * TPG * (k // 2))
                        for t in range(TPG):
                            at_tile = TPG * g + t
                            pool.indirect_dma_start(
                                out=edge[:, at_tile], out_offset=None, in_=tables[l],
                                in_offset=bass.IndirectOffsetOnAxis(ap=row_of_source[:, at_tile:at_tile + 1], axis=0),
                            ).then_inc(gathered[s], 16)

                @block.sync
                def _(sp):
                    def load(k, g, s, turn):
                        sp.wait_ge(spread_out, at(k, back=2))
                        sp.sem_inc(sp_paced, 1)
                        sp.dma_start(keep[:, s], lanes(keep_row[bass.ds(g * GE + 1, GE)], D)).then_inc(keep_in[s], 16)

                    pipelined(sp, ((0, load),), down=True)

                @block.tensor
                def _(t_):
                    for signal in (through, dst_in_psum):
                        t_.sem_inc(signal, AHEAD)

                    def weights(k, g, s, turn):
                        t_.wait_ge(ended_ready, at(k, back=2))
                        t_.matmul(bank[s][0:D], w_row[:, l, 0:D], wide[:, bass.ds(g * GE + 1, GE)], start=True, stop=True).then_inc(through, 1)

                    def dst_side(k, g, s, turn):
                        t_.wait_ge(spread_out, at(k))
                        t_.wait_ge(self_ready, at(k, back=2))
                        for t in range(TPG):
                            last = t_.matmul(bank[2 + s][:, t * EDGE_W:(t + 1) * EDGE_W], h_new[:, s, t * P:(t + 1) * P], w_edge[:, l + 1],
                                             start=True, stop=True)
                        last.then_inc(dst_in_psum, 1)

                    pipelined(t_, ((0, weights), (2, dst_side)), down=True)

                @block.vector
                def _(v):
                    for signal in (ended_ready, spread_out, self_ready):
                        v.sem_inc(signal, AHEAD)
                    v.memset(h_new[:, 1, 0:1], 0.0).then_inc(sp_paced, 1)

                    def end(k, g, s, turn):
                        v.wait_ge(keep_in[s], turn * 16 + 16)
                        v.wait_ge(through, at(k))
                        v.scalar_tensor_tensor(out=ended[:, s], in0=keep[:, s], scalar=0.0, in1=bank[s][0:D],
                                               op0=ALU.is_equal, op1=ALU.mult).then_inc(ended_ready, 1)

                    def back(k, g, s, turn):
                        v.wait_ge(ended_ready, at(k))
                        v.wait_ge(spread_out, at(k, back=1))
                        v.wait_ge(wide_ready, at(k, back=2))
                        v.wait_ge(dst_in_psum, at(k, back=2))
                        v.tensor_tensor_scan(out=h_new[:, s, ::-1], data0=keep[:, s, ::-1], data1=ended[:, s, ::-1],
                                             initial=h_new[:, 1 - s, 0:1], op0=ALU.mult, op1=ALU.add).then_inc(spread_out, 1)

                    def combine(k, g, s, turn):
                        tiles = bass.ds(g * TPG, TPG)
                        here = bank[2 + s][:, 0:TPG * EDGE_W].rearrange("p (t w) -> p t w", w=EDGE_W)
                        v.wait_ge(gathered[s], turn * (16 * TPG) + 16 * TPG)
                        v.wait_ge(dst_in_psum, at(k))
                        v.tensor_tensor(edge[:, tiles, 0:D], edge[:, tiles, 0:D], here[:, :, 0:D], ALU.subtract)
                        v.tensor_tensor(edge[:, tiles, D:ROW], edge[:, tiles, D:ROW], here[:, :, D:D + H], ALU.add)
                        v.tensor_scalar(self_logit[:, tiles], here[:, :, D + H:], 0.0, None, ALU.add).then_inc(self_ready, 1)

                    pipelined(v, ((1, end), (1, back), (3, combine)), down=True)

                @block.scalar
                def _(s_):
                    s_.preload_act_table_set(ACT_TABLES)
                    s_.sem_inc(wide_ready, AHEAD)

                    def finish(k, g, s, turn):
                        s_.wait_ge(spread_out, at(k))
                        s_.sem_inc(act_paced, 1)
                        s_.activation(wide[D:P, bass.ds(g * GE + 1, GE)], h_new[:, s], ACT.Copy).then_inc(wide_ready, 1)

                    pipelined(s_, ((1, finish),), down=True)

        def attention_step(l):
            with ExitStack() as st:
                alpha = mem(st, f"alpha_{l}", [P, TILES, H])
                softmax_weights(l, alpha)
                messages(l, alpha)
            if l < L - 1:
                spread(l)
            clear_signals()

        keep_q = mem(top, "keep_q", [Q, CE + 1])
        carry_in = mem(top, "carry_in", [1, 4, Q])
        with ExitStack() as st:
            keep_u = mem(st, "keep_u8", [Q, CE + 1], U8)
            tmp = [mem(st, f"tmp{n}", [P, TILES]) for n in range(5)]
            own_numbered = sem(st, "own_numbered")
            low = mem(st, "low", [Q, 2])
            keep_in = sem(st, "keep_in")
            own = sem(st, "own")
            low_t = sem(st, "low_t")
            block = st.enter_context(nc.Block())

            @block.gpsimd
            def _(pool):
                pool.iota(row_of_source[:], pattern=[[1, TILES]], base=0, channel_multiplier=TILES).then_inc(own_numbered, 1)

            @block.sync
            def _(sp):
                for s in range(CH):
                    sp.dma_start(keep_u[s * H:(s + 1) * H], lanes(keep_row[s * CE:(s + 1) * CE + 1], H)).then_inc(keep_in, 16)

            @block.vector
            def _(v):
                count = [0]

                def link(ins):
                    count[0] += 1
                    ins.then_inc(own, 1)
                    v.wait_ge(own, count[0])

                known, above, row, delta, own_row = tmp
                link(v.tensor_scalar(known[:], equal_to[:], 0.0, None, ALU.is_gt))
                link(v.tensor_scalar(above[:], not_above[:], 1.0, float(P * TILES - 1), ALU.is_equal, ALU.mult))
                link(v.tensor_scalar(row[:], not_above[:], -2.0, float(TILES), ALU.add, ALU.mult))
                link(v.tensor_tensor(row[:], row[:], tiles_before[:], ALU.add))
                link(v.tensor_tensor(row[:], row[:], above[:], ALU.add))
                v.wait_ge(own_numbered, 1)
                link(v.tensor_copy(own_row[:], row_of_source[:]))
                for first, other, to in ((EP, own_row, row_of_source), (N, src_f, row_of_x1)):
                    link(v.scalar_tensor_tensor(out=delta[:], in0=row[:], scalar=float(first), in1=other[:], op0=ALU.add, op1=ALU.subtract))
                    link(v.tensor_tensor(delta[:], delta[:], known[:], ALU.mult))
                    link(v.tensor_tensor(delta[:], delta[:], other[:], ALU.add))
                    link(v.tensor_copy(to[:], delta[:]))
                v.wait_ge(keep_in, 16 * CH)
                link(v.tensor_copy(keep_q[:], keep_u[:]))
                link(v.tensor_reduce(low[:, 0:1], keep_q[:, 0:CE], AX_X, ALU.min))
                link(v.tensor_reduce(low[:, 1:2], keep_q[:, 1:CE + 1], AX_X, ALU.min))
                KEEP_LOW = count[0]
                v.wait_ge(low_t, 2)
                for n in range(2):
                    link(v.tensor_copy(carry_in[:, n], bank[n][0:1, 0:Q]))
                link(v.tensor_scalar(carry_in[:, 2:4], carry_in[:, 0:2], -1.0, BIG, ALU.add, ALU.mult))
                marks["keep_low"] = KEEP_LOW

            @block.tensor
            def _(t):
                t.wait_ge(own, marks["keep_low"])
                for n in range(2):
                    t.matmul(bank[n][0:1, 0:Q], low[:, n:n + 1], ident[0:Q, 0:Q], start=True, stop=True).then_inc(low_t, 1)

        clear_signals()
        for l in range(L):
            attention_step(l)

        bn_scale = mem(top, "bn_scale", [P, 2])
        with ExitStack() as st:
            l = L - 1
            keep = mem(st, "keep_last", [D, 2, GE], U8)
            ended = mem(st, "ended_last", [D, 2, GE])
            h_new = mem(st, "h_new_last", [D, 2, GE])
            h_full = mem(st, "h_full_last", [D, 2, GE])
            x_again = mem(st, "x_last", [P, 2, TPG, D])
            norm = mem(st, "norm_last", [P, 2, TPG, 2, D])
            square = mem(st, "square_last", [P, TPG * 2 * D])
            norm_t = mem(st, "norm_t_last", [P, GE])
            attr = mem(st, "attr", [P, 2, TPG, D])
            attr_t = mem(st, "attr_t", [D, GE])
            stat = mem(st, "stat_last", [P, 2, 4, 2 * TPG])
            logs = mem(st, "logs_last", [P, 2 * TPG])
            conv_stat = mem(st, "conv_stat", [P, G, 6])
            moments = mem(st, "moments", [P, 4])
            keep_in = [sem(st, f"keep_last_in{s}") for s in range(2)]
            x_in = [sem(st, f"x_last_in{s}") for s in range(2)]
            attr_in = [sem(st, f"attr_in{s}") for s in range(2)]
            h1_saved = [sem(st, f"h1_saved{s}") for s in range(2)]
            gathered = [pool_dma_sem(f"x1_gathered{s}") for s in range(2)]
            through, ended_ready, spread_out, full_ready, full_t, centered, squared, summed2, rstd_ready, \
                norm_ready, norm_in_psum, attr_in_psum, norm_t_ready, conv_ready, conv_kept, conv_counted, x_used = [
                    sem(st, f"{name}_last") for name in (
                        "through", "ended_ready", "spread_out", "full_ready", "full_t", "centered", "squared",
                        "summed2", "rstd_ready", "norm_ready", "norm_in_psum", "attr_in_psum", "norm_t_ready",
                        "conv_ready", "conv_kept", "conv_counted", "x_used")]
            own = sem(st, "own_last")
            act_own = sem(st, "act_own_last")
            zeroed = sem(st, "attr_zeroed")
            sp_paced = sem(st, "sp_paced_last")
            act_paced = sem(st, "act_paced_last")
            pe_paced = sem(st, "pe_paced_last")
            block = st.enter_context(nc.Block())
            LEAD = 8

            @block.gpsimd
            def _(pool):
                for k in range(G):
                    g, s = G - 1 - k, k % 2
                    if k >= 2:
                        pool.wait_ge(gathered[s], 16 * TPG * (k // 2))
                    for t in range(TPG):
                        tile = TPG * g + t
                        pool.indirect_dma_start(
                            out=edge[:, tile, 0:D], out_offset=None, in_=tables[l],
                            in_offset=bass.IndirectOffsetOnAxis(ap=row_of_x1[:, tile:tile + 1], axis=0),
                        ).then_inc(gathered[s], 16)

            @block.sync
            def _(sp):
                def load(k, g, s, turn):
                    sp.wait_ge(spread_out, at(k, back=2))
                    sp.sem_inc(sp_paced, 1)
                    sp.dma_start(keep[:, s], lanes(keep_row[bass.ds(g * GE + 1, GE)], D)).then_inc(keep_in[s], 16)

                def load_x(k, g, s, turn):
                    sp.wait_ge(x_used, at(k, back=2))
                    sp.sem_inc(sp_paced, 1)
                    sp.dma_start(x_again[:, s], x_dst.rearrange("p (t f) -> p t f", f=D)[:, bass.ds(g * TPG, TPG)]).then_inc(x_in[s], 16)

                def load_attr(k, g, s, turn):
                    if isinstance(k, int) and k == 0:
                        full = LAST_E // P
                        sp.wait_ge(zeroed, 1)
                        sp.dma_start(attr[:, s, 0:full], edge_attr[(G - 1) * GE:(G - 1) * GE + full * P].rearrange("(t p) f -> p t f", p=P)).then_inc(attr_in[s], 16)
                        sp.dma_start(attr[0:LAST_E - full * P, s, full], edge_attr[(G - 1) * GE + full * P:E]).then_inc(attr_in[s], 16)
                        return
                    sp.wait_ge(attr_in_psum, at(k, back=2))
                    sp.sem_inc(sp_paced, 1)
                    if s == 0 and isinstance(k, int) and k == 2:
                        sp.wait_ge(attr_in[0], 32)
                    sp.dma_start(attr[:, s], edge_attr[bass.ds(g * GE, GE)].rearrange("(t p) f -> p t f", p=P)).then_inc(attr_in[s], 16)

                def save_h1(k, g, s, turn):
                    sp.wait_ge(norm_ready, at(k))
                    sp.sem_inc(sp_paced, 1)
                    sp.dma_start(h1_dst.rearrange("p (t f) -> p t f", f=D)[:, bass.ds(g * TPG, TPG)], norm[:, s, :, 1]).then_inc(h1_saved[s], 16)

                for s in range(2):
                    sp.sem_inc(h1_saved[s], 32)
                pipelined(sp, ((0, load), (2, load_x), (4, load_attr), (5, save_h1)), down=True, lead=LEAD)
                sp.wait_ge(h1_saved[0], 16 * (G // 2 + 1) + 32)
                sp.wait_ge(h1_saved[1], 16 * (G // 2) + 32)

            @block.tensor
            def _(t_):
                for signal in (through, full_t, norm_in_psum, attr_in_psum, conv_ready):
                    t_.sem_inc(signal, AHEAD)

                def weights(k, g, s, turn):
                    t_.wait_ge(ended_ready, at(k, back=2))
                    t_.matmul(bank[s][0:D], w_row[:, l, 0:D], wide[:, bass.ds(g * GE + 1, GE)], start=True, stop=True).then_inc(through, 1)

                def to_edges(k, g, s, turn):
                    t_.wait_ge(full_ready, at(k))
                    t_.wait_ge(x_used, at(k, back=1))
                    t_.sem_inc(pe_paced, 1)
                    for t in range(TPG):
                        last = t_.transpose(bank[2][:, t * D:(t + 1) * D], h_full[:, s, t * P:(t + 1) * P], ident[0:D, 0:D])
                    last.then_inc(full_t, 1)

                def transposes(k, g, s, turn):
                    t_.wait_ge(norm_ready, at(k))
                    t_.wait_ge(norm_t_ready, at(k, back=1))
                    for t in range(TPG):
                        last = t_.transpose(bank[4][:, t * P:(t + 1) * P], norm[:, s, t].rearrange("p e f -> p (e f)"), ident[:])
                    last.then_inc(norm_in_psum, 1)
                    if isinstance(k, int):
                        t_.wait_ge(attr_in[s], 16 * (turn + (1 if s else 2)))
                    else:
                        t_.wait_ge(attr_in[s], turn * 16 + (16 if s else 32))
                        t_.sem_inc(pe_paced, 1)
                    for t in range(TPG):
                        last = t_.transpose(bank[3][0:D, t * P:(t + 1) * P], attr[:, s, t], ident[:])
                    last.then_inc(attr_in_psum, 1)

                def convolve(k, g, s, turn):
                    t_.wait_ge(norm_t_ready, at(k))
                    t_.wait_ge(conv_counted, at(k, back=2))
                    t_.matmul(bank[5 + s][:], w_conv[:], norm_t[:], start=True, stop=False)
                    t_.matmul(bank[5 + s][:], w_conv3[:], attr_t[:], start=False, stop=True).then_inc(conv_ready, 1)

                pipelined(t_, ((0, weights), (5, transposes), (6, convolve), (2, to_edges)), down=True, lead=LEAD)

            @block.vector
            def _(v):
                for signal in (ended_ready, spread_out, x_used, centered, summed2, norm_ready, conv_counted):
                    v.sem_inc(signal, AHEAD)
                v.memset(h_new[:, 1, 0:1], 0.0).then_inc(sp_paced, 1)
                v.memset(attr[:], 0.0).then_inc(zeroed, 1)
                OWN = 3

                def end(k, g, s, turn):
                    v.wait_ge(keep_in[s], turn * 16 + 16)
                    v.wait_ge(through, at(k))
                    v.scalar_tensor_tensor(out=ended[:, s], in0=keep[:, s], scalar=0.0, in1=bank[s][0:D],
                                           op0=ALU.is_equal, op1=ALU.mult).then_inc(ended_ready, 1)

                def back(k, g, s, turn):
                    v.wait_ge(ended_ready, at(k))
                    v.wait_ge(spread_out, at(k, back=1))
                    v.wait_ge(full_ready, at(k, back=2))
                    v.tensor_tensor_scan(out=h_new[:, s, ::-1], data0=keep[:, s, ::-1], data1=ended[:, s, ::-1],
                                         initial=h_new[:, 1 - s, 0:1], op0=ALU.mult, op1=ALU.add).then_inc(spread_out, 1)

                def center(k, g, s, turn):
                    count = [0]

                    def link(ins):
                        count[0] += 1
                        ins.then_inc(own, 1)
                        v.wait_ge(own, k * OWN + count[0])

                    tiles = bass.ds(g * TPG, TPG)
                    here = edge[:, tiles, 0:D]
                    now = stat[:, s].rearrange("p n (t e) -> p n t e", e=2)
                    v.wait_ge(gathered[s], turn * (16 * TPG) + 16 * TPG)
                    v.wait_ge(norm_in_psum, at(k, back=2))
                    v.wait_ge(h1_saved[s], turn * 16 + 32)
                    v.sem_inc(sp_paced, 1)
                    link(v.tensor_reduce(now[:, 0, :, 0], here, AX_X, ALU.add))
                    link(v.scalar_tensor_tensor(out=norm[:, s, :, 0], in0=inner(now[:, 0, :, 0], [P, TPG, D]), scalar=-1.0 / D,
                                                in1=here, op0=ALU.mult, op1=ALU.add))
                    v.wait_ge(x_in[s], turn * 16 + 16)
                    v.wait_ge(full_t, at(k))
                    v.tensor_tensor(here, bank[2][:, 0:TPG * D].rearrange("p (t f) -> p t f", f=D), x_again[:, s], ALU.add).then_inc(x_used, 1)
                    v.wait_ge(x_used, at(k))
                    v.sem_inc(sp_paced, 1)
                    link(v.tensor_reduce(now[:, 0, :, 1], here, AX_X, ALU.add))
                    assert count[0] == OWN
                    v.scalar_tensor_tensor(out=norm[:, s, :, 1], in0=inner(now[:, 0, :, 1], [P, TPG, D]), scalar=-1.0 / D,
                                           in1=here, op0=ALU.mult, op1=ALU.add).then_inc(centered, 1)

                def variance(k, g, s, turn):
                    v.wait_ge(squared, at(k))
                    v.tensor_reduce(stat[:, s, 2], square[:].rearrange("p (t f) -> p t f", f=D), AX_X, ALU.add).then_inc(summed2, 1)

                def normalize(k, g, s, turn):
                    v.wait_ge(rstd_ready, at(k))
                    part = norm[:, s].rearrange("p t e f -> p (t e) f")
                    v.scalar_tensor_tensor(out=part, in0=part, scalar=0.0, in1=inner(stat[:, s, 3], [P, 2 * TPG, D]),
                                           op0=ALU.max, op1=ALU.mult).then_inc(norm_ready, 1)

                def count_in(k, g, s, turn):
                    used = LAST_E if isinstance(k, int) and k == 0 else GE
                    v.wait_ge(conv_kept, at(k))
                    v.sem_inc(sp_paced, 1)
                    v.bn_stats(conv_stat[:, bass.ds(g, 1)].rearrange("p a n -> p (a n)"), bank[5 + s][:, 0:used]).then_inc(conv_counted, 1)

                pipelined(v, ((5, normalize), (1, end), (1, back), (4, variance), (3, center), (7, count_in)), down=True, lead=LEAD)
                count = [G * OWN]

                def link(ins):
                    count[0] += 1
                    ins.then_inc(own, 1)
                    v.wait_ge(own, count[0])

                v.wait_ge(conv_counted, at(G - 1))
                link(v.bn_aggr(moments[:, 0:2], conv_stat[:]))
                v.sem_inc(summed2, 1)
                v.wait_ge(rstd_ready, at(G))
                link(v.tensor_tensor(bn_scale[:, 0:1], moments[:, 3:4], bn_cols[:, 1:2], ALU.mult))
                link(v.tensor_tensor(bn_scale[:, 1:2], moments[:, 0:1], bn_cols[:, 0:1], ALU.add))
                link(v.tensor_tensor(bn_scale[:, 1:2], bn_scale[:, 1:2], bn_scale[:, 0:1], ALU.mult))
                link(v.tensor_tensor(bn_scale[:, 1:2], bn_cols[:, 2:3], bn_scale[:, 1:2], ALU.subtract))
                link(v.tensor_scalar(bn_scale[0:D], bn_scale[0:D], -1.0, None, ALU.mult))

            @block.scalar
            def _(s_):
                s_.preload_act_table_set(ACT_TABLES)
                for signal in (full_ready, squared, rstd_ready, norm_t_ready, conv_kept):
                    s_.sem_inc(signal, AHEAD)

                def finish(k, g, s, turn):
                    s_.wait_ge(spread_out, at(k))
                    s_.wait_ge(full_t, at(k, back=2))
                    s_.activation(h_full[:, s], h_new[:, s], ACT.Identity, bias=const_h[:, L:L + 1]).then_inc(full_ready, 1)

                def squares(k, g, s, turn):
                    s_.wait_ge(centered, at(k))
                    s_.wait_ge(summed2, at(k, back=1))
                    s_.activation(square[:], norm[:, s].rearrange("p t e f -> p (t e f)"), ACT.Square).then_inc(squared, 1)

                def rstd(k, g, s, turn):
                    s_.wait_ge(summed2, at(k))
                    s_.activation(logs[:], stat[:, s, 2], ACT.Ln, bias=eps[:], scale=1.0 / D).then_inc(act_own, 1)
                    s_.wait_ge(act_own, k + 1)
                    s_.activation(stat[:, s, 3], logs[:], ACT.Exp, scale=-0.5).then_inc(rstd_ready, 1)

                def take(k, g, s, turn):
                    s_.wait_ge(norm_in_psum, at(k))
                    s_.wait_ge(conv_ready, at(k, back=1))
                    s_.activation(norm_t[:], bank[4][:], ACT.Copy)
                    s_.wait_ge(attr_in_psum, at(k))
                    s_.activation(attr_t[:], bank[3][0:D], ACT.Copy).then_inc(norm_t_ready, 1)

                def keep_conv(k, g, s, turn):
                    s_.wait_ge(conv_ready, at(k))
                    s_.sem_inc(act_paced, 1)
                    s_.activation(wide[:, bass.ds(g * GE + 1, GE)], bank[5 + s][:], ACT.Identity, bias=bn_cols[:, 0:1]).then_inc(conv_kept, 1)

                pipelined(s_, ((1, finish), (4, rstd), (3, squares), (5, take), (6, keep_conv)), down=True, lead=LEAD)
                s_.wait_ge(summed2, at(G))
                s_.activation(moments[:, 2:3], moments[:, 1:2], ACT.Ln, bias=eps[:]).then_inc(act_own, 1)
                s_.wait_ge(act_own, G + 1)
                s_.activation(moments[:, 3:4], moments[:, 2:3], ACT.Exp, scale=-0.5).then_inc(rstd_ready, 1)
        clear_signals()

        upd_scale = mem(top, "upd_scale", [D, 2])
        shift_row = mem(top, "shift_row", [P, D])
        with ExitStack() as st:
            SLOTS = 4
            keep = mem(st, "keep_conv", [D, SLOTS, GE], U8)
            keep_next = mem(st, "keep_conv_next", [D, SLOTS, GE], U8)
            arg = mem(st, "arg", [P, SLOTS, GE])
            soft = mem(st, "soft", [P, SLOTS, GE])
            gate = mem(st, "gate", [P, 2, GE])
            last_sum = mem(st, "last_sum", [D, 2, GE])
            upd_stat = mem(st, "upd_stat", [D, G, 6])
            m2 = mem(st, "m2", [D, 6])
            shift_rep = mem(st, "shift_rep", [D, P])
            keep_in = [sem(st, f"keep_conv_in{s}") for s in range(SLOTS)]
            arg_ready, ended, exped, logged, soft_ready, gate_ready, message_ready, summed, counted = [
                sem(st, f"{name}_conv") for name in ("arg_ready", "ended", "exped", "logged", "soft_ready", "gate_ready",
                                                     "message_ready", "summed", "counted")]
            own = sem(st, "own_conv")
            rstd_ready = sem(st, "rstd_conv")
            moments_ready = sem(st, "moments_conv")
            rep_ready = sem(st, "rep_conv")
            row_ready = sem(st, "row_conv")
            sp_paced = sem(st, "sp_paced_conv")
            act_paced = sem(st, "act_paced_conv")
            block = st.enter_context(nc.Block())

            @block.sync
            def _(sp):
                def load(k, g, s, turn):
                    sp.wait_ge(counted, at(k, back=4))
                    sp.sem_inc(sp_paced, 1)
                    sp.dma_start(keep[:, s], lanes(keep_row[bass.ds(g * GE, GE)], D)).then_inc(keep_in[s], 16)
                    sp.dma_start(keep_next[:, s], lanes(keep_row[bass.ds(g * GE + 1, GE)], D)).then_inc(keep_in[s], 16)

                pipelined(sp, ((1, load),), lead=6, slots=SLOTS)

            @block.scalar
            def _(s_):
                s_.preload_act_table_set(ACT_TABLES)
                for signal in (arg_ready, exped, logged, gate_ready):
                    s_.sem_inc(signal, AHEAD)

                def norm1(k, g, s, turn):
                    s_.wait_ge(message_ready, at(k, back=4))
                    s_.sem_inc(act_paced, 1)
                    here = wide[:, bass.ds(g * GE + 1, GE)]
                    s_.activation(arg[:, s], here, ACT.Identity, bias=bn_scale[:, 1:2], scale=bn_scale[:, 0:1])
                    s_.activation(soft[:, s], here, ACT.Abs, bias=bn_scale[:, 1:2], scale=bn_scale[:, 0:1]).then_inc(arg_ready, 1)

                def exponential(k, g, s, turn):
                    s_.wait_ge(arg_ready, at(k))
                    s_.activation(soft[:, s], soft[:, s], ACT.Exp, scale=-1.0).then_inc(exped, 1)

                def logarithm(k, g, s, turn):
                    s_.wait_ge(exped, at(k))
                    s_.activation(soft[:, s], soft[:, s], ACT.Ln, bias=1.0).then_inc(logged, 1)

                def sigmoid(k, g, s, turn):
                    s_.wait_ge(soft_ready, at(k))
                    s_.wait_ge(summed, at(k, back=2))
                    s_.activation(gate[D:P, s % 2], soft[0:D, s], ACT.Exp, scale=-1.0).then_inc(gate_ready, 1)

                pipelined(s_, ((1, exponential), (2, logarithm), (3, sigmoid), (0, norm1)), lead=6, slots=SLOTS)
                s_.wait_ge(moments_ready, 1)
                s_.activation(m2[:, 4:5], m2[:, 3:4], ACT.Ln, bias=eps[0:D]).then_inc(act_paced, 1)
                s_.wait_ge(act_paced, G + 1)
                s_.activation(m2[:, 5:6], m2[:, 4:5], ACT.Exp, scale=-0.5).then_inc(rstd_ready, 1)

            @block.vector
            def _(v):
                for signal in (ended, soft_ready, message_ready, summed, counted):
                    v.sem_inc(signal, AHEAD)

                def larger(k, g, s, turn):
                    v.wait_ge(logged, at(k))
                    v.scalar_tensor_tensor(out=soft[:, s], in0=arg[:, s], scalar=0.0, in1=soft[:, s], op0=ALU.max, op1=ALU.add).then_inc(soft_ready, 1)

                def message(k, g, s, turn):
                    v.wait_ge(gate_ready, at(k))
                    v.tensor_tensor(gate[0:D, s % 2], gate[D:P, s % 2], soft[D:P, s], ALU.mult).then_inc(message_ready, 1)

                def scan(k, g, s, turn):
                    v.wait_ge(message_ready, at(k))
                    v.wait_ge(keep_in[s], turn * 32 + 32)
                    v.wait_ge(summed, at(k, back=1))
                    v.tensor_tensor_scan(out=wide[0:D, bass.ds(g * GE + 1, GE)], data0=keep[:, s], data1=gate[0:D, s % 2],
                                         initial=wide[0:D, bass.ds(g * GE, 1)], op0=ALU.mult, op1=ALU.add).then_inc(summed, 1)

                def end(k, g, s, turn):
                    v.wait_ge(summed, at(k))
                    v.wait_ge(counted, at(k, back=2))
                    v.scalar_tensor_tensor(out=last_sum[:, s % 2], in0=keep_next[:, s], scalar=0.0, in1=wide[0:D, bass.ds(g * GE + 1, GE)],
                                           op0=ALU.is_equal, op1=ALU.mult).then_inc(ended, 1)

                def count_in(k, g, s, turn):
                    used = LAST_E if isinstance(k, int) and k == G - 1 else GE
                    v.wait_ge(ended, at(k))
                    v.sem_inc(sp_paced, 1)
                    v.bn_stats(upd_stat[:, bass.ds(g, 1)].rearrange("p a n -> p (a n)"), last_sum[:, s % 2, 0:used]).then_inc(counted, 1)

                pipelined(v, ((5, end), (4, message), (2, larger), (4, scan), (5, count_in)), lead=6, slots=SLOTS)
                count = [0]

                def link(ins):
                    count[0] += 1
                    ins.then_inc(own, 1)
                    v.wait_ge(own, count[0])

                v.wait_ge(counted, at(G - 1))
                link(v.bn_aggr(m2[:, 0:2], upd_stat[:]))
                link(v.tensor_tensor(m2[:, 2:3], m2[:, 0:1], m2[:, 0:1], ALU.mult))
                link(v.tensor_tensor(m2[:, 1:2], m2[:, 1:2], m2[:, 2:3], ALU.add))
                link(v.tensor_scalar(m2[:, 0:2], m2[:, 0:2], E / N, None, ALU.mult))
                link(v.tensor_tensor(m2[:, 2:3], m2[:, 0:1], m2[:, 0:1], ALU.mult))
                v.tensor_tensor(m2[:, 3:4], m2[:, 1:2], m2[:, 2:3], ALU.subtract).then_inc(moments_ready, 1)
                v.wait_ge(rstd_ready, 1)
                link(v.tensor_tensor(upd_scale[:, 0:1], m2[:, 5:6], bn_cols[0:D, 3:4], ALU.mult))
                link(v.tensor_tensor(upd_scale[:, 1:2], m2[:, 0:1], upd_scale[:, 0:1], ALU.mult))
                link(v.tensor_tensor(upd_scale[:, 1:2], bn_cols[0:D, 4:5], upd_scale[:, 1:2], ALU.subtract))
                v.tensor_scalar(shift_rep[:], ones[0:D], upd_scale[:, 1:2], None, ALU.mult).then_inc(rep_ready, 1)
                v.wait_ge(row_ready, 1)
                link(v.tensor_copy(shift_row[:], bank[0][:, 0:D]))

            @block.tensor
            def _(t_):
                t_.wait_ge(rep_ready, 1)
                t_.matmul(bank[0][:, 0:D], shift_rep[:], ident[0:D, 0:D], start=True, stop=True).then_inc(row_ready, 1)
        clear_signals()

        with ExitStack() as st:
            SLOTS = 4
            uses = [(G - s + SLOTS - 1) // SLOTS for s in range(SLOTS)]
            nodes = mem(st, "nodes_out", [P, SLOTS, NODE_T, D])
            n_norm = mem(st, "n_norm_out", [P, SLOTS, NODE_T, D])
            n_soft = mem(st, "n_soft", [P, SLOTS, NODE_T, D])
            n_stat = mem(st, "n_stat_out", [P, SLOTS, 4, NODE_T])
            n_logs = mem(st, "n_logs_out", [P, NODE_T])
            update = mem(st, "update", [D, GE])
            e_arg = mem(st, "e_arg", [P, SLOTS, TPG, D])
            e_soft = mem(st, "e_soft", [P, 2, TPG, D])
            nodes_in = [sem(st, f"nodes_out_in{s}") for s in range(SLOTS)]
            h1_in = [sem(st, f"h1_in{s}") for s in range(SLOTS)]
            stored = [sem(st, f"out_stored{s}") for s in range(SLOTS)]
            scattered = [pool_dma_sem(f"scattered{s}") for s in range(2)]
            n_centered, n_squared, n_summed2, n_rstd, n_abs, n_exped, n_logged, n_arg, n_larger, n_ready, n_log, \
                update_ready, update_t, e_abs, e_exped, e_logged, e_ready, e_larger = [
                    sem(st, f"{name}_out") for name in (
                        "n_centered", "n_squared", "n_summed2", "n_rstd", "n_abs", "n_exped", "n_logged", "n_arg", "n_larger",
                        "n_ready", "n_log", "update_ready", "update_t", "e_abs", "e_exped", "e_logged", "e_ready", "e_larger")]
            n_sum = sem(st, "n_sum_out")
            nodes_cleared = sem(st, "nodes_cleared")
            n_normed = sem(st, "n_normed_out")
            e_arg_ready = sem(st, "e_arg_ready_out")
            sp_paced = sem(st, "sp_paced_out")
            act_paced = sem(st, "act_paced_out")
            pe_paced = sem(st, "pe_paced_out")
            block = st.enter_context(nc.Block())

            @block.sync
            def _(sp):
                def load(k, g, s, turn):
                    used = LAST_P if isinstance(k, int) and k == G - 1 else P
                    sp.wait_ge(n_ready, at(k, back=4))
                    sp.sem_inc(sp_paced, 1)
                    sp.dma_start(nodes[0:used, s], tables[L - 1][bass.ds(k * GN, used * NODE_T)].rearrange("(p j) w -> p j w", j=NODE_T)).then_inc(nodes_in[s], 16)
                    sp.wait_ge(e_ready, at(k, back=4))
                    sp.sem_inc(sp_paced, 1)
                    sp.dma_start(e_arg[:, s], h1_dst.rearrange("p (t f) -> p t f", f=D)[:, bass.ds(k * TPG, TPG)]).then_inc(h1_in[s], 16)

                def save(k, g, s, turn):
                    used = LAST_P if isinstance(k, int) and k == G - 1 else P
                    sp.wait_ge(n_ready, at(k))
                    sp.sem_inc(sp_paced, 1)
                    sp.dma_start(out[bass.ds(k * GN, used * NODE_T)].rearrange("(p j) f -> p j f", j=NODE_T), n_soft[0:used, s]).then_inc(stored[s], 16)

                for s in range(SLOTS):
                    sp.sem_inc(stored[s], 16)
                sp.wait_ge(nodes_cleared, 1)
                pipelined(sp, ((4, save), (0, load)), slots=SLOTS)

            @block.gpsimd
            def _(pool):
                for signal in (n_arg, n_ready):
                    pool.sem_inc(signal, AHEAD)

                def argument(k, g, s, turn):
                    v_shift = shift_row[:].unsqueeze(1).broadcast_to([P, NODE_T, D])
                    pool.wait_ge(n_normed, at(k))
                    pool.tensor_tensor(n_norm[:, s], n_norm[:, s], v_shift, ALU.add).then_inc(n_arg, 1)

                def add_x1(k, g, s, turn):
                    pool.wait_ge(n_larger, at(k))
                    pool.tensor_tensor(n_soft[:, s], n_soft[:, s], nodes[:, s], ALU.add).then_inc(n_ready, 1)

                pipelined(pool, ((4, add_x1), (3, argument)), slots=SLOTS)
                for s in range(SLOTS):
                    pool.wait_ge(stored[s], 16 * uses[s] + 16)
                for k in range(G):
                    s = k % 2
                    pool.wait_ge(e_ready, at(k))
                    if k >= 2:
                        pool.wait_ge(scattered[s], 16 * TPG * (k // 2))
                    for t in range(TPG):
                        tile = TPG * k + t
                        pool.indirect_dma_start(
                            out=out, out_offset=bass.IndirectOffsetOnAxis(ap=scatter_row[:, tile:tile + 1], axis=0),
                            in_=edge[:, tile, 0:D], in_offset=None, bounds_check=N - 1, oob_is_err=False,
                        ).then_inc(scattered[s], 16)
                pool.wait_ge(scattered[0], 16 * TPG * (G // 2 + 1))
                pool.wait_ge(scattered[1], 16 * TPG * (G // 2))

            @block.vector
            def _(v):
                for signal in (n_sum, n_centered, n_summed2, n_normed, n_larger, e_arg_ready, e_larger, e_ready):
                    v.sem_inc(signal, AHEAD)
                v.memset(nodes[:], 0.0).then_inc(nodes_cleared, 1)

                def center(k, g, s, turn):
                    v.wait_ge(n_sum, at(k))
                    v.scalar_tensor_tensor(out=n_norm[:, s], in0=inner(n_stat[:, s, 0], [P, NODE_T, D]), scalar=-1.0 / D,
                                           in1=nodes[:, s], op0=ALU.mult, op1=ALU.add).then_inc(n_centered, 1)

                def node_sums(k, g, s, turn):
                    v.wait_ge(nodes_in[s], turn * 16 + 16)
                    v.tensor_reduce(n_stat[:, s, 0], nodes[:, s], AX_X, ALU.add).then_inc(n_sum, 1)

                def variance(k, g, s, turn):
                    v.wait_ge(n_squared, at(k))
                    v.tensor_reduce(n_stat[:, s, 2], n_soft[:, s], AX_X, ALU.add).then_inc(n_summed2, 1)

                def normalize(k, g, s, turn):
                    v.wait_ge(n_rstd, at(k))
                    v.scalar_tensor_tensor(out=n_norm[:, s], in0=n_norm[:, s], scalar=0.0, in1=inner(n_stat[:, s, 3], [P, NODE_T, D]),
                                           op0=ALU.max, op1=ALU.mult).then_inc(n_normed, 1)

                def finish(k, g, s, turn):
                    v.wait_ge(n_logged, at(k))
                    v.scalar_tensor_tensor(out=n_soft[:, s], in0=n_norm[:, s], scalar=0.0, in1=n_soft[:, s], op0=ALU.max, op1=ALU.add).then_inc(n_larger, 1)

                def e_argument(k, g, s, turn):
                    v.wait_ge(update_t, at(k))
                    v.wait_ge(h1_in[s], turn * 16 + 16)
                    v.tensor_tensor(e_arg[:, s], e_arg[:, s], bank[s % 2][:, 0:TPG * D].rearrange("p (t f) -> p t f", f=D), ALU.add).then_inc(e_arg_ready, 1)

                def e_finish(k, g, s, turn):
                    v.wait_ge(e_logged, at(k))
                    v.scalar_tensor_tensor(out=e_soft[:, s % 2], in0=e_arg[:, s], scalar=0.0, in1=e_soft[:, s % 2], op0=ALU.max, op1=ALU.add).then_inc(e_larger, 1)

                def e_store(k, g, s, turn):
                    tiles = bass.ds(k * TPG, TPG)
                    v.wait_ge(e_larger, at(k))
                    v.tensor_tensor(edge[:, tiles, 0:D], edge[:, tiles, 0:D], e_soft[:, s % 2], ALU.add).then_inc(e_ready, 1)

                pipelined(v, ((2, variance), (4, finish), (1, node_sums), (3, normalize), (1, center), (1, e_argument), (3, e_finish),
                              (3, e_store)), slots=SLOTS)

            @block.scalar
            def _(s_):
                s_.preload_act_table_set(ACT_TABLES)
                for signal in (update_ready, n_squared, n_log, n_rstd, n_abs, n_exped, n_logged, e_abs, e_exped, e_logged):
                    s_.sem_inc(signal, AHEAD)

                def updates(k, g, s, turn):
                    s_.wait_ge(update_t, at(k, back=1))
                    s_.sem_inc(act_paced, 1)
                    s_.activation(update[:], wide[0:D, bass.ds(k * GE + 1, GE)], ACT.Identity, bias=upd_scale[:, 1:2],
                                  scale=upd_scale[:, 0:1]).then_inc(update_ready, 1)

                def squares(k, g, s, turn):
                    s_.wait_ge(n_centered, at(k))
                    s_.wait_ge(stored[s], turn * 16 + 16)
                    s_.activation(n_soft[:, s].rearrange("p t f -> p (t f)"), n_norm[:, s].rearrange("p t f -> p (t f)"), ACT.Square).then_inc(n_squared, 1)

                def rstd(k, g, s, turn):
                    s_.wait_ge(n_summed2, at(k))
                    s_.activation(n_logs[:], n_stat[:, s, 2], ACT.Ln, bias=eps[:], scale=1.0 / D).then_inc(n_log, 1)
                    s_.wait_ge(n_log, at(k))
                    s_.activation(n_stat[:, s, 3], n_logs[:], ACT.Exp, scale=-0.5).then_inc(n_rstd, 1)

                def softplus(k, g, s, turn):
                    flat = n_soft[:, s].rearrange("p t f -> p (t f)")
                    s_.wait_ge(n_arg, at(k))
                    s_.activation(flat, n_norm[:, s].rearrange("p t f -> p (t f)"), ACT.Abs).then_inc(n_abs, 1)
                    s_.wait_ge(n_abs, at(k))
                    s_.activation(flat, flat, ACT.Exp, scale=-1.0).then_inc(n_exped, 1)
                    s_.wait_ge(n_exped, at(k))
                    s_.activation(flat, flat, ACT.Ln, bias=1.0).then_inc(n_logged, 1)

                def e_softplus(k, g, s, turn):
                    flat = e_soft[:, s % 2].rearrange("p t f -> p (t f)")
                    s_.wait_ge(e_arg_ready, at(k))
                    s_.wait_ge(e_ready, at(k, back=2))
                    s_.activation(flat, e_arg[:, s].rearrange("p t f -> p (t f)"), ACT.Abs).then_inc(e_abs, 1)
                    s_.wait_ge(e_abs, at(k))
                    s_.activation(flat, flat, ACT.Exp, scale=-1.0).then_inc(e_exped, 1)
                    s_.wait_ge(e_exped, at(k))
                    s_.activation(flat, flat, ACT.Ln, bias=1.0).then_inc(e_logged, 1)

                pipelined(s_, ((0, updates), (2, rstd), (1, squares), (2, e_softplus), (3, softplus)), slots=SLOTS)

            @block.tensor
            def _(t_):
                t_.sem_inc(update_t, AHEAD)

                def to_edges(k, g, s, turn):
                    t_.wait_ge(update_ready, at(k))
                    t_.wait_ge(e_arg_ready, at(k, back=2))
                    t_.sem_inc(pe_paced, 1)
                    for t in range(TPG):
                        last = t_.transpose(bank[s % 2][:, t * D:(t + 1) * D], update[:, t * P:(t + 1) * P], ident[0:D, 0:D])
                    last.then_inc(update_t, 1)

                pipelined(t_, ((0, to_edges),), slots=SLOTS)


_INS = ("x", "src", "dst", "edge_attr_64", "L0_gnn_Ws", "L0_gnn_attn_l", "L0_gnn_attn_r", "L0_gnn_gat_bias",
        "L0_gnn_h_bias", "L1_gnn_W_full", "L1_gnn_b_full", "L1_gnn_bn1_g", "L1_gnn_bn1_b", "L1_gnn_bn2_g",
        "L1_gnn_bn2_b")


def kernel(**inputs):
    import numpy as np
    import concourse.bacc as bacc
    from concourse.bass_utils import run_bass_kernel_spmd

    nc = bacc.Bacc("TRN2", target_bir_lowering=False, num_devices=1)
    arrays, args = {}, []
    for name in _INS:
        a = np.ascontiguousarray(inputs[name])
        arrays[f"in_{name}_dram"] = a
        args.append(nc.dram_tensor(f"in_{name}_dram", a.shape, mybir.dt.from_np(a.dtype), kind="ExternalInput").ap())
    args.append(nc.dram_tensor("out_0_dram", inputs["x"].shape, F32, kind="ExternalOutput").ap())
    build(nc, *args)
    results = run_bass_kernel_spmd(nc, [arrays], core_ids=[0])
    return results.results[0]["out_0_dram"]
```
